# Optimizing a Trainium2 kernel written in Bass

```python
import numpy as np
import jax
import jax.numpy as jnp

def _softmax(x, axis=-1):
    return jax.nn.softmax(x, axis=axis)

def _gelu(x):
    return jax.nn.gelu(x, approximate=True)

def _silu(x):
    return jax.nn.silu(x)

def _sigmoid(x):
    return jax.nn.sigmoid(x)

def _layernorm(x, axis=-1, eps=1e-05):
    m = jnp.mean(x, axis=axis, keepdims=True)
    v = jnp.var(x, axis=axis, keepdims=True)
    return (x - m) / jnp.sqrt(v + eps)

def _scatter_add(tgt, idx, src, axis=0):
    return tgt.at[idx].add(src)

def _segment_sum(src, seg, n):
    return jax.ops.segment_sum(src, seg, n)
kernel_name = 'mk_recurrent_d4_jaxref_r8_e63043'

def setup_inputs(seed: int=0):
    np.random.seed(seed)
    _w = jnp.asarray

    def _L0_attn_setup():
        import jax, jax.numpy as jnp
        from jax import lax
        import numpy as np
        D_MODEL = 128
        EXP = 2
        D_INNER = EXP * D_MODEL
        D_STATE = 16
        D_CONV = 4
        DT_RANK = 64
        NUM_GROUPS = 4
        BSZ, SEQ = (2, 256)
        EPS = 1e-05

        def _layernorm(x, g, b):
            m = jnp.mean(x, -1, keepdims=True)
            v = jnp.var(x, -1, keepdims=True)
            return (x - m) * lax.rsqrt(v + EPS) * g + b

        def _ste_sign(w):
            return w + lax.stop_gradient(jnp.sign(w) - w)

        def _quant_act_groupwise(x, b=8):
            Qb = float(2 ** (b - 1))
            B_, L, D = x.shape
            g = x.reshape(B_, NUM_GROUPS, L // NUM_GROUPS, D)
            gamma = jnp.max(jnp.abs(g), axis=(0, 2, 3), keepdims=True)
            q = jnp.clip(g * Qb / (gamma + EPS), -Qb + EPS, Qb - EPS)
            return q.reshape(B_, L, D)

        def _mamba(u, in_proj_w, conv_w, conv_b, x_proj_w, dt_proj_w, dt_proj_b, A_log, D_param, out_proj_w):
            B_, L, _ = u.shape
            xz = u @ in_proj_w.T
            xs, z = jnp.split(xz, 2, axis=-1)
            xt = jnp.transpose(xs, (0, 2, 1))
            xt = lax.conv_general_dilated(xt, conv_w, (1,), [(D_CONV - 1, 0)], feature_group_count=D_INNER, dimension_numbers=('NCH', 'OIH', 'NCH'))
            xt = xt + conv_b[None, :, None]
            xs = jax.nn.silu(jnp.transpose(xt, (0, 2, 1)))
            x_dbl = xs @ x_proj_w.T
            dt, Bm, Cm = jnp.split(x_dbl, [DT_RANK, DT_RANK + D_STATE], axis=-1)
            dt = jax.nn.softplus(dt @ dt_proj_w.T + dt_proj_b)
            A = -jnp.exp(A_log)

            def step(h, inp):
                dt_s, B_s, C_s, x_s = inp
                dA = jnp.exp(dt_s[..., None] * A)
                h = h * dA + (dt_s * x_s)[..., None] * B_s[:, None, :]
                y = jnp.einsum('bds,bs->bd', h, C_s)
                return (h, y)
            tm = lambda a: jnp.transpose(a, (1, 0, 2))
            h0 = jnp.zeros((B_, D_INNER, D_STATE), u.dtype)
            _, ys = lax.scan(step, h0, (tm(dt), tm(Bm), tm(Cm), tm(xs)))
            y = jnp.transpose(ys, (1, 0, 2)) + D_param * xs
            y = y * jax.nn.silu(z)
            return y @ out_proj_w.T
        key = jax.random.key(seed)
        ks = jax.random.split(key, 10)

        def n(k, shape, s=0.02):
            return jax.random.normal(k, shape, jnp.float32) * s
        return dict(x=jax.random.normal(ks[0], (BSZ, SEQ, D_MODEL), jnp.float32), ln1_g=jnp.ones((D_MODEL,), jnp.float32), ln1_b=jnp.zeros((D_MODEL,), jnp.float32), ln2_g=jnp.ones((D_MODEL,), jnp.float32), ln2_b=jnp.zeros((D_MODEL,), jnp.float32), W1=n(ks[1], (EXP * D_MODEL, D_MODEL)), b1=jnp.zeros((EXP * D_MODEL,), jnp.float32), W2=n(ks[2], (D_MODEL, EXP * D_MODEL)), b2=jnp.zeros((D_MODEL,), jnp.float32), in_proj_w=n(ks[3], (2 * D_INNER, D_MODEL)), conv_w=n(ks[4], (D_INNER, 1, D_CONV), 0.2), conv_b=jnp.zeros((D_INNER,), jnp.float32), x_proj_w=n(ks[5], (DT_RANK + 2 * D_STATE, D_INNER)), dt_proj_w=n(ks[6], (D_INNER, DT_RANK), 0.1), dt_proj_b=n(ks[7], (D_INNER,), 0.5), A_log=jnp.tile(jnp.log(jnp.arange(1, D_STATE + 1, dtype=jnp.float32)), (D_INNER, 1)), D_param=jnp.ones((D_INNER,), jnp.float32), out_proj_w=n(ks[8], (D_MODEL, D_INNER)))
    _L0_attn_in = _L0_attn_setup()

    def _L0_ffn_setup():
        import jax, jax.numpy as jnp
        import numpy as np
        K = 2
        key = jax.random.key(seed)
        ks = jax.random.split(key, 9)
        B, S, D, O, E = (4, 128, 128, 128, 8)
        sc = 0.02
        return {'x': jax.random.normal(ks[0], (B, S, D), dtype=jnp.float32), 'gate_w': jax.random.normal(ks[1], (D, E), dtype=jnp.float32) * sc, 'gate_b': jax.random.normal(ks[2], (E,), dtype=jnp.float32) * sc, 'w1': jax.random.normal(ks[3], (E, D, O), dtype=jnp.float32) * sc, 'b1': jax.random.normal(ks[4], (E, O), dtype=jnp.float32) * sc, 'w2': jax.random.normal(ks[5], (E, O, O), dtype=jnp.float32) * sc, 'b2': jax.random.normal(ks[6], (E, O), dtype=jnp.float32) * sc, 'w3': jax.random.normal(ks[7], (E, O, O), dtype=jnp.float32) * sc, 'b3': jax.random.normal(ks[8], (E, O), dtype=jnp.float32) * sc}
    _L0_ffn_in = _L0_ffn_setup()

    def _L1_attn_setup():
        import jax, jax.numpy as jnp
        import numpy as np
        SCALE = 128 ** (-0.5)
        key = jax.random.key(seed)
        ks = jax.random.split(key, 5)
        b, s, d = (4, 512, 128)
        x = jax.random.normal(ks[0], (b, s, d), dtype=jnp.float32)
        w_std = (2.0 / (d + d)) ** 0.5
        Wq = jax.random.normal(ks[1], (d, d), dtype=jnp.float32) * w_std
        Wk = jax.random.normal(ks[2], (d, d), dtype=jnp.float32) * w_std
        Wv = jax.random.normal(ks[3], (d, d), dtype=jnp.float32) * w_std
        Wr = jax.random.normal(ks[4], (d, d), dtype=jnp.float32) * w_std
        return {'x': x, 'Wq': Wq, 'Wk': Wk, 'Wv': Wv, 'Wr': Wr}
    _L1_attn_in = _L1_attn_setup()

    def _L1_ffn_setup():
        import jax, jax.numpy as jnp
        import numpy as np
        E, H, I, K = (8, 128, 256, 2)
        B, S = (4, 256)
        key = jax.random.key(seed)
        k1, k2, k3, k4 = jax.random.split(key, 4)
        x = jax.random.normal(k1, (B, S, H), dtype=jnp.float32)
        router_w = jax.random.uniform(k2, (E, H), dtype=jnp.float32, minval=-1.0, maxval=1.0) / np.sqrt(H).astype(np.float32)
        w13 = jax.random.normal(k3, (E, H, 2 * I), dtype=jnp.float32) * 0.02
        w2 = jax.random.normal(k4, (E, I, H), dtype=jnp.float32) * 0.02
        return {'x': x, 'router_w': router_w, 'w13': w13, 'w2': w2}
    _L1_ffn_in = _L1_ffn_setup()

    def _L2_attn_setup():
        import jax, jax.numpy as jnp
        import numpy as np
        H, P, HID, N, G, K, CS = (32, 64, 128, 128, 1, 4, 32)
        INTER = H * P
        CONV_DIM = INTER + 2 * G * N
        PROJ = INTER + CONV_DIM + H
        EPS = 1e-05

        def segsum(x):
            T = x.shape[-1]
            xx = jnp.broadcast_to(x[..., None], x.shape + (T,))
            xx = jnp.where(jnp.tril(jnp.ones((T, T), bool), -1), xx, 0.0)
            s = jnp.cumsum(xx, axis=-2)
            return jnp.where(jnp.tril(jnp.ones((T, T), bool)), s, -jnp.inf)
        key = jax.random.key(seed)
        ks = jax.random.split(key, 8)
        B_, S = (2, 256)
        x = jax.random.normal(ks[0], (B_, S, HID), jnp.float32)
        W_in = jax.random.normal(ks[1], (PROJ, HID), jnp.float32) / np.sqrt(HID)
        b_in = jnp.zeros((PROJ,), jnp.float32)
        conv_w = jax.random.normal(ks[2], (CONV_DIM, K), jnp.float32) / np.sqrt(K)
        dt = jnp.exp(jax.random.uniform(ks[3], (H,)) * (np.log(0.1) - np.log(0.001)) + np.log(0.001))
        dt = jnp.clip(dt, 0.0001)
        dt_bias = dt + jnp.log(-jnp.expm1(-dt))
        A_log = jnp.log(jax.random.uniform(ks[4], (H,), minval=1.0, maxval=16.0))
        D = jnp.ones((H,), jnp.float32)
        norm_w = jnp.ones((INTER,), jnp.float32)
        W_out = jax.random.normal(ks[5], (HID, INTER), jnp.float32) / np.sqrt(INTER)
        b_out = jnp.zeros((HID,), jnp.float32)
        return {'x': x, 'W_in': W_in, 'b_in': b_in, 'conv_w': conv_w, 'dt_bias': dt_bias, 'A_log': A_log, 'D': D, 'norm_w': norm_w, 'W_out': W_out, 'b_out': b_out}
    _L2_attn_in = _L2_attn_setup()

    def _L2_ffn_setup():
        import jax, jax.numpy as jnp
        import numpy as np
        B, S, D, E, H, K = (4, 256, 128, 8, 64, 2)
        key = jax.random.key(seed)
        ks = jax.random.split(key, 11)
        sc = 0.02
        return {'x': jax.random.normal(ks[0], (B, S, D), dtype=jnp.float32), 'gate_W': jax.random.normal(ks[1], (D, E), dtype=jnp.float32) * sc, 'W1': jax.random.normal(ks[2], (E, D, H), dtype=jnp.float32) * sc, 'b1': jnp.zeros((E, H), dtype=jnp.float32), 'W2': jax.random.normal(ks[3], (E, H, D), dtype=jnp.float32) * sc, 'b2': jnp.zeros((E, D), dtype=jnp.float32), 'Ws1': jax.random.normal(ks[4], (D, H), dtype=jnp.float32) * sc, 'bs1': jnp.zeros((H,), dtype=jnp.float32), 'Ws2': jax.random.normal(ks[5], (H, D), dtype=jnp.float32) * sc, 'bs2': jnp.zeros((D,), dtype=jnp.float32), 'route_scale': jnp.ones((), dtype=jnp.float32)}
    _L2_ffn_in = _L2_ffn_setup()

    def _L3_attn_setup():
        import jax, jax.numpy as jnp
        import numpy as np
        import math
        DK = 128
        key = jax.random.key(seed)
        k1, k2 = jax.random.split(key)
        x = jax.random.normal(k1, (4, 256, 128), dtype=jnp.float32)
        W = jax.random.normal(k2, (128, 3 * DK), dtype=jnp.float32) * (1.0 / math.sqrt(128))
        b = jnp.zeros((3 * DK,), dtype=jnp.float32)
        return {'x': x, 'W': W, 'b': b}
    _L3_attn_in = _L3_attn_setup()

    def _L3_ffn_setup():
        import jax, jax.numpy as jnp
        import numpy as np
        HIDDEN = 128
        INTER = 512
        key = jax.random.key(seed)
        k1, k2, k3, k4, k5 = jax.random.split(key, 5)
        hidden_states = jax.random.normal(k1, (4, 256, HIDDEN), dtype=jnp.float32)
        W1 = jax.random.normal(k2, (HIDDEN, INTER), dtype=jnp.float32) * (1.0 / np.sqrt(HIDDEN))
        b1 = jax.random.normal(k3, (INTER,), dtype=jnp.float32) * 0.02
        W2 = jax.random.normal(k4, (INTER, HIDDEN), dtype=jnp.float32) * (1.0 / np.sqrt(INTER))
        b2 = jax.random.normal(k5, (HIDDEN,), dtype=jnp.float32) * 0.02
        return {'hidden_states': hidden_states, 'W1': W1, 'b1': b1, 'W2': W2, 'b2': b2}
    _L3_ffn_in = _L3_ffn_setup()
    _d = {'L0_attn_x': _L0_attn_in['x'], 'L0_attn_ln1_g': _L0_attn_in['ln1_g'], 'L0_attn_ln1_b': _L0_attn_in['ln1_b'], 'L0_attn_ln2_g': _L0_attn_in['ln2_g'], 'L0_attn_ln2_b': _L0_attn_in['ln2_b'], 'L0_attn_W1': _L0_attn_in['W1'], 'L0_attn_b1': _L0_attn_in['b1'], 'L0_attn_W2': _L0_attn_in['W2'], 'L0_attn_b2': _L0_attn_in['b2'], 'L0_attn_in_proj_w': _L0_attn_in['in_proj_w'], 'L0_attn_conv_w': _L0_attn_in['conv_w'], 'L0_attn_conv_b': _L0_attn_in['conv_b'], 'L0_attn_x_proj_w': _L0_attn_in['x_proj_w'], 'L0_attn_dt_proj_w': _L0_attn_in['dt_proj_w'], 'L0_attn_dt_proj_b': _L0_attn_in['dt_proj_b'], 'L0_attn_A_log': _L0_attn_in['A_log'], 'L0_attn_D_param': _L0_attn_in['D_param'], 'L0_attn_out_proj_w': _L0_attn_in['out_proj_w'], 'L0_ffn_gate_w': _L0_ffn_in['gate_w'], 'L0_ffn_gate_b': _L0_ffn_in['gate_b'], 'L0_ffn_w1': _L0_ffn_in['w1'], 'L0_ffn_b1': _L0_ffn_in['b1'], 'L0_ffn_w2': _L0_ffn_in['w2'], 'L0_ffn_b2': _L0_ffn_in['b2'], 'L0_ffn_w3': _L0_ffn_in['w3'], 'L0_ffn_b3': _L0_ffn_in['b3'], 'L1_attn_Wq': _L1_attn_in['Wq'], 'L1_attn_Wk': _L1_attn_in['Wk'], 'L1_attn_Wv': _L1_attn_in['Wv'], 'L1_attn_Wr': _L1_attn_in['Wr'], 'L1_ffn_router_w': _L1_ffn_in['router_w'], 'L1_ffn_w13': _L1_ffn_in['w13'], 'L1_ffn_w2': _L1_ffn_in['w2'], 'L2_attn_W_in': _L2_attn_in['W_in'], 'L2_attn_b_in': _L2_attn_in['b_in'], 'L2_attn_conv_w': _L2_attn_in['conv_w'], 'L2_attn_dt_bias': _L2_attn_in['dt_bias'], 'L2_attn_A_log': _L2_attn_in['A_log'], 'L2_attn_D': _L2_attn_in['D'], 'L2_attn_norm_w': _L2_attn_in['norm_w'], 'L2_attn_W_out': _L2_attn_in['W_out'], 'L2_attn_b_out': _L2_attn_in['b_out'], 'L2_ffn_gate_W': _L2_ffn_in['gate_W'], 'L2_ffn_W1': _L2_ffn_in['W1'], 'L2_ffn_b1': _L2_ffn_in['b1'], 'L2_ffn_W2': _L2_ffn_in['W2'], 'L2_ffn_b2': _L2_ffn_in['b2'], 'L2_ffn_Ws1': _L2_ffn_in['Ws1'], 'L2_ffn_bs1': _L2_ffn_in['bs1'], 'L2_ffn_Ws2': _L2_ffn_in['Ws2'], 'L2_ffn_bs2': _L2_ffn_in['bs2'], 'L2_ffn_route_scale': _L2_ffn_in['route_scale'], 'L3_attn_W': _L3_attn_in['W'], 'L3_attn_b': _L3_attn_in['b'], 'L3_ffn_W1': _L3_ffn_in['W1'], 'L3_ffn_b1': _L3_ffn_in['b1'], 'L3_ffn_W2': _L3_ffn_in['W2'], 'L3_ffn_b2': _L3_ffn_in['b2']}
    _x0 = _d['L0_attn_x']
    _d['L0_attn_x'] = jax.random.normal(jax.random.fold_in(jax.random.key(seed), 1), (2, 1024, 128), dtype=_x0.dtype)
    del _x0
    return _d

def reference(L0_attn_x, L0_attn_ln1_g, L0_attn_ln1_b, L0_attn_ln2_g, L0_attn_ln2_b, L0_attn_W1, L0_attn_b1, L0_attn_W2, L0_attn_b2, L0_attn_in_proj_w, L0_attn_conv_w, L0_attn_conv_b, L0_attn_x_proj_w, L0_attn_dt_proj_w, L0_attn_dt_proj_b, L0_attn_A_log, L0_attn_D_param, L0_attn_out_proj_w, L0_ffn_gate_w, L0_ffn_gate_b, L0_ffn_w1, L0_ffn_b1, L0_ffn_w2, L0_ffn_b2, L0_ffn_w3, L0_ffn_b3, L1_attn_Wq, L1_attn_Wk, L1_attn_Wv, L1_attn_Wr, L1_ffn_router_w, L1_ffn_w13, L1_ffn_w2, L2_attn_W_in, L2_attn_b_in, L2_attn_conv_w, L2_attn_dt_bias, L2_attn_A_log, L2_attn_D, L2_attn_norm_w, L2_attn_W_out, L2_attn_b_out, L2_ffn_gate_W, L2_ffn_W1, L2_ffn_b1, L2_ffn_W2, L2_ffn_b2, L2_ffn_Ws1, L2_ffn_bs1, L2_ffn_Ws2, L2_ffn_bs2, L2_ffn_route_scale, L3_attn_W, L3_attn_b, L3_ffn_W1, L3_ffn_b1, L3_ffn_W2, L3_ffn_b2):

    def _L0_attn_ref(x, ln1_g, ln1_b, ln2_g, ln2_b, W1, b1, W2, b2, in_proj_w, conv_w, conv_b, x_proj_w, dt_proj_w, dt_proj_b, A_log, D_param, out_proj_w):
        import jax, jax.numpy as jnp
        from jax import lax
        import numpy as np
        D_MODEL = 128
        EXP = 2
        D_INNER = EXP * D_MODEL
        D_STATE = 16
        D_CONV = 4
        DT_RANK = 64
        NUM_GROUPS = 4
        BSZ, SEQ = (2, 256)
        EPS = 1e-05

        def _layernorm(x, g, b):
            m = jnp.mean(x, -1, keepdims=True)
            v = jnp.var(x, -1, keepdims=True)
            return (x - m) * lax.rsqrt(v + EPS) * g + b

        def _ste_sign(w):
            return w + lax.stop_gradient(jnp.sign(w) - w)

        def _quant_act_groupwise(x, b=8):
            Qb = float(2 ** (b - 1))
            B_, L, D = x.shape
            g = x.reshape(B_, NUM_GROUPS, L // NUM_GROUPS, D)
            gamma = jnp.max(jnp.abs(g), axis=(0, 2, 3), keepdims=True)
            q = jnp.clip(g * Qb / (gamma + EPS), -Qb + EPS, Qb - EPS)
            return q.reshape(B_, L, D)

        def _mamba(u, in_proj_w, conv_w, conv_b, x_proj_w, dt_proj_w, dt_proj_b, A_log, D_param, out_proj_w):
            B_, L, _ = u.shape
            xz = u @ in_proj_w.T
            xs, z = jnp.split(xz, 2, axis=-1)
            xt = jnp.transpose(xs, (0, 2, 1))
            xt = lax.conv_general_dilated(xt, conv_w, (1,), [(D_CONV - 1, 0)], feature_group_count=D_INNER, dimension_numbers=('NCH', 'OIH', 'NCH'))
            xt = xt + conv_b[None, :, None]
            xs = jax.nn.silu(jnp.transpose(xt, (0, 2, 1)))
            x_dbl = xs @ x_proj_w.T
            dt, Bm, Cm = jnp.split(x_dbl, [DT_RANK, DT_RANK + D_STATE], axis=-1)
            dt = jax.nn.softplus(dt @ dt_proj_w.T + dt_proj_b)
            A = -jnp.exp(A_log)

            def step(h, inp):
                dt_s, B_s, C_s, x_s = inp
                dA = jnp.exp(dt_s[..., None] * A)
                h = h * dA + (dt_s * x_s)[..., None] * B_s[:, None, :]
                y = jnp.einsum('bds,bs->bd', h, C_s)
                return (h, y)
            tm = lambda a: jnp.transpose(a, (1, 0, 2))
            h0 = jnp.zeros((B_, D_INNER, D_STATE), u.dtype)
            _, ys = lax.scan(step, h0, (tm(dt), tm(Bm), tm(Cm), tm(xs)))
            y = jnp.transpose(ys, (1, 0, 2)) + D_param * xs
            y = y * jax.nn.silu(z)
            return y @ out_proj_w.T
        qW1 = _ste_sign(W1)
        qW2 = _ste_sign(W2)
        gated = jnp.clip(_layernorm(x, ln1_g, ln1_b) @ qW1.T + b1, -1.0, 1.0)
        x = x + gated @ qW2.T + b2
        qx = _quant_act_groupwise(x)
        out = qx + _mamba(_layernorm(qx, ln2_g, ln2_b), in_proj_w, conv_w, conv_b, x_proj_w, dt_proj_w, dt_proj_b, A_log, D_param, out_proj_w)
        return out

    def _L0_ffn_ref(x, gate_w, gate_b, w1, b1, w2, b2, w3, b3):
        import jax, jax.numpy as jnp
        import numpy as np
        K = 2
        E = gate_w.shape[-1]
        logits = jnp.einsum('bsd,de->bse', x, gate_w) + gate_b
        probs = jax.nn.softmax(logits, axis=1)
        vals, idx = jax.lax.top_k(probs, K)
        h = jax.nn.relu(jnp.einsum('bsd,edo->ebso', x, w1) + b1[:, None, None, :])
        h = jax.nn.relu(jnp.einsum('ebso,eop->ebsp', h, w2) + b2[:, None, None, :])
        y = jax.nn.relu(jnp.einsum('ebso,eop->ebsp', h, w3) + b3[:, None, None, :])
        onehot = jax.nn.one_hot(idx, E, dtype=x.dtype)
        w_tok = jnp.einsum('bske,bsk->bse', onehot, vals)
        ind = onehot.max(axis=2)
        v = jnp.einsum('ebso,bse->eo', y, w_tok)
        out = jnp.einsum('bse,eo->bso', ind, v)
        return out

    def _L1_attn_ref(x, Wq, Wk, Wv, Wr):
        import jax, jax.numpy as jnp
        import numpy as np
        SCALE = 128 ** (-0.5)
        query = jnp.einsum('bsd,de->bse', x, Wq)
        key_ = jnp.einsum('bsd,de->bse', x, Wk)
        value = jnp.einsum('bsd,de->bse', x, Wv)
        alpha = jax.nn.softmax(query * SCALE, axis=-1)
        global_query = jnp.sum(query * alpha, axis=1)
        p = global_query[:, None, :] * key_
        beta = jax.nn.softmax(p * SCALE, axis=-1)
        global_key = jnp.sum(p * beta, axis=1)
        u = global_key[:, None, :] * value
        r = jnp.einsum('bsd,de->bse', u, Wr)
        return query + r

    def _L1_ffn_ref(x, router_w, w13, w2):
        import jax, jax.numpy as jnp
        import numpy as np
        E, H, I, K = (8, 128, 256, 2)
        B, S = (4, 256)
        logits = jnp.einsum('bsh,eh->bse', x, router_w)
        probs = jax.nn.softmax(logits, axis=-1)
        weights, indices = jax.lax.top_k(probs, K)
        weights = weights / (weights.sum(axis=-1, keepdims=True) + 1e-06)
        h13 = jnp.einsum('bsh,ehi->bsei', x, w13)
        gate, up = jnp.split(h13, 2, axis=-1)
        h = jax.nn.silu(gate) * up
        y = jnp.einsum('bsei,eih->bseh', h, w2)
        y_sel = jnp.take_along_axis(y, indices[..., None], axis=2)
        return (y_sel * weights[..., None]).sum(axis=2)

    def _L2_attn_ref(x, W_in, b_in, conv_w, dt_bias, A_log, D, norm_w, W_out, b_out):
        import jax, jax.numpy as jnp
        import numpy as np
        H, P, HID, N, G, K, CS = (32, 64, 128, 128, 1, 4, 32)
        INTER = H * P
        CONV_DIM = INTER + 2 * G * N
        PROJ = INTER + CONV_DIM + H
        EPS = 1e-05

        def segsum(x):
            T = x.shape[-1]
            xx = jnp.broadcast_to(x[..., None], x.shape + (T,))
            xx = jnp.where(jnp.tril(jnp.ones((T, T), bool), -1), xx, 0.0)
            s = jnp.cumsum(xx, axis=-2)
            return jnp.where(jnp.tril(jnp.ones((T, T), bool)), s, -jnp.inf)
        B_, S, _ = x.shape
        proj = x @ W_in.T + b_in
        gate = proj[..., :INTER]
        hBC = proj[..., INTER:INTER + CONV_DIM]
        dt = proj[..., INTER + CONV_DIM:]
        xp = jnp.pad(hBC, ((0, 0), (K - 1, 0), (0, 0)))
        conv = sum((xp[:, i:i + S, :] * conv_w[:, i] for i in range(K)))
        hBC = jax.nn.silu(conv)
        h = hBC[..., :INTER]
        Bm = hBC[..., INTER:INTER + G * N]
        Cm = hBC[..., INTER + G * N:]
        A = -jnp.exp(A_log.astype(jnp.float32))
        dt = jax.nn.softplus(dt + dt_bias)
        h = h.reshape(B_, S, H, P).astype(jnp.float32)
        Bm = jnp.tile(Bm.reshape(B_, S, G, N).astype(jnp.float32), (1, 1, H // G, 1))
        Cm = jnp.tile(Cm.reshape(B_, S, G, N).astype(jnp.float32), (1, 1, H // G, 1))
        pad = -S % CS
        D_res = D[..., None] * jnp.pad(h, ((0, 0), (0, pad), (0, 0), (0, 0)))
        h = h * dt[..., None]
        Adt = A * dt

        def chunk(t):
            t = jnp.pad(t, [(0, 0), (0, pad)] + [(0, 0)] * (t.ndim - 2))
            return t.reshape(B_, -1, CS, *t.shape[2:])
        h_c, B_c, C_c = (chunk(h), chunk(Bm), chunk(Cm))
        A_c = chunk(Adt).transpose(0, 3, 1, 2)
        A_cum = jnp.cumsum(A_c, axis=-1)
        Lmat = jnp.exp(segsum(A_c))
        Gm = jnp.einsum('bclhn,bcshn->bclsh', C_c, B_c)
        M = Gm * Lmat.transpose(0, 2, 3, 4, 1)
        Y_diag = jnp.einsum('bclsh,bcshp->bclhp', M, h_c)
        decay = jnp.exp(A_cum[..., -1:] - A_cum)
        B_decay = B_c * decay.transpose(0, 2, 3, 1)[..., None]
        states = jnp.einsum('bclhn,bclhp->bchpn', B_decay, h_c)
        states = jnp.concatenate([jnp.zeros_like(states[:, :1]), states], axis=1)
        dc = jnp.exp(segsum(jnp.pad(A_cum[..., -1], ((0, 0), (0, 0), (1, 0)))))
        states = jnp.einsum('bhij,bjhpn->bihpn', dc, states)[:, :-1]
        sdo = jnp.exp(A_cum).transpose(0, 2, 3, 1)
        Y_off = jnp.einsum('bclhn,bchpn->bclhp', C_c, states) * sdo[..., None]
        y = (Y_diag + Y_off).reshape(B_, -1, H, P) + D_res
        y = y[:, :S].reshape(B_, S, INTER)
        g = y * jax.nn.silu(gate.astype(jnp.float32))
        g = g * jax.lax.rsqrt(jnp.mean(g * g, axis=-1, keepdims=True) + EPS) * norm_w
        return g.astype(x.dtype) @ W_out.T + b_out

    def _L2_ffn_ref(x, gate_W, W1, b1, W2, b2, Ws1, bs1, Ws2, bs2, route_scale):
        import jax, jax.numpy as jnp
        import numpy as np
        B, S, D, E, H, K = (4, 256, 128, 8, 64, 2)
        scores = jax.nn.sigmoid(x @ gate_W) * route_scale
        topk_scores, topk_idx = jax.lax.top_k(scores, K)
        topk_w = topk_scores / topk_scores.sum(-1, keepdims=True)
        onehot = jax.nn.one_hot(topk_idx, E, dtype=x.dtype)
        gate_full = jnp.einsum('bsk,bske->bse', topk_w, onehot)
        h = jax.nn.gelu(jnp.einsum('bsd,edh->bseh', x, W1) + b1, approximate=False)
        y = jnp.einsum('bseh,ehd->bsed', h, W2) + b2
        expert_out = jnp.einsum('bse,bsed->bsd', gate_full, y)
        shared = jax.nn.gelu(x @ Ws1 + bs1, approximate=False) @ Ws2 + bs2
        return expert_out + shared

    def _L3_attn_ref(x, W, b):
        import jax, jax.numpy as jnp
        import numpy as np
        import math
        DK = 128
        qkv = jnp.einsum('btc,cd->btd', x, W) + b
        q, k, v = jnp.split(qkv, 3, axis=-1)
        scale = 1.0 / math.sqrt(DK)
        weights = jnp.einsum('btc,bTc->btT', q, k) * scale
        T = weights.shape[-1]
        mask = jnp.tril(jnp.ones((T, T), dtype=jnp.float32))
        logits = jnp.where(mask == 0, jnp.float32(-9000000000000000.0), weights)
        attention = jax.nn.softmax(logits, axis=-1)
        values = jnp.einsum('btT,bTc->btc', attention, v)
        return values

    def _L3_ffn_ref(hidden_states, W1, b1, W2, b2):
        import jax, jax.numpy as jnp
        import numpy as np
        HIDDEN = 128
        INTER = 512
        h = jax.nn.relu(jnp.einsum('bsh,hi->bsi', hidden_states, W1) + b1)
        return jnp.einsum('bsi,ih->bsh', h, W2) + b2
    x = L0_attn_x
    xn = _layernorm(x, axis=-1)
    s = _L0_attn_ref(xn, L0_attn_ln1_g, L0_attn_ln1_b, L0_attn_ln2_g, L0_attn_ln2_b, L0_attn_W1, L0_attn_b1, L0_attn_W2, L0_attn_b2, L0_attn_in_proj_w, L0_attn_conv_w, L0_attn_conv_b, L0_attn_x_proj_w, L0_attn_dt_proj_w, L0_attn_dt_proj_b, L0_attn_A_log, L0_attn_D_param, L0_attn_out_proj_w)
    g = _silu(_L0_ffn_ref(xn, L0_ffn_gate_w, L0_ffn_gate_b, L0_ffn_w1, L0_ffn_b1, L0_ffn_w2, L0_ffn_b2, L0_ffn_w3, L0_ffn_b3))
    x = x + s * g
    xn = _layernorm(x, axis=-1)
    s = _L1_attn_ref(xn, L1_attn_Wq, L1_attn_Wk, L1_attn_Wv, L1_attn_Wr)
    g = _silu(_L1_ffn_ref(xn, L1_ffn_router_w, L1_ffn_w13, L1_ffn_w2))
    x = x + s * g
    xn = _layernorm(x, axis=-1)
    s = _L2_attn_ref(xn, L2_attn_W_in, L2_attn_b_in, L2_attn_conv_w, L2_attn_dt_bias, L2_attn_A_log, L2_attn_D, L2_attn_norm_w, L2_attn_W_out, L2_attn_b_out)
    g = _silu(_L2_ffn_ref(xn, L2_ffn_gate_W, L2_ffn_W1, L2_ffn_b1, L2_ffn_W2, L2_ffn_b2, L2_ffn_Ws1, L2_ffn_bs1, L2_ffn_Ws2, L2_ffn_bs2, L2_ffn_route_scale))
    x = x + s * g
    xn = _layernorm(x, axis=-1)
    s = _L3_attn_ref(xn, L3_attn_W, L3_attn_b)
    g = _silu(_L3_ffn_ref(xn, L3_ffn_W1, L3_ffn_b1, L3_ffn_W2, L3_ffn_b2))
    x = x + s * g
    return x

_drawn_inputs = setup_inputs


def setup_inputs(seed=0):
    import zlib

    import numpy as np

    out = dict(_drawn_inputs(seed))
    spreads = {'L0_attn_ln1_g': (1.0, 0.2),
     'L0_attn_ln1_b': (0.0, 0.1),
     'L0_attn_ln2_g': (1.0, 0.2),
     'L0_attn_ln2_b': (0.0, 0.1),
     'L0_attn_b1': (0.0, 0.1),
     'L0_attn_b2': (0.0, 0.1),
     'L0_attn_conv_b': (0.0, 0.1),
     'L0_attn_D_param': (1.0, 0.2),
     'L2_attn_b_in': (0.0, 0.1),
     'L2_attn_D': (1.0, 0.2),
     'L2_attn_norm_w': (1.0, 0.2),
     'L2_attn_b_out': (0.0, 0.1),
     'L2_ffn_b1': (0.0, 0.1),
     'L2_ffn_b2': (0.0, 0.1),
     'L2_ffn_bs1': (0.0, 0.1),
     'L2_ffn_bs2': (0.0, 0.1),
     'L3_attn_b': (0.0, 0.1)}
    factors = {}
    for name, (base, spread) in spreads.items():
        noise = np.random.default_rng([zlib.crc32(name.encode()), seed]).standard_normal(out[name].shape)
        drawn = base * np.exp(spread * noise) if base else spread * noise
        out[name] = jnp.asarray(drawn.astype(out[name].dtype))
    for name, factor in factors.items():
        out[name] = (out[name] * factor).astype(out[name].dtype)
    return out
```

```python
from contextlib import ExitStack

import concourse.bass as bass
from concourse import mybir

ALU = mybir.AluOpType
ACT = mybir.ActivationFunctionType
AX = mybir.AxisListType
F32 = mybir.dt.float32
BF16 = mybir.dt.bfloat16
RMAX = bass.bass_isa.ReduceOp.max

P = 128
BATCH, SEQ = 2, 1024
T = BATCH * SEQ
BL = 512
NB = T // BL
NT = T // P
TB = SEQ // P
EPS = 1e-5
BIG = 1e30
E = 8

DI, DS, DR, DC = 256, 16, 64, 4
MI = DI // P
QB = 128.0
GROUPS = 4
GL = SEQ // GROUPS
I1 = 256
H2, P2, N2 = 32, 64, 128
INTER = H2 * P2
CT = INTER // P
HE = 64
F3 = 512

VECTORS = [
    ("ln1_g", 1), ("ln1_b", 1), ("ln2_g", 1), ("ln2_b", 1), ("b1", MI), ("b2", 1),
    ("conv_w", MI * DC), ("conv_b", MI), ("dt_b", MI), ("a_log", MI * DS), ("d", MI),
    ("gate_b", 1), ("fb1", E), ("fb2", E), ("fb3", E),
    ("bc_bias", 2), ("bc_conv", 2 * DC), ("b_out", 1), ("d2", CT),
    ("eb1", E * HE // P), ("sb1", 1), ("sb2", 1), ("route_scale", 1),
    ("b_q", 1), ("b_k", 1), ("b_v", 1), ("c1", F3 // P), ("c2", 1),
]
VCOL = {}
NV = 0
for _name, _n in VECTORS:
    VCOL[_name] = NV
    NV += _n

TILE_W = [("gate", P), ("h", P), ("out", P), ("gate_bias", 1), ("h_bias", 1), ("taps", DC), ("norm_w", 1)]
TW = sum(c for _, c in TILE_W)
TCOL = {n: sum(c for _, c in TILE_W[:k]) for k, (n, _) in enumerate(TILE_W)}

FIRST = [
    ("w1", P, DI), ("w2", P, MI * P), ("in_proj", P, 2 * DI), ("x_proj", P, MI * (DR + 2 * DS)),
    ("dt_proj", DR, DI), ("out_proj", P, MI * P), ("gate0", P, E),
    ("wq", P, P), ("wk", P, P), ("wvT", P, P), ("wr", P, P), ("router", P, E),
    ("w_dt", P, H2), ("gate2", P, E), ("eb2", 4 * E, P), ("sw1", P, HE), ("sw2", HE, P),
]
POOLED = [("f1", P, E * P), ("f2", P, E * P), ("f3", P, E * P)]
LATE = [
    ("w_bc", P, 2 * N2), ("ew1", P, E * HE), ("ew2", P, E * HE),
    ("qkv", P, 3 * P), ("g1", P, F3), ("g2", P, F3),
]
EXPERTS = [("w13", P, E * 2 * I1), ("w2e", P, E * I1)]


class Chain:

    def __init__(self, eng, sem):
        self.eng, self.sem, self.n, self.at = eng, sem, 0, None

    def __call__(self, ins):
        ins.then_inc(self.sem, 1)
        self.n += 1
        self.eng.wait_ge(self.sem, self.n if self.at is None else self.at + self.n)

    def later(self, ins):
        ins.then_inc(self.sem, 1)
        self.n += 1

    def due(self, but):
        self.eng.wait_ge(self.sem, (self.n if self.at is None else self.at + self.n) - but)

    def rounds(self, i, per):
        self.at, self.start, self.per = i * per, self.n, per

    def end(self, count):
        assert self.n - self.start == self.per, (self.n - self.start, self.per)
        self.n = self.start + self.per * count
        self.at = None


def build(nc, a, out, upto=4):
    ctx = ExitStack()
    with ctx:
        def sb(name, shape, dt=F32):
            return ctx.enter_context(nc.sbuf_tensor(name, shape, dt))

        def sems(prefix, names):
            return {n: ctx.enter_context(nc.semaphore(f"{prefix}_{n}")) for n in names.split()}

        def stages(prefix, each, **engines):
            ns = sems(prefix, each)
            for eng, names in engines.items():
                ns[eng] = ctx.enter_context(nc.semaphore(f"{prefix}_{eng}"))
                at = 0
                for item in names.split():
                    name, count = item.split(":")
                    ns[name] = at
                    at += int(count)
            return ns

        ps = ctx.enter_context(nc.psum_tensor("ps", [P, 8, BL], F32))
        W = {n: sb("w_" + n, [p, c])[:, :] for n, p, c in FIRST}
        shared = sb("shared", [P, max(sum(c for _, _, c in g) for g in (POOLED, LATE))])
        vec = sb("vec", [P, NV])
        work = sb("work", [P, 14 * T])
        ones_d = sb("ones_d", [P, P])
        ones_n = sb("ones_n", [P, P])
        ones_1 = sb("ones_1", [P, P])
        upper = sb("upper", [P, P])
        zero = sb("zero", [P, P])
        ident = sb("ident", [P, P])
        ident_b = sb("ident_b", [P, P], BF16)
        mask_t = sb("mask_t", [P, 4, P], BF16)
        mask_q = sb("mask_q", [P, P], BF16)
        sel = sb("sel", [96, H2, P], BF16)
        sel2 = sb("sel2", [96, H2, P2], BF16)
        selr = sb("selr", [4 * E, E, P], BF16)
        selr2 = sb("selr2", [4 * E, E, HE], BF16)
        tie = sb("tie", [P, NT, E])
        eps_t = sb("eps_t", [P, 1])
        A = sb("A", [P, MI * DS])
        ssum = sb("ssum", [P, BATCH, SEQ])
        sq, lnv = ssum[:, 0, :].rearrange("p (k t) -> p k t", t=BL), ssum[:, 1, :].rearrange("p (k t) -> p k t", t=BL)
        rs = sb("rs", [P, 2, BL])
        gam = sb("gam", [P, 4, 8])
        rt = sb("rt", [P, NT, 4 * E])
        rw = sb("rw", [P, 6, NT, E])
        rm = sb("rm", [P, 4, NT])
        rwb = sb("rwb", [P, 2, NT, E], BF16)
        rtf = sb("rtf", [4 * E, T])
        rtb = sb("rtb", [4 * E, T], BF16)
        pad = work[:, 11 * T:11 * T + 2 * BATCH * (DC - 1 + SEQ)].rearrange("p (j t) -> p j t", j=2 * BATCH)
        parts = sb("parts", [96, T], BF16)
        part_tmp = sb("part_tmp", [32, BL], BF16)
        gmx = sb("gmx", [P, 4])
        gsm = sb("gsm", [P, 4])
        vacc = sb("vacc", [P, E * NB])
        vsum = sb("vsum", [P, E])
        vT = sb("vT", [E, P])
        wks = sb("wks", [P, BATCH, P])
        wvs = sb("wvs", [P, BATCH, P])
        wcomb = sb("wcomb", [P, BATCH, P])
        w_t = sb("w_t", [P, 2, TW])
        wo_t = sb("wo_t", [P, 2, P])
        dtr = sb("dtr", [P, 3 * H2])
        stat = sb("stat", [P, 4, NT])

        def V(name, k=0, p=P):
            return vec[0:p, VCOL[name] + k:VCOL[name] + k + 1]

        def blk(t, k):
            return t[:, k * BL:(k + 1) * BL]

        for group in (POOLED, LATE):
            at = 0
            for n, _, c in group:
                W[n] = shared[:, at:at + c]
                at += c
        slot = lambda n: work[:, n * T:(n + 1) * T]
        slots = lambda n, m: work[:, n * T:(n + m) * T]
        W["w13"] = slots(9, 2)
        W["w2e"] = slot(11)
        X = slot(0)
        XN = slot(1)
        S = slot(2)

        load = sems("load", "x vec weights pooled late experts row")
        const = sems("const", "fill ready")
        act_own, dve_own, pool_own = (ctx.enter_context(nc.semaphore(n)) for n in ("act_own", "dve_own", "pool_own"))
        NORM = "mean centred square var log rstd out"
        norm = sems("norm", NORM)
        m0 = stages("m0", pe="up:8 down:4 proj:16 xd:8 dtp:8 outp:4",
                    act="sign:3 biased:8 evac:16 xs:4 xd_out:4 e_ready:8",
                    dve="weff:1 gated:8 x1:4 peak:1 scaled:4 conv:4 bc:4 delta:8 dtx:4 ygate:4 s_out:4",
                    each="gamma b_ready c_ready ysum decay drive scan state")
        f0 = stages("f0", pe="logit:4 probs_T:1 picked_T:1 vT:1 mix:4", act="lg:4 exps:2 v_out:1 g:4",
                    dve="top:2 probs:2 picked:1 v:1 x_out:4", each="rt_out h1 h2 h3 wbc r1 r2 r3 pooled")
        m1 = stages("m1", pe="q:4 logit:1 gq:2 p:4 gk:2 comb:2 s:4", act="q_exp:4 exps:1 p_exp:4 s_out:4",
                    dve="q_sub:4 q_weighted:4 sub:1 wk_scaled:2 p_sub:4 p_weighted:4 wv_scaled:2 comb_out:2", each="")
        f1 = stages("f1", pe="picked_T:1", act="g:4", dve="picked:1 x_out:4", each="rt_out wbc xw gate silu up h y")
        m2 = stages("m2", pe="dt_mm:1 cum:1 tot:1 cumT:1 bc_mm:8 bt:4 gt:4 rms:4",
                    act="arow:1 dt_soft:1 dec:1 cdec:1 neg:4 bc_pad:8 bc:4 bt_out:4 rstd:4",
                    dve="row:1 dt_biased:1 dt:1 adt:1 acum:1 dec_sub:1 parts:4 bc_conv:4 gt_out:4 s_out:4",
                    each="w_in0 w_in1 h_mm h_pad g_mm sg conv hc tr hdt hdd arg L sdo_mm sdo st rec M yoff ydiag yd yoff_used y sqr ss wo outp first_out")
        f2 = stages("f2", pe="logit:1 picked_T:1 y:4", act="sig:1 y_out:4 g:4", dve="picked:1 x_out:4", each="rt_out h gelu wbc hw")
        m3 = stages("m3", pe="qk:8 v:4", act="qk_out:8 v_out:4", dve="s_out:2", each="s peak e p pT pT_out o o_out")
        f3 = stages("f3", pe="y:4", act="g:4", dve="x_out:4", each="h relu")
        ends = [f0, f1, f2, f3]
        done = sems("done", "stored")
        block = ctx.enter_context(nc.Block())

        def norm_pe(pe, r, src, ready=None, ready_at=0):
            def var(k):
                pe.wait_ge(norm["square"], NB * r + k + 1)
                if k >= 2:
                    pe.wait_ge(norm["log"], NB * r + k - 1)
                pe.matmul(ps[:, 2 + k % 2, :], ones_d[:, :], sq[:, k % 2, :], start=True, stop=True).then_inc(norm["var"], 1)

            for k in range(NB):
                if ready is not None:
                    pe.wait_ge(ready, ready_at + k + 1)
                if k >= 2:
                    pe.wait_ge(norm["centred"], NB * r + k - 1)
                pe.matmul(ps[:, k % 2, :], ones_d[:, :], blk(src, k), start=True, stop=True).then_inc(norm["mean"], 1)
                if k >= 1:
                    var(k - 1)
            var(NB - 1)

        def norm_dve(dve, own, r, src, dst, gain=None, bias=None):
            def scale(k):
                dve.wait_ge(norm["rstd"], NB * r + k + 1)
                mul = dve.tensor_tensor(blk(dst, k), blk(dst, k), rs[:, k % 2, :], ALU.mult)
                if gain is None:
                    mul.then_inc(norm["out"], 1)
                else:
                    own(mul)
                    dve.tensor_scalar(blk(dst, k), blk(dst, k), gain, bias, ALU.mult, ALU.add).then_inc(norm["out"], 1)

            for k in range(NB):
                dve.wait_ge(norm["mean"], NB * r + k + 1)
                dve.tensor_tensor(blk(dst, k), blk(src, k), ps[:, k % 2, :], ALU.subtract).then_inc(norm["centred"], 1)
                if k >= 1:
                    scale(k - 1)
            scale(NB - 1)

        def norm_act(act, r, dst):
            def root(k):
                act.wait_ge(norm["var"], NB * r + k + 1)
                act.activation(lnv[:, k % 2, :], ps[:, 2 + k % 2, :], ACT.Ln, bias=eps_t[:, :]).then_inc(norm["log"], 1)
                act.wait_ge(norm["log"], NB * r + k + 1)
                if k >= 2:
                    act.wait_ge(norm["out"], NB * r + k - 1)
                act.activation(rs[:, k % 2, :], lnv[:, k % 2, :], ACT.Exp, scale=-0.5).then_inc(norm["rstd"], 1)

            act.preload_act_table_set("natural_log_exp_and_others")
            for k in range(NB):
                act.wait_ge(norm["centred"], NB * r + k + 1)
                if k >= 2:
                    act.wait_ge(norm["var"], NB * r + k - 1)
                act.activation(sq[:, k % 2, :], blk(dst, k), ACT.Square).then_inc(norm["square"], 1)
                if k >= 1:
                    root(k - 1)
            root(NB - 1)

        def top2(dve, own, score, ind):
            cur, eq, t, pick = rw[:, 2], rw[:, 3], rw[:, 4], rw[:, 5]
            bc = lambda m: m.unsqueeze(2).to_broadcast([P, NT, E])
            for k in range(2):
                s = score if k == 0 else cur
                own(dve.tensor_reduce(rm[:, 0, :], s, AX.X, ALU.max))
                own(dve.tensor_tensor(eq, s, bc(rm[:, 0, :]), ALU.is_equal))
                own(dve.tensor_tensor(t, eq, tie[:, :, :], ALU.mult))
                own(dve.tensor_reduce(rm[:, 1, :], t, AX.X, ALU.max))
                if k == 0:
                    own(dve.tensor_tensor(ind, t, bc(rm[:, 1, :]), ALU.is_equal))
                    own(dve.scalar_tensor_tensor(cur, ind, -BIG, score, ALU.mult, ALU.add))
                else:
                    own(dve.tensor_tensor(pick, t, bc(rm[:, 1, :]), ALU.is_equal))
                    own(dve.tensor_tensor(ind, ind, pick, ALU.add))

        def split3(dve, own, w):
            hi, mid, lo = (rt[:, :, E * (k + 1):E * (k + 2)] for k in range(3))
            rest = rw[:, 3]
            own(dve.tensor_copy(rwb[:, 0], w))
            own(dve.tensor_copy(hi, rwb[:, 0]))
            own(dve.tensor_tensor(rest, w, hi, ALU.subtract))
            own(dve.tensor_copy(rwb[:, 1], rest))
            own(dve.tensor_copy(mid, rwb[:, 1]))
            return dve.tensor_tensor(lo, rest, mid, ALU.subtract)

        X1, H0 = slot(6), slot(3)
        gated = [slot(4), slot(5)]
        zgate = [slot(4), slot(5)]
        seqs = lambda n: slots(n, 2).rearrange("p (b t) -> p b t", t=SEQ)
        XS, DL, DX = seqs(7), seqs(9), seqs(11)
        dA = slot(13).rearrange("p (k t) -> p k t", t=SEQ)
        HS = slot(3).rearrange("p (k t) -> p k t", t=SEQ)
        tmp4 = slot(13).rearrange("p (k t) -> p k t", t=BL)
        dt_low = slot(11)[0:DR, :]
        bc_rest = slot(12)[0:32, :].rearrange("p (k t) -> p k t", t=BL)

        def l0_pe(pe):
            pe.wait_ge(f0["act"], f0["v_out"] + 1)
            norm_pe(pe, 1, XN, norm["out"])
            pe.wait_ge(m0["dve"], m0["weff"] + 1)
            for k in range(NB):
                pe.wait_ge(norm["out"], NB * 1 + k + 1)
                for m in range(MI):
                    n = MI * k + m
                    if n >= 4:
                        pe.wait_ge(m0["act"], m0["biased"] + n - 3)
                    pe.matmul(ps[:, 4 + n % 4, :], W["w1"][:, m * P:(m + 1) * P], blk(H0, k),
                              start=True, stop=True).then_inc(m0["pe"], 1)
            for k in range(NB):
                pe.wait_ge(m0["dve"], m0["gated"] + MI * (k + 1))
                for m in range(MI):
                    mm = pe.matmul(ps[:, k, :], W["w2"][:, m * P:(m + 1) * P], blk(gated[m], k),
                                   start=(m == 0), stop=(m == MI - 1))
                mm.then_inc(m0["pe"], 1)
            norm_pe(pe, 2, X1, m0["dve"], m0["scaled"])
            for k in range(NB):
                pe.wait_ge(norm["out"], NB * 2 + k + 1)
                for m in range(2 * MI):
                    n = 2 * MI * k + m
                    if n >= 4:
                        pe.wait_ge(m0["act"], m0["evac"] + n - 3)
                    pe.matmul(ps[:, 4 + m, :], W["in_proj"][:, m * P:(m + 1) * P], blk(H0, k),
                              start=True, stop=True).then_inc(m0["pe"], 1)
            for k in range(NB):
                b, h = divmod(k, NB // BATCH)
                pe.wait_ge(m0["act"], m0["xs"] + MI * (b + 1))
                if k >= 2:
                    pe.wait_ge(m0["act"], m0["xd_out"] + k - 1)
                    pe.wait_ge(m0["dve"], m0["bc"] + k - 1)
                for part, (c0, c1) in enumerate(((0, DR), (DR, DR + 2 * DS))):
                    for m in range(MI):
                        mm = pe.matmul(ps[0:c1 - c0, 2 * (k % 2) + part, :],
                                       W["x_proj"][:, m * (DR + 2 * DS) + c0:m * (DR + 2 * DS) + c1],
                                       XS[:, MI * b + m, h * BL:(h + 1) * BL], start=(m == 0), stop=(m == MI - 1))
                    mm.then_inc(m0["pe"], 1)
            for k in range(NB):
                pe.wait_ge(m0["act"], m0["xd_out"] + k + 1)
                for m in range(MI):
                    n = MI * k + m
                    if n >= 4:
                        pe.wait_ge(m0["dve"], m0["delta"] + n - 3)
                    pe.matmul(ps[:, 4 + n % 4, :], W["dt_proj"][:, m * P:(m + 1) * P], blk(dt_low, k),
                              start=True, stop=True).then_inc(m0["pe"], 1)

            def spread(j, s, n):
                for which, used, ready in ((0, m0["drive"], m0["b_ready"]), (DS, m0["state"], m0["c_ready"])):
                    if not (isinstance(n, int) and n == 0):
                        pe.wait_ge(used, n)
                    for h in range(2):
                        mm = pe.matmul(ps[:, 2 * (which // DS) + h, :], sel[:, which + s, :],
                                       parts[:, (j // MI) * SEQ + h * BL:(j // MI) * SEQ + (h + 1) * BL],
                                       start=True, stop=True)
                    mm.then_inc(ready, 1)

            def ysum(j, n, start, stop):
                pe.wait_ge(m0["state"], n + 1)
                for h in range(2):
                    mm = pe.matmul(ps[:, 4 + 2 * (j % 2) + h, :], ident[:, :],
                                   HS[:, par(n), h * BL:(h + 1) * BL], start=start, stop=stop, skip_group_check=True)
                mm.then_inc(m0["ysum"], 1)

            par = lambda n: self_par[0]
            self_par = [0]
            pe.wait_ge(m0["dve"], m0["bc"] + NB)
            for j in range(BATCH * MI):
                n0_ = DS * j
                spread(j, 0, n0_)
                spread(j, 1, n0_ + 1)
                if j >= 2:
                    pe.wait_ge(m0["dve"], m0["ygate"] + j - 1)
                if j == 0:
                    pe.wait_ge(m0["dve"], m0["delta"] + MI * NB)
                self_par[0] = 0
                ysum(j, n0_, True, False)
                with pe.Fori(0, DS // 2 - 1) as i:
                    for u in range(2):
                        spread(j, i * 2 + (2 + u), i * 2 + (n0_ + 2 + u))
                        self_par[0] = (1 + u) % 2
                        ysum(j, i * 2 + (n0_ + 1 + u), False, False)
                self_par[0] = 1
                ysum(j, n0_ + DS - 1, False, True)
            for k in range(NB):
                b, h = divmod(k, NB // BATCH)
                pe.wait_ge(m0["dve"], m0["ygate"] + MI * (b + 1))
                for m in range(MI):
                    mm = pe.matmul(ps[:, k, :], W["out_proj"][:, m * P:(m + 1) * P],
                                   XS[:, MI * b + m, h * BL:(h + 1) * BL], start=(m == 0), stop=(m == MI - 1))
                mm.then_inc(m0["pe"], 1)

        def l0_act(act, own):
            act.activation(tmp4[:, 0, 0:DI], W["w1"][:, :], ACT.Sign).then_inc(m0["act"], 1)
            act.activation(tmp4[:, 1, 0:DI], W["w2"][:, :], ACT.Sign).then_inc(m0["act"], 1)
            act.activation(A[:, :], vec[:, VCOL["a_log"]:VCOL["a_log"] + MI * DS], ACT.Exp).then_inc(m0["act"], 1)
            norm_act(act, 1, H0)
            for k in range(NB):
                for m in range(MI):
                    act.wait_ge(m0["pe"], m0["up"] + MI * k + m + 1)
                    act.activation(blk(gated[m], k), ps[:, 4 + (MI * k + m) % 4, :], ACT.Identity,
                                   bias=V("b1", m)).then_inc(m0["act"], 1)
            norm_act(act, 2, H0)
            for k in range(NB):
                b, h = divmod(k, NB // BATCH)
                for m in range(2 * MI):
                    act.wait_ge(m0["pe"], m0["proj"] + 2 * MI * k + m + 1)
                    if m < MI:
                        act.activation(pad[:, MI * b + m, DC - 1 + h * BL:DC - 1 + (h + 1) * BL], ps[:, 4 + m, :],
                                       ACT.Copy).then_inc(m0["act"], 1)
                    else:
                        act.activation(blk(zgate[m - MI], k), ps[:, 4 + m, :], ACT.Silu).then_inc(m0["act"], 1)
            for j in range(BATCH * MI):
                act.wait_ge(m0["dve"], m0["conv"] + j + 1)
                act.activation(XS[:, j, :], DL[:, j, :], ACT.Silu).then_inc(m0["act"], 1)
            for k in range(NB):
                act.wait_ge(m0["pe"], m0["xd"] + 2 * k + 1)
                act.activation(blk(dt_low, k), ps[0:DR, 2 * (k % 2), :], ACT.Copy).then_inc(m0["act"], 1)
            act.preload_act_table_set("natural_log_exp_and_others")
            for k in range(NB):
                for m in range(MI):
                    n = MI * k + m
                    act.wait_ge(m0["pe"], m0["dtp"] + n + 1)
                    if n >= 2:
                        act.wait_ge(m0["dve"], m0["delta"] + n - 1)
                    t = tmp4[:, n % 2, :]
                    own(act.activation(t, ps[:, 4 + n % 4, :], ACT.Abs, bias=V("dt_b", m)))
                    own(act.activation(t, t, ACT.Exp, scale=-1.0))
                    act.activation(t, t, ACT.Ln, bias=1.0).then_inc(m0["act"], 1)
            act.wait_ge(m0["dve"], m0["delta"] + MI * NB)
            for j in range(BATCH * MI):
                def decay(s, n, u, first):
                    if not first:
                        act.wait_ge(m0["scan"], n - 1)
                    act.activation(dA[:, u, :], DL[:, j, :], ACT.Exp,
                                   scale=A[:, bass.ds((j % MI) * DS + s, 1)]).then_inc(m0["decay"], 1)

                if j == 0:
                    decay(0, 0, 0, True)
                    decay(1, 1, 1, True)
                with act.Fori(0 if j else 1, DS // 2) as i:
                    for u in range(2):
                        decay(i * 2 + u, i * 2 + (DS * j + u), u, False)

        def l0_dve(dve, own):
            own(dve.memset(pad[:, :, 0:DC - 1], 0.0))
            dve.wait_ge(m0["act"], m0["sign"] + 3)
            for n, w in enumerate((W["w1"], W["w2"])):
                own(dve.tensor_tensor(tmp4[:, n, 0:DI], tmp4[:, n, 0:DI], w[:, :], ALU.subtract))
                own(dve.tensor_tensor(w[:, :], w[:, :], tmp4[:, n, 0:DI], ALU.add))
            dve.tensor_scalar(A[:, :], A[:, :], -1.0, None, ALU.mult).then_inc(m0["dve"], 1)
            norm_dve(dve, own, 1, XN, H0, V("ln1_g"), V("ln1_b"))
            for k in range(NB):
                for m in range(MI):
                    dve.wait_ge(m0["act"], m0["biased"] + MI * k + m + 1)
                    dve.tensor_scalar(blk(gated[m], k), blk(gated[m], k), 1.0, -1.0, ALU.min, ALU.max).then_inc(m0["dve"], 1)
            for k in range(NB):
                dve.wait_ge(m0["pe"], m0["down"] + k + 1)
                dve.scalar_tensor_tensor(blk(X1, k), ps[:, k, :], V("b2"), blk(XN, k), ALU.add, ALU.add).then_inc(m0["dve"], 1)
            dve.wait_ge(m0["dve"], m0["x1"] + NB)
            own(dve.tensor_reduce(gam[:, 0, :], X1.rearrange("p (g t) -> p g t", t=GL), AX.X, ALU.max,
                                  apply_absolute_value=True))
            dve.tensor_tensor(gam[:, 1, 0:GROUPS], gam[:, 0, 0:GROUPS], gam[:, 0, GROUPS:], ALU.max).then_inc(m0["dve"], 1)
            dve.wait_ge(m0["gamma"], 1)
            g = gam[:, 3, 0:GROUPS]
            own(dve.tensor_scalar(g, gam[:, 2, 0:GROUPS], EPS, None, ALU.add))
            own(dve.reciprocal(g, g))
            own(dve.tensor_scalar(g, g, QB, None, ALU.mult))
            lim = QB - EPS
            for k in range(NB):
                for h in range(BL // GL):
                    part = X1[:, k * BL + h * GL:k * BL + (h + 1) * GL]
                    q = (k * BL // GL + h) % GROUPS
                    own(dve.tensor_scalar(part, part, gam[:, 3, q:q + 1], lim, ALU.mult, ALU.min))
                dve.tensor_scalar(blk(X1, k), blk(X1, k), -lim, None, ALU.max).then_inc(m0["dve"], 1)
            norm_dve(dve, own, 2, X1, H0, V("ln2_g"), V("ln2_b"))
            for b in range(BATCH):
                dve.wait_ge(m0["act"], m0["evac"] + 2 * MI * (NB // BATCH) * (b + 1))
                for m in range(MI):
                    j = MI * b + m
                    own(dve.tensor_scalar(DL[:, j, :], pad[:, j, DC - 1:DC - 1 + SEQ], V("conv_w", m * DC + DC - 1),
                                          V("conv_b", m), ALU.mult, ALU.add))
                    for i in range(DC - 1):
                        c = dve.scalar_tensor_tensor(DL[:, j, :], pad[:, j, i:i + SEQ], V("conv_w", m * DC + i),
                                                     DL[:, j, :], ALU.mult, ALU.add)
                        if i < DC - 2:
                            own(c)
                    c.then_inc(m0["dve"], 1)
            for k in range(NB):
                dve.wait_ge(m0["pe"], m0["xd"] + 2 * k + 2)
                if k == 0:
                    dve.wait_ge(const["ready"], 1)
                src = ps[0:32, 2 * (k % 2) + 1, :]
                r, tb = bc_rest[:, k % 2, :], part_tmp[0:32, :]
                own(dve.tensor_copy(blk(parts[0:32, :], k), src))
                own(dve.tensor_tensor(r, src, blk(parts[0:32, :], k), ALU.subtract))
                own(dve.tensor_copy(tb, r))
                own(dve.tensor_copy(blk(parts[32:64, :], k), tb))
                own(dve.tensor_tensor(r, r, tb, ALU.subtract))
                dve.tensor_copy(blk(parts[64:96, :], k), r).then_inc(m0["dve"], 1)
            dve.wait_ge(m0["act"], m0["xs"] + BATCH * MI)
            dve.wait_ge(m0["dve"], m0["bc"] + NB)
            for k in range(NB):
                b, h = divmod(k, NB // BATCH)
                for m in range(MI):
                    n, j = MI * k + m, MI * b + m
                    d = DL[:, j, h * BL:(h + 1) * BL]
                    dve.wait_ge(m0["act"], m0["e_ready"] + n + 1)
                    own(dve.tensor_scalar(d, ps[:, 4 + n % 4, :], V("dt_b", m), 0.0, ALU.add, ALU.max))
                    dve.tensor_tensor(d, d, tmp4[:, n % 2, :], ALU.add).then_inc(m0["dve"], 1)
            dve.wait_ge(m0["dve"], m0["delta"] + MI * NB)
            dve.wait_ge(m0["pe"], m0["dtp"] + MI * NB)
            for j in range(BATCH * MI):
                dve.tensor_tensor(DX[:, j, :], DL[:, j, :], XS[:, j, :], ALU.mult).then_inc(m0["dve"], 1)
            dve.wait_ge(m0["dve"], m0["dtx"] + BATCH * MI)
            for j in range(BATCH * MI):
                def state(n, u, first):
                    hs = HS[:, u, :]
                    dve.wait_ge(m0["b_ready"], n + 1)
                    if not first:
                        dve.wait_ge(m0["ysum"], n - 1)
                    dve.tensor_tensor(hs.rearrange("p (h t) -> p h t", t=BL), DX[:, j, :].rearrange("p (h t) -> p h t", t=BL),
                                      ps[:, 0:2, :], ALU.mult).then_inc(m0["drive"], 1)
                    dve.wait_ge(m0["drive"], n + 1)
                    dve.wait_ge(m0["decay"], n + 1)
                    dve.tensor_tensor_scan(hs, dA[:, u, :], hs, 0.0, ALU.mult, ALU.add).then_inc(m0["scan"], 1)
                    dve.wait_ge(m0["scan"], n + 1)
                    dve.wait_ge(m0["c_ready"], n + 1)
                    dve.tensor_tensor(hs.rearrange("p (h t) -> p h t", t=BL), hs.rearrange("p (h t) -> p h t", t=BL),
                                      ps[:, 2:4, :], ALU.mult).then_inc(m0["state"], 1)

                if j == 0:
                    state(0, 0, True)
                    state(1, 1, True)
                with dve.Fori(0 if j else 1, DS // 2) as i:
                    for u in range(2):
                        state(i * 2 + (DS * j + u), u, False)
                dve.wait_ge(m0["ysum"], DS * (j + 1))
                own(dve.scalar_tensor_tensor(XS[:, j, :].rearrange("p (h t) -> p h t", t=BL),
                                             XS[:, j, :].rearrange("p (h t) -> p h t", t=BL), V("d", j % MI),
                                             ps[:, 4 + 2 * (j % 2):6 + 2 * (j % 2), :], ALU.mult, ALU.add))
                dve.tensor_tensor(XS[:, j, :], XS[:, j, :], zgate[j % MI][:, (j // MI) * SEQ:(j // MI + 1) * SEQ],
                                  ALU.mult).then_inc(m0["dve"], 1)
            for k in range(NB):
                dve.wait_ge(m0["pe"], m0["outp"] + k + 1)
                dve.tensor_tensor(blk(S, k), ps[:, k, :], blk(X1, k), ALU.add).then_inc(m0["dve"], 1)

        def l0_pool(pool):
            pool.wait_ge(m0["dve"], m0["peak"] + 1)
            pool.partition_all_reduce(gam[:, 2, 0:GROUPS], gam[:, 1, 0:GROUPS], P, RMAX).then_inc(m0["gamma"], 1)

        def picked_pe(pe, g):
            pe.wait_ge(g["dve"], g["picked"] + 1)
            for i in range(NT):
                mm = pe.transpose(ps[0:4 * E, 4 + i // 4, (i % 4) * P:(i % 4 + 1) * P], rt[:, i, :], ident[:, :])
            mm.then_inc(g["pe"], 1)

        def picked_out_act(act, g):
            act.wait_ge(g["rt_out"], 1)
            act.activation(rtb[:, :], rtf[:, :], ACT.Copy).then_inc(g["rt_out"], 1)

        def picked_out_dve(dve, g):
            dve.wait_ge(g["pe"], g["picked_T"] + 1)
            dve.tensor_copy(rtf[:, :].rearrange("p (k t) -> p k t", t=BL), ps[0:4 * E, 4:8, :]).then_inc(g["rt_out"], 1)

        lg, pr = slot(11)[0:E, :], slot(12)[0:E, :]
        fh = [[blk(slot(4 + q), u) for u in range(4)] for q in range(3)]

        def f0_pe(pe):
            for k in range(NB):
                pe.wait_ge(norm["out"], NB * 0 + k + 1)
                pe.matmul(ps[0:E, 4 + k, :], W["gate0"][:, :], blk(XN, k), start=True, stop=True).then_inc(f0["pe"], 1)
            pe.wait_ge(f0["dve"], f0["probs"] + BATCH)
            for i in range(NT):
                mm = pe.transpose(ps[:, 0, i * E:(i + 1) * E], pr[:, i * P:(i + 1) * P], ident[0:E, 0:E])
            mm.then_inc(f0["pe"], 1)
            picked_pe(pe, f0)
            pe.wait_ge(f0["rt_out"], 2)
            N = E * NB
            for n in range(N + 2):
                if n < N:
                    e, k = divmod(n, NB)
                    if n >= 2:
                        pe.wait_ge(f0["r1"], n - 1)
                    pe.matmul(ps[:, n % 2, :], W["f1"][:, e * P:(e + 1) * P], blk(XN, k), start=True, stop=True).then_inc(f0["h1"], 1)
                if 1 <= n < N + 1:
                    q = n - 1
                    pe.wait_ge(f0["r1"], q + 1)
                    if q >= 2:
                        pe.wait_ge(f0["r2"], q - 1)
                    pe.matmul(ps[:, 2 + q % 2, :], W["f2"][:, (q // NB) * P:(q // NB + 1) * P], fh[0][q % 4],
                              start=True, stop=True).then_inc(f0["h2"], 1)
                if n >= 2:
                    q = n - 2
                    pe.wait_ge(f0["r2"], q + 1)
                    if q >= 2:
                        pe.wait_ge(f0["r3"], q - 1)
                        pe.wait_ge(f0["pooled"], q - 1)
                    pe.matmul(ps[:, 4 + q % 2, :], W["f3"][:, (q // NB) * P:(q // NB + 1) * P], fh[1][q % 4],
                              start=True, stop=True).then_inc(f0["h3"], 1)
                    pe.matmul(ps[:, 6 + q % 2, :], selr[:, q // NB, :], blk(rtb, q % NB),
                              start=True, stop=True).then_inc(f0["wbc"], 1)
            pe.wait_ge(f0["dve"], f0["v"] + 1)
            pe.transpose(ps[0:E, 0, 0:P], vsum[:, :], ident[:, :]).then_inc(f0["pe"], 1)

        def f0_mix_pe(pe):
            pe.wait_ge(f0["act"], f0["v_out"] + 1)
            for k in range(NB):
                pe.matmul(ps[:, 4 + k, :], vT[:, :], blk(rtf[0:E, :], k), start=True, stop=True).then_inc(f0["pe"], 1)

        def f0_act(act, own):
            for k in range(NB):
                act.wait_ge(f0["pe"], f0["logit"] + k + 1)
                act.activation(blk(lg, k), ps[0:E, 4 + k, :], ACT.Identity, bias=V("gate_b", 0, E)).then_inc(f0["act"], 1)
            for b in range(BATCH):
                act.wait_ge(f0["dve"], f0["top"] + b + 1)
                act.activation(pr[:, b * SEQ:(b + 1) * SEQ], lg[:, b * SEQ:(b + 1) * SEQ], ACT.Exp,
                               bias=gmx[0:E, b:b + 1], accum_out=gsm[0:E, b:b + 1]).then_inc(f0["act"], 1)
            picked_out_act(act, f0)
            N = E * NB
            for n in range(N + 1):
                if n < N:
                    act.wait_ge(f0["h1"], n + 1)
                    if n >= 4:
                        act.wait_ge(f0["h2"], n - 3)
                    act.activation(fh[0][n % 4], ps[:, n % 2, :], ACT.Relu, bias=V("fb1", n // NB)).then_inc(f0["r1"], 1)
                if n >= 1:
                    q = n - 1
                    act.wait_ge(f0["h3"], q + 1)
                    if q >= 4:
                        act.wait_ge(f0["pooled"], q - 3)
                    act.activation(fh[2][q % 4], ps[:, 4 + q % 2, :], ACT.Relu, bias=V("fb3", q // NB)).then_inc(f0["r3"], 1)
            act.wait_ge(f0["pe"], f0["vT"] + 1)
            act.activation(vT[:, :], ps[0:E, 0, 0:P], ACT.Copy).then_inc(f0["act"], 1)

        def f0_dve(dve, own):
            for b in range(BATCH):
                dve.wait_ge(f0["act"], f0["lg"] + (b + 1) * NB // BATCH)
                dve.tensor_reduce(gmx[0:E, b:b + 1], lg[:, b * SEQ:(b + 1) * SEQ], AX.X, ALU.max, negate=True).then_inc(f0["dve"], 1)
            dve.wait_ge(f0["act"], f0["exps"] + BATCH)
            own(dve.reciprocal(gsm[0:E, 2:4], gsm[0:E, 0:2]))
            for b in range(BATCH):
                dve.tensor_scalar(pr[:, b * SEQ:(b + 1) * SEQ], pr[:, b * SEQ:(b + 1) * SEQ], gsm[0:E, 2 + b:3 + b], None,
                                  ALU.mult).then_inc(f0["dve"], 1)
            dve.wait_ge(f0["pe"], f0["probs_T"] + 1)
            own(dve.tensor_copy(rw[:, 0], ps[:, 0, 0:NT * E].rearrange("p (i e) -> p i e", e=E)))
            top2(dve, own, rw[:, 0], rt[:, :, 0:E])
            own(dve.tensor_tensor(rw[:, 1], rw[:, 0], rt[:, :, 0:E], ALU.mult))
            split3(dve, own, rw[:, 1]).then_inc(f0["dve"], 1)
            picked_out_dve(dve, f0)
            N = E * NB
            for n in range(N + 1):
                if n < N:
                    dve.wait_ge(f0["h2"], n + 1)
                    if n >= 4:
                        dve.wait_ge(f0["h3"], n - 3)
                    dve.tensor_scalar(fh[1][n % 4], ps[:, 2 + n % 2, :], V("fb2", n // NB), 0.0, ALU.add, ALU.max).then_inc(f0["r2"], 1)
                if n >= 1:
                    q = n - 1
                    dve.wait_ge(f0["r3"], q + 1)
                    dve.wait_ge(f0["wbc"], q + 1)
                    dve.tensor_tensor_reduce(fh[2][q % 4], fh[2][q % 4], ps[:, 6 + q % 2, :], 1.0, 0.0, ALU.mult, ALU.add,
                                             vacc[:, q:q + 1]).then_inc(f0["pooled"], 1)
            dve.wait_ge(f0["pooled"], N)
            dve.tensor_reduce(vsum[:, :], vacc[:, :].rearrange("p (e k) -> p e k", k=NB), AX.X, ALU.add).then_inc(f0["dve"], 1)

        G = slot(13)

        def gate_act(act, f):
            for k in range(NB):
                act.wait_ge(f["pe"], f["mix"] + k + 1)
                act.activation(blk(G, k), ps[:, 4 + k, :], ACT.Silu).then_inc(f["act"], 1)

        def gate_dve(dve, own, f, s_ready, s_at):
            for k in range(NB):
                dve.wait_ge(f["act"], f["g"] + k + 1)
                dve.wait_ge(s_ready, s_at + k + 1)
                own(dve.tensor_tensor(blk(S, k), blk(S, k), blk(G, k), ALU.mult))
                dve.tensor_tensor(blk(X, k), blk(X, k), blk(S, k), ALU.add).then_inc(f["dve"], 1)

        SC1 = float(P) ** -0.5
        tiles = lambda n: slot(n).rearrange("p (i e) -> p i e", e=P)
        QW, PW = tiles(3), tiles(4)
        tile = lambda t, i: t[:, i * P:(i + 1) * P]
        four = lambda k: ps[:, k, :].rearrange("p (i e) -> p i e", e=P)
        xw = [blk(slot(5), u) for u in range(2)]
        sil = [[blk(slot(6), 2 * u + m) for m in range(2)] for u in range(2)]
        hid = [[blk(slot(7), 2 * u + m) for m in range(2)] for u in range(2)]

        def l1_pe(pe):
            norm_pe(pe, 3, X, f0["dve"], f0["x_out"])
            for k in range(NB):
                pe.wait_ge(norm["out"], NB * 3 + k + 1)
                for i in range(4):
                    mm = pe.matmul(four(4 + k)[:, i, :], tile(XN, 4 * k + i), W["wq"], start=True, stop=True)
                mm.then_inc(m1["pe"], 1)
            for i in range(NT):
                mm = pe.matmul(ps[:, 2, i * E:(i + 1) * E], tile(XN, i), W["router"], start=True, stop=True)
            mm.then_inc(m1["pe"], 1)
            for b in range(BATCH):
                pe.wait_ge(m1["dve"], m1["q_weighted"] + (b + 1) * NB // BATCH)
                for i in range(TB):
                    mm = pe.matmul(ps[:, b, 0:P], ones_1[:, :], QW[:, b * TB + i, :], start=(i == 0), stop=(i == TB - 1))
                mm.then_inc(m1["pe"], 1)
            for k in range(NB):
                b = k // (NB // BATCH)
                pe.wait_ge(m1["dve"], m1["wk_scaled"] + b + 1)
                for i in range(4):
                    mm = pe.matmul(four(4 + k)[:, i, :], tile(XN, 4 * k + i), wks[:, b, :], start=True, stop=True)
                mm.then_inc(m1["pe"], 1)
            for b in range(BATCH):
                pe.wait_ge(m1["dve"], m1["p_weighted"] + (b + 1) * NB // BATCH)
                for i in range(TB):
                    mm = pe.matmul(ps[:, b, 0:1], PW[:, b * TB + i, :], ones_1[:, 0:1], start=(i == 0), stop=(i == TB - 1))
                mm.then_inc(m1["pe"], 1)
            for b in range(BATCH):
                pe.wait_ge(m1["dve"], m1["wv_scaled"] + b + 1)
                pe.matmul(ps[:, 2 + b, 0:P], wvs[:, b, :], W["wr"], start=True, stop=True).then_inc(m1["pe"], 1)
            for k in range(NB):
                pe.wait_ge(m1["dve"], m1["comb_out"] + k // (NB // BATCH) + 1)
                pe.matmul(ps[:, 4 + k, :], wcomb[:, k // (NB // BATCH), :], blk(XN, k), start=True, stop=True).then_inc(m1["pe"], 1)
            pe.wait_ge(m1["act"], m1["s_out"] + NB)
            picked_pe(pe, f1)
            pe.wait_ge(f1["rt_out"], 2)
            pe.wait_ge(load["experts"], 16 * len(EXPERTS))
            N = E * NB
            for n in range(-1, N + 1):
                if n + 1 < N:
                    k, e = divmod(n + 1, E)
                    if n >= 0:
                        pe.wait_ge(f1["xw"], n + 1)
                    pe.matmul(ps[:, 0, :], selr[:, e, :], blk(rtb, k), start=True, stop=True).then_inc(f1["wbc"], 1)
                    for m in range(2):
                        if n >= 0:
                            pe.wait_ge(f1["silu"], 2 * n + m + 1)
                        c = e * 2 * I1 + m * P
                        pe.matmul(ps[:, 1 + m, :], W["w13"][:, c:c + P], blk(XN, k), start=True, stop=True).then_inc(f1["gate"], 1)
                if 0 <= n < N:
                    k, e = divmod(n, E)
                    pe.wait_ge(f1["xw"], n + 1)
                    for m in range(2):
                        if n >= 1:
                            pe.wait_ge(f1["h"], 2 * (n - 1) + m + 1)
                        c = e * 2 * I1 + I1 + m * P
                        pe.matmul(ps[:, 3 + m, :], W["w13"][:, c:c + P], xw[n % 2], start=True, stop=True).then_inc(f1["up"], 1)
                if n >= 1:
                    q = n - 1
                    k, e = divmod(q, E)
                    if e == 0 and k >= 2:
                        pe.wait_ge(f1["act"], f1["g"] + k - 1)
                    for m in range(2):
                        pe.wait_ge(f1["h"], 2 * q + m + 1)
                        mm = pe.matmul(ps[:, 5 + k % 2, :], W["w2e"][:, (2 * e + m) * P:(2 * e + m + 1) * P], hid[q % 2][m],
                                       start=(e == 0 and m == 0), stop=(e == E - 1 and m == 1))
                    mm.then_inc(f1["y"], 1)

        def l1_act(act, own):
            norm_act(act, 3, XN)
            for k in range(NB):
                act.wait_ge(m1["dve"], m1["q_sub"] + k + 1)
                act.activation(QW[:, 4 * k:4 * k + 4, :], QW[:, 4 * k:4 * k + 4, :], ACT.Exp, scale=SC1).then_inc(m1["act"], 1)
            act.wait_ge(m1["dve"], m1["sub"] + 1)
            act.activation(rw[:, 0], rw[:, 0], ACT.Exp).then_inc(m1["act"], 1)
            for k in range(NB):
                act.wait_ge(m1["dve"], m1["p_sub"] + k + 1)
                act.activation(PW[:, 4 * k:4 * k + 4, :], PW[:, 4 * k:4 * k + 4, :], ACT.Exp, scale=SC1).then_inc(m1["act"], 1)
            for k in range(NB):
                act.wait_ge(m1["pe"], m1["s"] + k + 1)
                act.activation(blk(S, k), ps[:, 4 + k, :], ACT.Copy).then_inc(m1["act"], 1)
            picked_out_act(act, f1)
            N = E * NB
            for n in range(N):
                for m in range(2):
                    act.wait_ge(f1["gate"], 2 * n + m + 1)
                    if n >= 2:
                        act.wait_ge(f1["h"], 2 * (n - 2) + m + 1)
                    act.activation(sil[n % 2][m], ps[:, 1 + m, :], ACT.Silu).then_inc(f1["silu"], 1)
                if n % E == 2 and n > E:
                    k = n // E - 1
                    act.wait_ge(f1["y"], E * (k + 1))
                    act.activation(blk(G, k), ps[:, 5 + k % 2, :], ACT.Silu).then_inc(f1["act"], 1)
            act.wait_ge(f1["y"], N)
            act.activation(blk(G, NB - 1), ps[:, 5 + (NB - 1) % 2, :], ACT.Silu).then_inc(f1["act"], 1)

        def soft_rows(dve, own, buf, row, mm, exps):
            bc = lambda v: v.unsqueeze(2).to_broadcast([P, 4, P])
            for k in range(NB):
                q = buf[:, 4 * k:4 * k + 4, :]
                dve.wait_ge(m1["pe"], mm + k + 1)
                own(dve.tensor_reduce(stat[:, row, 4 * k:4 * k + 4], four(4 + k), AX.X, ALU.max))
                dve.tensor_tensor(q, four(4 + k), bc(stat[:, row, 4 * k:4 * k + 4]), ALU.subtract).then_inc(m1["dve"], 1)
            for k in range(NB):
                q = buf[:, 4 * k:4 * k + 4, :]
                dve.wait_ge(m1["act"], exps + k + 1)
                own(dve.tensor_reduce(stat[:, row + 1, 4 * k:4 * k + 4], q, AX.X, ALU.add))
                own(dve.reciprocal(stat[:, row + 1, 4 * k:4 * k + 4], stat[:, row + 1, 4 * k:4 * k + 4]))
                own(dve.tensor_tensor(q, q, four(4 + k), ALU.mult))
                dve.tensor_tensor(q, q, bc(stat[:, row + 1, 4 * k:4 * k + 4]), ALU.mult).then_inc(m1["dve"], 1)

        def l1_dve(dve, own):
            bc = lambda v: v.unsqueeze(2).to_broadcast([P, NT, E])
            norm_dve(dve, own, 3, X, XN)
            soft_rows(dve, own, QW, 0, m1["q"], m1["q_exp"])
            dve.wait_ge(m1["pe"], m1["logit"] + 1)
            lgt = ps[:, 2, 0:NT * E].rearrange("p (i e) -> p i e", e=E)
            own(dve.tensor_reduce(rm[:, 0, :], lgt, AX.X, ALU.max))
            dve.tensor_tensor(rw[:, 0], lgt, bc(rm[:, 0, :]), ALU.subtract).then_inc(m1["dve"], 1)
            for b in range(BATCH):
                dve.wait_ge(m1["pe"], m1["gq"] + b + 1)
                dve.tensor_tensor(wks[:, b, :], W["wk"], ps[:, b, 0:P], ALU.mult).then_inc(m1["dve"], 1)
            soft_rows(dve, own, PW, 2, m1["p"], m1["p_exp"])
            for b in range(BATCH):
                dve.wait_ge(m1["pe"], m1["gk"] + b + 1)
                dve.tensor_scalar(wvs[:, b, :], W["wvT"], ps[:, b, 0:1], None, ALU.mult).then_inc(m1["dve"], 1)
            for b in range(BATCH):
                dve.wait_ge(m1["pe"], m1["comb"] + b + 1)
                dve.tensor_tensor(wcomb[:, b, :], W["wq"], ps[:, 2 + b, 0:P], ALU.add).then_inc(m1["dve"], 1)
            dve.wait_ge(m1["act"], m1["exps"] + 1)
            own(dve.tensor_reduce(rm[:, 2, :], rw[:, 0], AX.X, ALU.add))
            own(dve.reciprocal(rm[:, 2, :], rm[:, 2, :]))
            own(dve.tensor_tensor(rw[:, 0], rw[:, 0], bc(rm[:, 2, :]), ALU.mult))
            share(dve, own, rw[:, 0], 1e-6).then_inc(f1["dve"], 1)
            picked_out_dve(dve, f1)
            N = E * NB
            for n in range(N + 1):
                if n < N:
                    dve.wait_ge(f1["wbc"], n + 1)
                    if n >= 2:
                        dve.wait_ge(f1["up"], 2 * (n - 1))
                    dve.tensor_tensor(xw[n % 2], blk(XN, n // E), ps[:, 0, :], ALU.mult).then_inc(f1["xw"], 1)
                if n >= 1:
                    q = n - 1
                    for m in range(2):
                        dve.wait_ge(f1["up"], 2 * q + m + 1)
                        dve.wait_ge(f1["silu"], 2 * q + m + 1)
                        if q >= 2:
                            dve.wait_ge(f1["y"], q - 1)
                        dve.tensor_tensor(hid[q % 2][m], sil[q % 2][m], ps[:, 3 + m, :], ALU.mult).then_inc(f1["h"], 1)
            gate_dve(dve, own, f1, m1["act"], m1["s_out"])

        def share(dve, own, score, floor):
            bc = lambda v: v.unsqueeze(2).to_broadcast([P, NT, E])
            top2(dve, own, score, rt[:, :, 0:E])
            own(dve.tensor_tensor(rw[:, 1], score, rt[:, :, 0:E], ALU.mult))
            own(dve.tensor_reduce(rm[:, 2, :], rw[:, 1], AX.X, ALU.add))
            if floor:
                own(dve.tensor_scalar(rm[:, 2, :], rm[:, 2, :], floor, None, ALU.add))
            own(dve.reciprocal(rm[:, 2, :], rm[:, 2, :]))
            own(dve.tensor_tensor(rw[:, 1], rw[:, 1], bc(rm[:, 2, :]), ALU.mult))
            return split3(dve, own, rw[:, 1])

        BCH = [slot(3), slot(4)]
        BT, GT = tiles(5), tiles(6)
        nparts = slot(7)[0:96, 0:T // 2].bitcast(BF16)
        acum = slot(7)[:, SEQ:SEQ + NT * H2]
        DT, ADT, DEC, CDEC = (slot(8)[:, k * NT * H2:(k + 1) * NT * H2].rearrange("p (i h) -> p i h", h=H2) for k in range(4))
        cv = slots(9, 2).rearrange("p (j t) -> p j t", t=SEQ)
        flat = lambda o, n: work[:, 9 * T + o:9 * T + o + n]
        HP = flat(0, 1028)
        HC = [flat(1028 + SEQ * u, SEQ) for u in range(2)]
        SG = [flat(1028 + SEQ * (2 + u), SEQ) for u in range(2)]
        HDT, HDD = flat(1028 + 4 * SEQ, SEQ), flat(1028 + 5 * SEQ, SEQ)
        LM = flat(1028 + 6 * SEQ, 2 * SEQ)
        Y = [slot(2)[:, SEQ * u:SEQ * (u + 1)] for u in range(2)]
        ST = slot(7)[:, SEQ:]
        first_sum = [slot(8)[:, NT * H2:2 * NT * H2], flat(1028 + 8 * SEQ, BL)]
        K3 = DC - 1
        two = lambda k: ps[:, k:k + 2, :]
        wide = lambda t: t.rearrange("p (k t) -> p k t", t=BL)
        flat2 = lambda k: two(k).rearrange("p k t -> p (k t)")
        heads = lambda t: t.rearrange("p (c h q) -> p c h q", h=2, q=P2)
        FRONT, MID, BACK, ACC = 0, 2, 4, 6
        LAST = CT - 1

        par = lambda u, name, k=0: w_t[:, u, TCOL[name] + k:TCOL[name] + k + 1]

        def steps(eng, step):
            for b in range(BATCH):
                n0 = CT * b
                step(n0, b, 0, 0, n0 // 2, 1)
                with eng.Fori(0, (CT - 2) // 2) as i:
                    for v in range(2):
                        step(i * 2 + (n0 + 1 + v), b, i * 2 + (1 + v), (1 + v) % 2, i + (n0 // 2 + 1), i * 2 + (2 + v))
                step(n0 + LAST, b, LAST, LAST % 2, n0 // 2 + CT // 2, None)

        def l2_sync(sp):
            def load_tile(t, u):
                sp.dma_start(w_t[:, u, :], a["tile_w"][:, bass.ds(t * TW, TW)]).then_inc((m2["w_in0"], m2["w_in1"])[u], 16)

            def used(n):
                sp.wait_ge(m2["hc"], n + 1)
                sp.wait_ge(m2["wo"], n + 1)

            load_tile(0, 0)
            load_tile(1, 1)
            for b in range(BATCH):
                with sp.Fori(0, CT // 2 - 1) as i:
                    for u in range(2):
                        used(i * 2 + (CT * b + u))
                        load_tile(i * 2 + (2 + u), u)
                if b < BATCH - 1:
                    for u in range(2):
                        used(CT * b + CT - 2 + u)
                        load_tile(u, u)

        def l2_pe(pe):
            norm_pe(pe, 4, X, f1["dve"], f1["x_out"])
            pe.wait_ge(norm["out"], NB * 5)
            for i in range(NT):
                mm = pe.matmul(ps[:, 0, i * H2:(i + 1) * H2], tile(XN, i), W["w_dt"], start=True, stop=True)
            mm.then_inc(m2["pe"], 1)
            pe.wait_ge(m2["dve"], m2["adt"] + 1)
            adt = slot(8)[:, NT * H2:2 * NT * H2]
            pe.matmul(ps[:, 1, :], upper[:, :], adt, start=True, stop=True).then_inc(m2["pe"], 1)
            pe.matmul(ps[:, 2, :], ones_1[:, :], adt, start=True, stop=True).then_inc(m2["pe"], 1)
            for i in range(NT):
                mm = pe.matmul(ps[0:H2, 4 + i // 4, (i % 4) * P:(i % 4 + 1) * P], ADT[:, i, :], upper[:, :], start=True, stop=True)
            mm.then_inc(m2["pe"], 1)
            pe.wait_ge(load["late"], 16 * len(LATE))
            pe.wait_ge(m2["act"], m2["cdec"] + 1)
            for k in range(NB):
                for m in range(2):
                    n = 2 * k + m
                    if n >= 4:
                        pe.wait_ge(m2["act"], m2["bc_pad"] + n - 3)
                    pe.matmul(ps[:, n % 4, :], W["w_bc"][:, m * P:(m + 1) * P], blk(XN, k), start=True, stop=True).then_inc(m2["pe"], 1)
            pe.wait_ge(m2["dve"], m2["parts"] + NB)
            pe.wait_ge(m2["act"], m2["bc"] + 2 * BATCH)
            for k in range(NB):
                for i in range(4):
                    mm = pe.transpose(four(4 + k)[:, i, :], tile(BCH[0], 4 * k + i), ident[:, :])
                mm.then_inc(m2["pe"], 1)
            for k in range(NB):
                for i in range(4):
                    c = 4 * k + i
                    mm = pe.matmul(four(k)[:, i, :], tile(BCH[0], c), tile(BCH[1], c), start=True, stop=True)
                mm.then_inc(m2["pe"], 1)
            pe.wait_ge(m2["act"], m2["bt_out"] + NB)
            pe.wait_ge(m2["dve"], m2["gt_out"] + NB)
            pe.sem_inc(m2["outp"], 1)

            def project_h(n, b, u, half):
                pe.wait_ge((m2["w_in0"], m2["w_in1"])[u], half * 16 + 16)
                for h in range(2):
                    mm = pe.matmul(ps[:, FRONT + h, :], w_t[:, u, TCOL["h"]:TCOL["h"] + P], blk(XN, 2 * b + h), start=True, stop=True)
                mm.then_inc(m2["h_mm"], 1)

            def project_gate(n, b, u):
                pe.wait_ge(m2["h_pad"], n + 1)
                for h in range(2):
                    mm = pe.matmul(ps[:, FRONT + h, :], w_t[:, u, TCOL["gate"]:TCOL["gate"] + P], blk(XN, 2 * b + h), start=True, stop=True)
                mm.then_inc(m2["g_mm"], 1)

            def arguments(n, b, t):
                for q in range(4):
                    if q >= 2:
                        pe.wait_ge(m2["L"], n * 4 + (q - 1))
                    bank = BACK + q % 2
                    pe.matmul(ps[:, bank, :], ident_b[:, :], mask_t[:, :, :], start=True, stop=False, skip_group_check=True)
                    for cc in range(2):
                        c = b * TB + 2 * q + cc
                        pe.matmul(ps[:, bank, cc * 2 * P:(cc + 1) * 2 * P], nparts[:, c * P:(c + 1) * P],
                                  sel[:, bass.ds(t * 2, 2), :], start=False, stop=False, skip_group_check=True)
                        for h in range(2):
                            mm = pe.matmul(ps[:, bank, (2 * cc + h) * P:(2 * cc + h + 1) * P], sel[:, bass.ds(t * 2 + h, 1), :].rearrange("k a p -> k (a p)"),
                                           parts[:, c * P:(c + 1) * P], start=False, stop=(cc == 1 and h == 1),
                                           skip_group_check=True)
                    mm.then_inc(m2["arg"], 1)

            def turn_h(n, u):
                pe.wait_ge(m2["hc"], n + 1)
                pe.wait_ge(m2["sg"], n + 1)
                for c in range(TB):
                    mm = pe.transpose(four(FRONT + c // 4)[:, c % 4, :], tile(HC[u], c), ident[:, :])
                mm.then_inc(m2["tr"], 1)

            def spread_sums(n, b, t):
                for h in range(2):
                    mm = pe.matmul(ps[:, MID + h, :], sel2[:, bass.ds(t * 2, 2), :].rearrange("k a p -> k (a p)"),
                                   parts[:, b * SEQ + h * BL:b * SEQ + (h + 1) * BL], start=True, stop=True)
                mm.then_inc(m2["sdo_mm"], 1)

            def step(n, b, t, u, half, t1):
                b1, u1 = (b, 1 - u) if t1 is not None else (b + 1, 0)
                t1 = 0 if t1 is None else t1
                more = b1 < BATCH
                if more:
                    pe.wait_ge(m2["hdt"], n + 1)
                    project_h(n + 1, b1, u1, half)
                pe.wait_ge(m2["sdo"], n + 1)
                pe.wait_ge(m2["hdd"], n + 1)
                for c in range(TB - 1):
                    mm = pe.matmul(four(MID + c // 4)[:, c % 4, :], BT[:, b * TB + c, :], HDD[:, c * P:(c + 1) * P], start=True, stop=True)
                mm.then_inc(m2["st"], 1)
                pe.wait_ge(m2["M"], n + 1)
                for c in range(TB):
                    for h in range(2):
                        mm = pe.matmul(four(BACK + c // 4)[h * P2:(h + 1) * P2, c % 4, :], HDT[:, c * P + h * P2:c * P + (h + 1) * P2],
                                       LM[:, (2 * c + h) * P:(2 * c + h + 1) * P], start=True, stop=True)
                mm.then_inc(m2["ydiag"], 1)
                pe.wait_ge(m2["rec"], n + 1)
                for c in range(1, TB):
                    mm = pe.matmul(four(MID + c // 4)[:, c % 4, :], ST[:, c * P:(c + 1) * P], tile(BCH[1], b * TB + c),
                                   start=True, stop=True)
                mm.then_inc(m2["yoff"], 1)
                if more:
                    project_gate(n + 1, b1, u1)
                    pe.wait_ge(m2["yd"], n + 1)
                    arguments(n + 1, b1, t1)
                    turn_h(n + 1, u1)
                    pe.wait_ge(m2["yoff_used"], n + 1)
                    spread_sums(n + 1, b1, t1)
                pe.wait_ge(m2["y"], n + 2)
                pe.wait_ge(m2["wo"], n + 1)
                first = isinstance(t, int) and t == 0
                if first and b > 0:
                    pe.wait_ge(m2["first_out"], 1)
                for h in range(2):
                    if first:
                        pe.matmul(ps[:, ACC + h, :], zero[:, :], blk(XN, h), start=True, stop=False, skip_group_check=True)
                    mm = pe.matmul(ps[:, ACC + h, :], wo_t[:, u, :], Y[u][:, h * BL:(h + 1) * BL], start=False, stop=False,
                                   skip_group_check=True)
                mm.then_inc(m2["outp"], 1)

            project_h(0, 0, 0, 0)
            project_gate(0, 0, 0)
            arguments(0, 0, 0)
            turn_h(0, 0)
            spread_sums(0, 0, 0)
            steps(pe, step)
            pe.wait_ge(m2["ss"], CT * BATCH + 1)
            for k in range(NB):
                pe.matmul(ps[:, k, :], ones_n[:, :], ssum[:, k // 2, (k % 2) * BL:(k % 2 + 1) * BL], start=True, stop=True).then_inc(m2["pe"], 1)

        def l2_act(act, own):
            norm_act(act, 4, XN)
            act.wait_ge(load["row"], 16)
            act.activation(dtr[:, 2 * H2:], dtr[:, 2 * H2:], ACT.Exp).then_inc(m2["act"], 1)
            act.wait_ge(m2["dve"], m2["dt_biased"] + 1)
            own(act.activation(ADT, DT, ACT.Abs))
            own(act.activation(ADT, ADT, ACT.Exp, scale=-1.0))
            act.activation(ADT, ADT, ACT.Ln, bias=1.0).then_inc(m2["act"], 1)
            act.wait_ge(m2["dve"], m2["dec_sub"] + 1)
            act.activation(DEC, DEC, ACT.Exp).then_inc(m2["act"], 1)
            act.activation(CDEC, ps[:, 2, :].rearrange("p (i h) -> p i h", h=H2), ACT.Exp).then_inc(m2["act"], 1)
            for k in range(NB):
                act.wait_ge(m2["dve"], m2["parts"] + k + 1)
                act.activation(blk(nparts, k), blk(parts, k), ACT.Copy, scale=-1.0).then_inc(m2["act"], 1)
            for k in range(NB):
                b, h = divmod(k, NB // BATCH)
                for m in range(2):
                    act.wait_ge(m2["pe"], m2["bc_mm"] + 2 * k + m + 1)
                    act.activation(pad[:, 2 * b + m, K3 + h * BL:K3 + (h + 1) * BL], ps[:, (2 * k + m) % 4, :], ACT.Identity,
                                   bias=V("bc_bias", m)).then_inc(m2["act"], 1)
            for j in range(2 * BATCH):
                act.wait_ge(m2["dve"], m2["bc_conv"] + j + 1)
                act.activation(BCH[j % 2][:, (j // 2) * SEQ:(j // 2 + 1) * SEQ], cv[:, j, :], ACT.Silu).then_inc(m2["act"], 1)
            for k in range(NB):
                act.wait_ge(m2["pe"], m2["bt"] + k + 1)
                act.activation(blk(slot(5), k), ps[:, 4 + k, :], ACT.Copy).then_inc(m2["act"], 1)
            act.sem_inc(m2["sqr"], 1)

            def pad_h(n, u):
                act.wait_ge(m2["h_mm"], n + 1)
                act.wait_ge(m2["conv"], n + 1)
                act.activation(wide(HP[:, K3:K3 + SEQ]), two(FRONT), ACT.Identity, bias=par(u, "h_bias")).then_inc(m2["h_pad"], 1)

            def begin(n, u):
                act.wait_ge(m2["g_mm"], n + 1)
                if not (isinstance(n, int) and n == 0):
                    act.wait_ge(m2["y"], n)
                act.activation(wide(SG[u]), two(FRONT), ACT.Silu, bias=par(u, "gate_bias")).then_inc(m2["sg"], 1)
                act.wait_ge(m2["conv"], n + 2)
                act.activation(HC[u], HC[u], ACT.Silu).then_inc(m2["hc"], 1)
                for q in range(4):
                    act.wait_ge(m2["arg"], n * 4 + (q + 1))
                    act.activation(LM[:, q * BL:(q + 1) * BL], ps[:, BACK + q % 2, :], ACT.Exp).then_inc(m2["L"], 1)
                act.wait_ge(m2["sdo_mm"], n + 1)
                if not (isinstance(n, int) and n == 0):
                    act.wait_ge(m2["outp"], n)
                    act.wait_ge(m2["sqr"], n)
                act.activation(wide(Y[u]), two(MID), ACT.Exp).then_inc(m2["sdo"], 1)

            def step(n, b, t, u, half, t1):
                b1, u1 = (b, 1 - u) if t1 is not None else (b + 1, 0)
                if b1 < BATCH:
                    pad_h(n + 1, u1)
                act.wait_ge(m2["ydiag"], n + 1)
                act.activation(wide(HDD), two(BACK), ACT.Copy).then_inc(m2["yd"], 1)
                if b1 < BATCH:
                    begin(n + 1, u1)
                act.wait_ge(m2["y"], n + 2)
                act.wait_ge(m2["ss"], n + 1)
                act.activation(rs[:, :, :], wide(Y[u]), ACT.Square).then_inc(m2["sqr"], 1)
                if b1 == 1 and t1 is None:
                    act.wait_ge(m2["outp"], n + 2)
                    for h in range(2):
                        ins = act.activation(first_sum[h], ps[:, ACC + h, :], ACT.Copy)
                    ins.then_inc(m2["first_out"], 1)

            pad_h(0, 0)
            begin(0, 0)
            steps(act, step)
            act.preload_act_table_set("natural_log_exp_and_others")
            for k in range(NB):
                act.wait_ge(m2["pe"], m2["rms"] + k + 1)
                own(act.activation(flat(k * BL, BL), ps[:, k, :], ACT.Ln, bias=eps_t[:, :]))
                act.activation(flat(k * BL, BL), flat(k * BL, BL), ACT.Exp, scale=-0.5).then_inc(m2["act"], 1)

        def l2_dve(dve, own):
            norm_dve(dve, own, 4, X, XN)
            own(dve.memset(pad[:, :, 0:K3], 0.0))
            dve.wait_ge(load["row"], 16)
            dve.tensor_tensor(dtr[:, 0:H2], dtr[:, 0:H2], dtr[:, H2:2 * H2], ALU.add).then_inc(m2["dve"], 1)
            dve.wait_ge(m2["dve"], m2["row"] + 1)
            dve.wait_ge(m2["pe"], m2["dt_mm"] + 1)
            bc = lambda v: v.unsqueeze(1).to_broadcast([P, NT, H2])
            bank = lambda k: ps[:, k, :].rearrange("p (i h) -> p i h", h=H2)
            dve.tensor_tensor(DT, bank(0), bc(dtr[:, 0:H2]), ALU.add).then_inc(m2["dve"], 1)
            dve.wait_ge(m2["act"], m2["dt_soft"] + 1)
            dve.scalar_tensor_tensor(DT, DT, 0.0, ADT, ALU.max, ALU.add).then_inc(m2["dve"], 1)
            dve.wait_ge(m2["act"], m2["arow"] + 1)
            own(dve.tensor_scalar(dtr[:, 2 * H2:], dtr[:, 2 * H2:], -1.0, None, ALU.mult))
            dve.wait_ge(m2["dve"], m2["dt"] + 1)
            dve.tensor_tensor(ADT, DT, bc(dtr[:, 2 * H2:]), ALU.mult).then_inc(m2["dve"], 1)
            dve.wait_ge(m2["pe"], m2["tot"] + 1)
            dve.tensor_copy(acum, ps[:, 1, :]).then_inc(m2["dve"], 1)
            dve.wait_ge(m2["dve"], m2["acum"] + 1)
            dve.tensor_tensor(DEC, bank(2), acum.rearrange("p (i h) -> p i h", h=H2), ALU.subtract).then_inc(m2["dve"], 1)
            dve.wait_ge(m2["pe"], m2["cumT"] + 1)
            for k in range(NB):
                src = ps[0:H2, 4 + k, :]
                r, tb = rs[0:H2, k % 2, :], part_tmp[0:H2, :]
                own(dve.tensor_copy(blk(parts[0:32, :], k), src))
                own(dve.tensor_tensor(r, src, blk(parts[0:32, :], k), ALU.subtract))
                own(dve.tensor_copy(tb, r))
                own(dve.tensor_copy(blk(parts[32:64, :], k), tb))
                own(dve.tensor_tensor(r, r, tb, ALU.subtract))
                dve.tensor_copy(blk(parts[64:96, :], k), r).then_inc(m2["dve"], 1)
            for b in range(BATCH):
                dve.wait_ge(m2["act"], m2["bc_pad"] + 4 * (b + 1))
                for m in range(2):
                    j = 2 * b + m
                    col = lambda i: V("bc_conv", m * DC + i)
                    own(dve.tensor_scalar(cv[:, j, :], pad[:, j, K3:K3 + SEQ], col(K3), None, ALU.mult))
                    for i in range(K3):
                        c = dve.scalar_tensor_tensor(cv[:, j, :], pad[:, j, i:i + SEQ], col(i), cv[:, j, :], ALU.mult, ALU.add)
                        if i < K3 - 1:
                            own(c)
                    c.then_inc(m2["dve"], 1)
            for k in range(NB):
                dve.wait_ge(m2["pe"], m2["gt"] + k + 1)
                dve.tensor_copy(blk(slot(6), k), ps[:, k, :]).then_inc(m2["dve"], 1)
            own(dve.memset(HP[:, 0:K3], 0.0))
            bc4 = lambda v: v.unsqueeze(3).to_broadcast([P, TB, 2, P2])
            lm = LM.rearrange("p (c h l) -> p c h l", h=2, l=P)
            dve.sem_inc(m2["conv"], 1)
            dve.sem_inc(m2["y"], 1)

            def convolve(n, u):
                dve.wait_ge(m2["h_pad"], n + 1)
                own(dve.tensor_scalar(HC[u], HP[:, K3:K3 + SEQ], par(u, "taps", K3), None, ALU.mult))
                for tap in range(K3):
                    c = dve.scalar_tensor_tensor(HC[u], HP[:, tap:tap + SEQ], par(u, "taps", tap), HC[u], ALU.mult, ALU.add)
                    if tap < K3 - 1:
                        own(c)
                c.then_inc(m2["conv"], 1)

            def weigh(n, b, t):
                dve.wait_ge(m2["tr"], n + 1)
                dve.tensor_tensor(heads(HDT), two(FRONT).rearrange("p k (c h q) -> p (k c) h q", h=2, q=P2),
                                  bc4(DT[:, b * TB:(b + 1) * TB, bass.ds(t * 2, 2)]), ALU.mult).then_inc(m2["hdt"], 1)
                dve.wait_ge(m2["hdt"], n + 1)
                dve.tensor_tensor(heads(HDD), heads(HDT), bc4(DEC[:, b * TB:(b + 1) * TB, bass.ds(t * 2, 2)]),
                                  ALU.mult).then_inc(m2["hdd"], 1)
                dve.wait_ge(m2["L"], n * 4 + 4)
                dve.tensor_tensor(lm, lm, GT[:, b * TB:(b + 1) * TB, :].unsqueeze(2).to_broadcast([P, TB, 2, P]),
                                  ALU.mult).then_inc(m2["M"], 1)

            def step(n, b, t, u, half, t1):
                b1, u1 = (b, 1 - u) if t1 is not None else (b + 1, 0)
                t1 = 0 if t1 is None else t1
                dve.wait_ge(m2["st"], n + 1)
                if not (isinstance(n, int) and n == 0):
                    dve.wait_ge(m2["yoff"], n)
                own(dve.tensor_copy(ST[:, P:2 * P], four(MID)[:, 0, :]))
                for c in range(2, TB):
                    for h in range(2):
                        o = h * P2
                        if c > 2:
                            own.due(1)
                        s = dve.scalar_tensor_tensor(ST[:, c * P + o:c * P + o + P2], ST[:, (c - 1) * P + o:(c - 1) * P + o + P2],
                                                     CDEC[:, b * TB + c - 1, bass.ds(t * 2 + h, 1)],
                                                     four(MID + (c - 1) // 4)[:, (c - 1) % 4, o:o + P2], ALU.mult, ALU.add)
                        if c < TB - 1 or h == 0:
                            own.later(s)
                s.then_inc(m2["rec"], 1)
                if b1 < BATCH:
                    convolve(n + 1, u1)
                dve.wait_ge(m2["yd"], n + 1)
                own(dve.scalar_tensor_tensor(HDD, HC[u], vec[:, bass.ds(t + VCOL["d2"], 1)], HDD, ALU.mult, ALU.add))
                dve.wait_ge(m2["yoff"], n + 1)
                dve.wait_ge(m2["sdo"], n + 1)
                dve.tensor_tensor(Y[u][:, P:], Y[u][:, P:], flat2(MID)[:, P:], ALU.mult).then_inc(m2["yoff_used"], 1)
                dve.wait_ge(m2["yoff_used"], n + 1)
                own(dve.tensor_tensor(HDD[:, P:], HDD[:, P:], Y[u][:, P:], ALU.add))
                dve.tensor_tensor(Y[u], HDD, SG[u], ALU.mult).then_inc(m2["y"], 1)
                if b1 < BATCH:
                    weigh(n + 1, b1, t1)

            convolve(0, 0)
            weigh(0, 0, 0)
            for b in range(BATCH):
                per = K3 + 2 + 2 * (TB - 2)
                n0 = CT * b
                step(n0, b, 0, 0, None, 1)
                with dve.Fori(0, (CT - 2) // 2) as i:
                    own.rounds(i, 2 * per)
                    for v in range(2):
                        step(i * 2 + (n0 + 1 + v), b, i * 2 + (1 + v), (1 + v) % 2, None, i * 2 + (2 + v))
                    own.end((CT - 2) // 2)
                step(n0 + LAST, b, LAST, LAST % 2, None, None)
            for k in range(NB):
                b, h = divmod(k, NB // BATCH)
                dve.wait_ge(m2["act"], m2["rstd"] + k + 1)
                dve.wait_ge(m2["outp"], CT * BATCH + 1)
                total = first_sum[h] if b == 0 else ps[:, ACC + h, :]
                own(dve.tensor_tensor(blk(S, k), total, flat(k * BL, BL), ALU.mult))
                dve.tensor_scalar(blk(S, k), blk(S, k), V("b_out"), None, ALU.add).then_inc(m2["dve"], 1)

        def l2_pool(pool, own):
            pool.wait_ge(norm["out"], NB * 5)
            own(pool.memset(ssum[:, :, :], 0.0))
            pool.sem_inc(m2["ss"], 1)

            def weights_out(n, u, half):
                pool.wait_ge((m2["w_in0"], m2["w_in1"])[u], half * 16 + 16)
                if not (isinstance(n, int) and n == 0):
                    pool.wait_ge(m2["outp"], n)
                pool.tensor_tensor(wo_t[:, u, :], w_t[:, u, TCOL["out"]:TCOL["out"] + P],
                                   par(u, "norm_w").to_broadcast([P, P]), ALU.mult).then_inc(m2["wo"], 1)

            def step(n, b, t, u, half, t1):
                if t1 is not None or b + 1 < BATCH:
                    weights_out(n + 1, 0 if t1 is None else 1 - u, half)
                pool.wait_ge(m2["sqr"], n + 2)
                if not (isinstance(n, int) and n == 0):
                    pool.wait_ge(m2["ss"], n + 1)
                pool.tensor_tensor(ssum[:, b, :], ssum[:, b, :], rs[:, :, :].rearrange("p k t -> p (k t)"), ALU.add).then_inc(m2["ss"], 1)

            weights_out(0, 0, 0)
            steps(pool, step)

        pairs = E * HE // P
        gb = [blk(slot(4), u) for u in range(2)]
        hw = [blk(slot(5), u) for u in range(2)]

        def f2_pe(pe):
            pe.wait_ge(m2["dve"], m2["s_out"] + NB)
            for i in range(NT):
                mm = pe.matmul(ps[:, 0, i * E:(i + 1) * E], tile(XN, i), W["gate2"], start=True, stop=True)
            mm.then_inc(f2["pe"], 1)
            picked_pe(pe, f2)
            pe.wait_ge(f2["rt_out"], 2)
            per = pairs + 1
            for n in range(NB * per + 1):
                if n < NB * per:
                    k, q = divmod(n, per)
                    if n >= 2:
                        pe.wait_ge(f2["gelu"], n - 1)
                        pe.wait_ge(f2["hw"], n - 1)
                    if q < pairs:
                        pe.matmul(ps[:, 4 + n % 2, :], selr2[:, 2 * q:2 * q + 2, :].rearrange("k a p -> k (a p)"), blk(rtb, k),
                                  start=True, stop=True).then_inc(f2["wbc"], 1)
                        pe.matmul(ps[:, n % 2, :], W["ew1"][:, q * P:(q + 1) * P], blk(XN, k), start=True, stop=True).then_inc(f2["h"], 1)
                    else:
                        pe.matmul(ps[0:HE, n % 2, :], W["sw1"], blk(XN, k), start=True, stop=True).then_inc(f2["h"], 1)
                if n >= 1:
                    k, q = divmod(n - 1, per)
                    y = ps[:, 2 + k % 2, :]
                    if q == 0:
                        if k >= 2:
                            pe.wait_ge(f2["act"], f2["y_out"] + k - 1)
                        pe.matmul(y, W["eb2"], blk(rtf, k), start=True, stop=False)
                    pe.wait_ge(f2["hw"], n)
                    if q < pairs:
                        pe.matmul(y, W["ew2"][:, q * P:(q + 1) * P], hw[(n - 1) % 2], start=False, stop=False)
                    else:
                        pe.matmul(y, W["sw2"], hw[(n - 1) % 2][0:HE, :], start=False, stop=True).then_inc(f2["pe"], 1)

        def f2_act(act, own):
            act.wait_ge(f2["pe"], f2["logit"] + 1)
            act.activation(rw[:, 0], ps[:, 0, 0:NT * E].rearrange("p (i e) -> p i e", e=E), ACT.Sigmoid).then_inc(f2["act"], 1)
            picked_out_act(act, f2)
            per = pairs + 1
            for n in range(NB * per + 1):
                if n < NB * per:
                    k, q = divmod(n, per)
                    act.wait_ge(f2["h"], n + 1)
                    if n >= 2:
                        act.wait_ge(f2["hw"], n - 1)
                    p = P if q < pairs else HE
                    act.activation(gb[n % 2][0:p, :], ps[0:p, n % 2, :], ACT.Gelu,
                                   bias=V("eb1", q) if q < pairs else V("sb1", 0, HE)).then_inc(f2["gelu"], 1)
                if n >= per and n % per == 0:
                    act.wait_ge(f2["pe"], f2["y"] + n // per)
                    act.activation(blk(G, n // per - 1), ps[:, 2 + (n // per - 1) % 2, :], ACT.Identity,
                                   bias=V("sb2")).then_inc(f2["act"], 1)
            act.wait_ge(f2["act"], f2["y_out"] + NB)
            for k in range(NB):
                act.activation(blk(G, k), blk(G, k), ACT.Silu).then_inc(f2["act"], 1)

        def f2_dve(dve, own):
            dve.wait_ge(f2["act"], f2["sig"] + 1)
            own(dve.tensor_scalar(rw[:, 0], rw[:, 0], V("route_scale"), None, ALU.mult))
            share(dve, own, rw[:, 0], 0.0).then_inc(f2["dve"], 1)
            picked_out_dve(dve, f2)
            per = pairs + 1
            for n in range(NB * per):
                k, q = divmod(n, per)
                dve.wait_ge(f2["gelu"], n + 1)
                if q < pairs:
                    dve.wait_ge(f2["wbc"], k * pairs + q + 1)
                    dve.tensor_tensor(hw[n % 2], gb[n % 2], ps[:, 4 + n % 2, :], ALU.mult).then_inc(f2["hw"], 1)
                else:
                    dve.tensor_copy(hw[n % 2][0:HE, :], gb[n % 2][0:HE, :]).then_inc(f2["hw"], 1)
            gate_dve(dve, own, f2, m2["dve"], m2["s_out"])

        QK = [slot(3), slot(4)]
        VT = tiles(5)
        prob = [slots(6, 1)[:, 0:SEQ], slots(6, 1)[:, SEQ:]]
        probT = [slot(7)[:, 0:SEQ], slot(7)[:, SEQ:]]
        ROWS = BATCH * TB
        spans = [(r, r // TB, r % TB, r % TB + 1) for r in range(ROWS)]

        def l3_pe(pe):
            norm_pe(pe, 5, X, f2["dve"], f2["x_out"])
            for k in range(NB):
                pe.wait_ge(norm["out"], NB * 5 + k + 1)
                for m in range(2):
                    n = 2 * k + m
                    if n >= 4:
                        pe.wait_ge(m3["act"], m3["qk_out"] + n - 3)
                    pe.matmul(ps[:, 4 + n % 4, :], W["qkv"][:, m * P:(m + 1) * P], blk(XN, k), start=True, stop=True).then_inc(m3["pe"], 1)
            for k in range(NB):
                for i in range(4):
                    mm = pe.matmul(four(k)[:, i, :], tile(XN, 4 * k + i), W["qkv"][:, 2 * P:], start=True, stop=True)
                mm.then_inc(m3["pe"], 1)
            pe.wait_ge(m3["act"], m3["v_out"] + NB)

            def score(r, b, qi, w):
                if r >= 2:
                    pe.wait_ge(m3["e"], r - 1)
                for h in range((w * P + BL - 1) // BL):
                    c0, c1 = h * BL, min(w * P, (h + 1) * BL)
                    out = ps[:, 2 * (r % 2) + h, 0:c1 - c0]
                    last = c1 == w * P
                    mm = pe.matmul(out, tile(QK[0], r), QK[1][:, b * SEQ + c0:b * SEQ + c1], start=True, stop=not last,
                                   skip_group_check=True)
                    if last:
                        mm = pe.matmul(out[:, c1 - c0 - P:], ident_b[:, :], mask_q[:, :], start=False, stop=True, skip_group_check=True)
                mm.then_inc(m3["s"], 1)

            def values(r, b, qi, w):
                pe.wait_ge(m3["p"], r + 1)
                for h in range((w + 3) // 4):
                    if r >= 1:
                        pe.wait_ge(m3["pT_out"], halves_done[r])
                    for c in range(4 * h, min(w, 4 * h + 4)):
                        mm = pe.transpose(four(4 + h)[:, c % 4, :], prob[r % 2][:, c * P:(c + 1) * P], ident[:, :])
                    mm.then_inc(m3["pT"], 1)
                if r >= 2:
                    pe.wait_ge(m3["o_out"], r - 1)
                for c in range(w):
                    if c % 4 == 0:
                        pe.wait_ge(m3["pT_out"], halves_done[r] + c // 4 + 1)
                    mm = pe.matmul(ps[:, 6 + r % 2, 0:P], VT[:, b * TB + c, :], probT[r % 2][:, c * P:(c + 1) * P],
                                   start=(c == 0), stop=(c == w - 1))
                mm.then_inc(m3["o"], 1)

            for r in range(ROWS + 1):
                if r < ROWS:
                    score(*spans[r])
                if r >= 1:
                    values(*spans[r - 1])

        halves_done = [sum((w + 3) // 4 for _, _, _, w in spans[:r]) for r in range(ROWS + 1)]

        def l3_act(act, own):
            norm_act(act, 5, XN)
            for n in range(2 * NB):
                k, m = divmod(n, 2)
                act.wait_ge(m3["pe"], m3["qk"] + n + 1)
                act.activation(blk(QK[m], k), ps[:, 4 + n % 4, :], ACT.Identity, bias=V(("b_q", "b_k")[m])).then_inc(m3["act"], 1)
            for k in range(NB):
                act.wait_ge(m3["pe"], m3["v"] + k + 1)
                act.activation(blk(slot(5), k), ps[:, k, :], ACT.Copy).then_inc(m3["act"], 1)
            for r in range(ROWS + 1):
                if r < ROWS:
                    _, b, qi, w = spans[r]
                    act.wait_ge(m3["peak"], r + 1)
                    if r >= 2:
                        act.wait_ge(m3["pT"], halves_done[r - 1])
                    act.activation(prob[r % 2][:, 0:w * P],
                                   ps[:, 2 * (r % 2):2 * (r % 2) + 2, :].rearrange("p k t -> p (k t)")[:, 0:w * P], ACT.Exp,
                                   bias=stat[:, 1, r:r + 1], scale=SC1, accum_out=stat[:, 2, r:r + 1]).then_inc(m3["e"], 1)
                if r >= 1:
                    act.wait_ge(m3["o"], r)
                    act.activation(tile(S, r - 1), ps[:, 6 + (r - 1) % 2, 0:P], ACT.Identity, bias=V("b_v")).then_inc(m3["o_out"], 1)

        def l3_dve(dve, own):
            norm_dve(dve, own, 5, X, XN)

            def spread_out(r, b, qi, w):
                for h in range((w + 3) // 4):
                    dve.wait_ge(m3["pT"], halves_done[r] + h + 1)
                    n = min(4, w - 4 * h)
                    if r >= 2 and h == 0:
                        dve.wait_ge(m3["o"], r - 1)
                    dve.tensor_copy(probT[r % 2][:, h * BL:h * BL + n * P], ps[:, 4 + h, 0:n * P]).then_inc(m3["pT_out"], 1)

            for r in range(ROWS + 1):
                if r < ROWS:
                    _, b, qi, w = spans[r]
                    dve.wait_ge(m3["s"], r + 1)
                    own(dve.tensor_reduce(stat[:, 0, r:r + 1],
                                          ps[:, 2 * (r % 2):2 * (r % 2) + 2, :].rearrange("p k t -> p (k t)")[:, 0:w * P], AX.X, ALU.max))
                    dve.tensor_scalar(stat[:, 1, r:r + 1], stat[:, 0, r:r + 1], -SC1, None, ALU.mult).then_inc(m3["peak"], 1)
                if r >= 1:
                    spread_out(*spans[r - 1])
                if r < ROWS:
                    dve.wait_ge(m3["e"], r + 1)
                    own(dve.reciprocal(stat[:, 3, r:r + 1], stat[:, 2, r:r + 1]))
                    dve.tensor_scalar(prob[r % 2][:, 0:w * P], prob[r % 2][:, 0:w * P], stat[:, 3, r:r + 1], None, ALU.mult).then_inc(m3["p"], 1)

        mid = [[blk(slot(8 + u), m) for m in range(F3 // P)] for u in range(2)]

        def f3_pe(pe):
            M = F3 // P
            for k in range(NB + 1):
                if k < NB:
                    for m in range(M):
                        n = M * k + m
                        if n >= 4:
                            pe.wait_ge(f3["relu"], n - 3)
                        pe.matmul(ps[:, n % 4, :], W["g1"][:, m * P:(m + 1) * P], blk(XN, k), start=True, stop=True).then_inc(f3["h"], 1)
                if k == 1:
                    pe.wait_ge(m3["o_out"], ROWS)
                    pe.wait_ge(m3["pT_out"], halves_done[ROWS])
                if k >= 1:
                    for m in range(M):
                        pe.wait_ge(f3["relu"], M * (k - 1) + m + 1)
                        mm = pe.matmul(ps[:, 4 + k - 1, :], W["g2"][:, m * P:(m + 1) * P], mid[(k - 1) % 2][m],
                                       start=(m == 0), stop=(m == M - 1))
                    mm.then_inc(f3["pe"], 1)

        def f3_act(act, own):
            for k in range(NB):
                act.wait_ge(f3["pe"], f3["y"] + k + 1)
                act.activation(blk(G, k), ps[:, 4 + k, :], ACT.Silu, bias=V("c2")).then_inc(f3["act"], 1)

        def f3_dve(dve, own):
            M = F3 // P
            for n in range(M * NB):
                k, m = divmod(n, M)
                dve.wait_ge(f3["h"], n + 1)
                if k >= 2:
                    dve.wait_ge(f3["pe"], f3["y"] + k - 1)
                dve.tensor_scalar(mid[k % 2][m], ps[:, n % 4, :], V("c1", m), 0.0, ALU.add, ALU.max).then_inc(f3["relu"], 1)
            for k in range(NB):
                dve.wait_ge(m3["o_out"], ROWS)
                dve.wait_ge(f3["act"], f3["g"] + k + 1)
                own(dve.tensor_tensor(blk(S, k), blk(S, k), blk(G, k), ALU.mult))
                dve.tensor_tensor(blk(X, k), blk(X, k), blk(S, k), ALU.add).then_inc(f3["dve"], 1)

        @block.sync
        def _(sp):
            for k in range(NB):
                sp.dma_start(blk(X, k), a["x"][:, k * BL:(k + 1) * BL]).then_inc(load["x"], 16)
            sp.dma_start(vec[:, :], a["vec"]).then_inc(load["vec"], 16)
            sp.dma_start(dtr[:, :], a["dt_row"].to_broadcast([P, 3 * H2])).then_inc(load["row"], 16)
            for n, _, _ in FIRST:
                sp.dma_start(W[n], a[n]).then_inc(load["weights"], 16)
            for n, _, _ in POOLED:
                sp.dma_start(W[n], a[n]).then_inc(load["pooled"], 16)
            sp.wait_ge(f0["h3"], E * NB)
            for n, _, _ in LATE:
                sp.dma_start(W[n], a[n]).then_inc(load["late"], 16)
            sp.wait_ge(m0["ysum"], DS * BATCH * MI)
            sp.wait_ge(m0["state"], DS * BATCH * MI)
            for n, _, _ in EXPERTS:
                sp.dma_start(W[n], a[n]).then_inc(load["experts"], 16)
            if upto >= 3:
                l2_sync(sp)
            final = ends[upto - 1]
            for k in range(NB):
                sp.wait_ge(final["dve"], final["x_out"] + k + 1)
                sp.dma_start(out[:, k * BL:(k + 1) * BL], blk(X, k)).then_inc(done["stored"], 16)
            sp.wait_ge(done["stored"], 16 * NB)
        @block.gpsimd
        def _(pool):
            own = Chain(pool, pool_own)
            pool.memset(ones_d[:, :], 1.0 / P)
            pool.memset(ones_n[:, :], 1.0 / INTER)
            pool.memset(ones_1[:, :], 1.0)
            pool.memset(eps_t[:, :], EPS)
            for e in range(E):
                pool.memset(tie[:, :, e:e + 1], float(E - e))
            for t in (ident, ident_b, mask_t, mask_q, zero, sel, sel2, selr, selr2):
                pool.memset(t[:, :] if len(t.shape) == 2 else t[:, :, :], 0.0)
            own(pool.memset(upper[:, :], 1.0))
            for t in (ident, ident_b):
                pool.affine_select(t[:, :], t[:, :], [[-1, P]], ALU.not_equal, 1.0, base=0, channel_multiplier=1)
            pool.affine_select(upper[:, :], upper[:, :], [[1, P]], ALU.is_ge, 0.0, base=0, channel_multiplier=-1)
            pool.affine_select(mask_t[:, :, :], mask_t[:, :, :], [[0, 4], [1, P]], ALU.is_ge, -BIG, base=0, channel_multiplier=-1)
            pool.affine_select(mask_q[:, :], mask_q[:, :], [[-1, P]], ALU.is_ge, -BIG, base=0, channel_multiplier=1)
            for k in range(3):
                for t, w in ((sel, P), (sel2, P2)):
                    own(pool.affine_select(t[:, :, :], t[:, :, :], [[-1, H2], [0, w]], ALU.not_equal, 1.0,
                                           base=-H2 * k, channel_multiplier=1))
                for t, w in ((selr, P), (selr2, HE)):
                    ins = pool.affine_select(t[:, :, :], t[:, :, :], [[-1, E], [0, w]], ALU.not_equal, 1.0,
                                             base=-E * (k + 1), channel_multiplier=1)
                    if k == 2 and w == HE:
                        ins.then_inc(const["ready"], 1)
                    else:
                        own(ins)
            l0_pool(pool)
            if upto >= 3:
                l2_pool(pool, own)

        @block.tensor
        def _(pe):
            pe.wait_ge(const["ready"], 1)
            pe.wait_ge(load["x"], 16 * NB)
            pe.wait_ge(load["weights"], 16 * len(FIRST))
            pe.wait_ge(load["pooled"], 16 * len(POOLED))
            norm_pe(pe, 0, X)
            f0_pe(pe)
            l0_pe(pe)
            f0_mix_pe(pe)
            if upto >= 2:
                l1_pe(pe)
            if upto >= 3:
                l2_pe(pe)
                f2_pe(pe)
            if upto >= 4:
                l3_pe(pe)
                f3_pe(pe)

        @block.scalar
        def _(act):
            own = Chain(act, act_own)
            act.wait_ge(const["ready"], 1)
            act.wait_ge(load["x"], 16 * NB)
            act.wait_ge(load["vec"], 16)
            act.wait_ge(load["weights"], 16 * len(FIRST))
            norm_act(act, 0, XN)
            f0_act(act, own)
            l0_act(act, own)
            gate_act(act, f0)
            if upto >= 2:
                l1_act(act, own)
            if upto >= 3:
                l2_act(act, own)
                f2_act(act, own)
            if upto >= 4:
                l3_act(act, own)
                f3_act(act, own)

        @block.vector
        def _(dve):
            own = Chain(dve, dve_own)
            dve.wait_ge(load["x"], 16 * NB)
            dve.wait_ge(load["vec"], 16)
            dve.wait_ge(const["ready"], 1)
            norm_dve(dve, own, 0, X, XN)
            f0_dve(dve, own)
            l0_dve(dve, own)
            gate_dve(dve, own, f0, m0["dve"], m0["s_out"])
            if upto >= 2:
                l1_dve(dve, own)
            if upto >= 3:
                l2_dve(dve, own)
                f2_dve(dve, own)
            if upto >= 4:
                l3_dve(dve, own)
                f3_dve(dve, own)


def layout(inputs):
    import numpy as np

    f = {k: np.asarray(v) for k, v in inputs.items()}
    a0, f0, a1, f1 = ({k.split(p)[1]: v for k, v in f.items() if k.startswith(p)}
                      for p in ("L0_attn_", "L0_ffn_", "L1_attn_", "L1_ffn_"))
    a2, f2, a3, f3 = ({k.split(p)[1]: v for k, v in f.items() if k.startswith(p)}
                      for p in ("L2_attn_", "L2_ffn_", "L3_attn_", "L3_ffn_"))
    cols = lambda v: v.reshape(-1, P).T
    taps = lambda w: w.reshape(-1, P, w.shape[-1]).transpose(1, 0, 2).reshape(P, -1)
    rows = lambda w: w.reshape(-1, P, w.shape[-1]).transpose(1, 0, 2).reshape(P, -1)

    def low(v):
        z = np.zeros((P, 1), np.float32)
        z[:v.size, 0] = v.reshape(-1)
        return z

    vectors = dict(
        ln1_g=cols(a0["ln1_g"]), ln1_b=cols(a0["ln1_b"]), ln2_g=cols(a0["ln2_g"]), ln2_b=cols(a0["ln2_b"]),
        b1=cols(a0["b1"]), b2=cols(a0["b2"]), conv_w=taps(a0["conv_w"][:, 0, :]), conv_b=cols(a0["conv_b"]),
        dt_b=cols(a0["dt_proj_b"]), a_log=taps(a0["A_log"]), d=cols(a0["D_param"]), gate_b=low(f0["gate_b"]),
        fb1=f0["b1"].T, fb2=f0["b2"].T, fb3=f0["b3"].T,
        bc_bias=cols(a2["b_in"][2 * INTER:2 * INTER + 2 * N2]), bc_conv=taps(a2["conv_w"][INTER:]), b_out=cols(a2["b_out"]),
        d2=cols(np.repeat(a2["D"], P2)),
        eb1=cols(f2["b1"].reshape(-1)), sb1=low(f2["bs1"]), sb2=cols(f2["bs2"]),
        route_scale=np.broadcast_to(f2["route_scale"].reshape(1, 1), (P, 1)),
        b_q=cols(a3["b"][:P]), b_k=cols(a3["b"][P:2 * P]), b_v=cols(a3["b"][2 * P:]),
        c1=cols(f3["b1"]), c2=cols(f3["b2"]))
    w_in = a2["W_in"].T
    by_tile = lambda w: w.reshape(P, CT, -1)
    tile_w = dict(
        gate=by_tile(w_in[:, :INTER]), h=by_tile(w_in[:, INTER:2 * INTER]), out=by_tile(rows(a2["W_out"].T)),
        gate_bias=by_tile(cols(a2["b_in"][:INTER])), h_bias=by_tile(cols(a2["b_in"][INTER:2 * INTER])),
        taps=by_tile(taps(a2["conv_w"][:INTER])), norm_w=by_tile(cols(a2["norm_w"])))
    per_expert = lambda w: w.transpose(1, 0, 2).reshape(w.shape[1], -1)
    out = dict(
        x=f["L0_attn_x"].reshape(T, P).T,
        vec=np.concatenate([vectors[n] for n, _ in VECTORS], axis=1),
        dt_row=np.stack([a2["b_in"][2 * INTER + 2 * N2:], a2["dt_bias"], a2["A_log"]]).reshape(1, -1),
        tile_w=np.concatenate([tile_w[n] for n, _ in TILE_W], axis=2).reshape(P, -1),
        w1=a0["W1"].T, w2=rows(a0["W2"].T), in_proj=a0["in_proj_w"].T, x_proj=rows(a0["x_proj_w"].T),
        dt_proj=a0["dt_proj_w"].T, out_proj=rows(a0["out_proj_w"].T), gate0=f0["gate_w"],
        f1=per_expert(f0["w1"]), f2=per_expert(f0["w2"]), f3=per_expert(f0["w3"]),
        wq=a1["Wq"], wk=a1["Wk"], wvT=a1["Wv"].T, wr=a1["Wr"], router=f1["router_w"].T,
        w13=per_expert(f1["w13"]), w2e=rows(f1["w2"].reshape(E * I1, P)),
        w_bc=w_in[:, 2 * INTER:2 * INTER + 2 * N2], w_dt=w_in[:, 2 * INTER + 2 * N2:],
        gate2=f2["gate_W"], ew1=per_expert(f2["W1"]), ew2=rows(f2["W2"].reshape(E * HE, P)),
        eb2=np.concatenate([np.zeros((E, P), np.float32)] + [f2["b2"]] * 3), sw1=f2["Ws1"], sw2=f2["Ws2"],
        qkv=a3["W"], g1=f3["W1"], g2=rows(f3["W2"]))
    return {k: np.ascontiguousarray(v) for k, v in out.items()}


def kernel(**inputs):
    import numpy as np
    import concourse.bacc as bacc
    from concourse.bass_utils import run_bass_kernel_spmd

    nc = bacc.Bacc("TRN2", target_bir_lowering=False, num_devices=1)
    arrays = {f"in_{k}": v for k, v in layout(inputs).items()}
    a = {k[3:]: nc.dram_tensor(k, v.shape, mybir.dt.from_np(v.dtype), kind="ExternalInput").ap() for k, v in arrays.items()}
    out = nc.dram_tensor("out_x", [P, T], F32, kind="ExternalOutput").ap()
    build(nc, a, out)
    r = run_bass_kernel_spmd(nc, [arrays], core_ids=[0])
    return np.ascontiguousarray(np.asarray(r.results[0]["out_x"]).T).reshape(BATCH, SEQ, P)
```

```python
from contextlib import ExitStack

import concourse.bass as bass
from concourse import mybir

ALU = mybir.AluOpType
ACT = mybir.ActivationFunctionType
AX = mybir.AxisListType
F32 = mybir.dt.float32
BF16 = mybir.dt.bfloat16
RMAX = bass.bass_isa.ReduceOp.max

P = 128
BATCH, SEQ = 2, 1024
T = BATCH * SEQ
BL = 512
NB = T // BL
NT = T // P
TB = SEQ // P
EPS = 1e-5
BIG = 1e30
E = 8

DI, DS, DR, DC = 256, 16, 64, 4
MI = DI // P
QB = 128.0
GROUPS = 4
GL = SEQ // GROUPS
I1 = 256
H2, P2, N2 = 32, 64, 128
INTER = H2 * P2
CT = INTER // P
HE = 64
F3 = 512

VECTORS = [
    ("ln1_g", 1), ("ln1_b", 1), ("ln2_g", 1), ("ln2_b", 1), ("b1", MI), ("b2", 1),
    ("conv_w", MI * DC), ("conv_b", MI), ("dt_b", MI), ("a_log", MI * DS), ("d", MI),
    ("gate_b", 1), ("fb1", E), ("fb2", E), ("fb3", E),
    ("bc_bias", 2), ("bc_conv", 2 * DC), ("b_out", 1), ("d2", CT),
    ("eb1", E * HE // P), ("sb1", 1), ("sb2", 1), ("route_scale", 1),
    ("b_q", 1), ("b_k", 1), ("b_v", 1), ("c1", F3 // P), ("c2", 1),
]
VCOL = {}
NV = 0
for _name, _n in VECTORS:
    VCOL[_name] = NV
    NV += _n

TILE_W = [("gate", P), ("h", P), ("out", P), ("gate_bias", 1), ("h_bias", 1), ("taps", DC), ("norm_w", 1)]
TW = sum(c for _, c in TILE_W)
TCOL = {n: sum(c for _, c in TILE_W[:k]) for k, (n, _) in enumerate(TILE_W)}

SOON = [("gate0", P, E), ("w1", P, DI), ("w2", P, MI * P)]
FIRST = SOON + [
    ("in_proj", P, 2 * DI), ("x_proj", P, MI * (DR + 2 * DS)),
    ("dt_proj", DR, DI), ("out_proj", P, MI * P),
    ("wq", P, P), ("wk", P, P), ("wvT", P, P), ("wr", P, P), ("router", P, E),
    ("w_dt", P, H2), ("gate2", P, E), ("eb2", 4 * E, P), ("sw1", P, HE), ("sw2", HE, P),
]
POOLED = [("f1", P, E * P), ("f2", P, E * P), ("f3", P, E * P)]
LATE = [
    ("w_bc", P, 2 * N2), ("ew1", P, E * HE), ("ew2", P, E * HE),
    ("qkv", P, 3 * P), ("g1", P, F3), ("g2", P, F3),
]
EXPERTS = [("w13", P, E * 2 * I1), ("w2e", P, E * I1)]


class Chain:

    def __init__(self, eng, sem):
        self.eng, self.sem, self.n, self.at = eng, sem, 0, None

    def __call__(self, ins):
        ins.then_inc(self.sem, 1)
        self.n += 1
        self.eng.wait_ge(self.sem, self.n if self.at is None else self.at + self.n)

    def later(self, ins):
        ins.then_inc(self.sem, 1)
        self.n += 1

    def due(self, but):
        self.eng.wait_ge(self.sem, (self.n if self.at is None else self.at + self.n) - but)

    def rounds(self, i, per):
        self.at, self.start, self.per = i * per, self.n, per

    def end(self, count):
        assert self.n - self.start == self.per, (self.n - self.start, self.per)
        self.n = self.start + self.per * count
        self.at = None


def build(nc, a, out, upto=4):
    ctx = ExitStack()
    with ctx:
        def sb(name, shape, dt=F32):
            return ctx.enter_context(nc.sbuf_tensor(name, shape, dt))

        def sems(prefix, names):
            return {n: ctx.enter_context(nc.semaphore(f"{prefix}_{n}")) for n in names.split()}

        def stages(prefix, each, **engines):
            ns = sems(prefix, each)
            for eng, names in engines.items():
                ns[eng] = ctx.enter_context(nc.semaphore(f"{prefix}_{eng}"))
                at = 0
                for item in names.split():
                    name, count = item.split(":")
                    ns[name] = at
                    at += int(count)
            return ns

        ps = ctx.enter_context(nc.psum_tensor("ps", [P, 8, BL], F32))
        W = {n: sb("w_" + n, [p, c])[:, :] for n, p, c in FIRST}
        shared = sb("shared", [P, max(sum(c for _, _, c in g) for g in (POOLED, LATE))])
        vec = sb("vec", [P, NV])
        work = sb("work", [P, 14 * T])
        ones_d = sb("ones_d", [P, P])
        ones_n = sb("ones_n", [P, P])
        ones_1 = sb("ones_1", [P, P])
        upper = sb("upper", [P, P])
        zero = sb("zero", [P, P])
        ident = sb("ident", [P, P])
        ident_b = sb("ident_b", [P, P], BF16)
        mask_t = sb("mask_t", [P, 4, P], BF16)
        mask_q = sb("mask_q", [P, P], BF16)
        sel = sb("sel", [96, H2, P], BF16)
        sel2 = sb("sel2", [96, H2, P2], BF16)
        selr = sb("selr", [4 * E, E, P], BF16)
        selr2 = sb("selr2", [4 * E, E, HE], BF16)
        tie = sb("tie", [P, NT, E])
        eps_t = sb("eps_t", [P, 1])
        A = sb("A", [P, MI * DS])
        ssum = sb("ssum", [P, BATCH, SEQ])
        sq, lnv = ssum[:, 0, :].rearrange("p (k t) -> p k t", t=BL), ssum[:, 1, :].rearrange("p (k t) -> p k t", t=BL)
        rs = sb("rs", [P, 2, BL])
        gam = sb("gam", [P, 4, 8])
        rt = sb("rt", [P, NT, 4 * E])
        rw = sb("rw", [P, 6, NT, E])
        rm = sb("rm", [P, 4, NT])
        rwb = sb("rwb", [P, 2, NT, E], BF16)
        rtf = sb("rtf", [4 * E, T])
        rtb = sb("rtb", [4 * E, T], BF16)
        pad = work[:, 11 * T:11 * T + 2 * BATCH * (DC - 1 + SEQ)].rearrange("p (j t) -> p j t", j=2 * BATCH)
        parts = sb("parts", [96, T], BF16)
        part_tmp = sb("part_tmp", [32, 2, BL], BF16)
        gmx = sb("gmx", [P, 4])
        gsm = sb("gsm", [P, 4])
        vacc = sb("vacc", [P, E * NB])
        vsum = sb("vsum", [P, E])
        vT = sb("vT", [E, P])
        wks = sb("wks", [P, BATCH, P])
        wvs = sb("wvs", [P, BATCH, P])
        wcomb = sb("wcomb", [P, BATCH, P])
        w_t = sb("w_t", [P, 2, TW])
        wo_t = sb("wo_t", [P, 2, P])
        dtr = sb("dtr", [P, 3 * H2])
        stat = sb("stat", [P, 4, NT])

        def V(name, k=0, p=P):
            return vec[0:p, VCOL[name] + k:VCOL[name] + k + 1]

        def blk(t, k):
            return t[:, k * BL:(k + 1) * BL]

        for group in (POOLED, LATE):
            at = 0
            for n, _, c in group:
                W[n] = shared[:, at:at + c]
                at += c
        slot = lambda n: work[:, n * T:(n + 1) * T]
        slots = lambda n, m: work[:, n * T:(n + m) * T]
        W["w13"] = slots(9, 2)
        W["w2e"] = slot(11)
        X = slot(0)
        XN = slot(1)
        S = slot(2)

        load = sems("load", "x vec weights pooled late experts row")
        const = sems("const", "fill ready")
        act_own, dve_own, pool_own = (ctx.enter_context(nc.semaphore(n)) for n in ("act_own", "dve_own", "pool_own"))
        NORM = "mean centred square var log rstd out"
        norm = sems("norm", NORM)
        m0 = stages("m0", pe="up:8 down:4 proj:16 xd:8 dtp:8 outp:4",
                    act="sign:3 biased:8 evac:16 xs:4 xd_out:4 e_ready:8 sum_out:4",
                    dve="weff:1 gated:8 x1:4 peak:1 scaled:4 conv:4 bc:4 delta:8 dtx:4 ygate:4 s_out:4",
                    each="gamma b_mm c_mm b_ready c_ready ysum decay drive scan state")
        f0 = stages("f0", pe="logit:4 probs_T:1 picked_T:1 vT:1 mix:4", act="lg:4 exps:2 v_out:1 g:4",
                    dve="top:2 probs:2 probs_out:1 picked:1 v:1 x_out:4", each="rt_out h1 h2 h3 wbc r1 r2 r3 pooled")
        m1 = stages("m1", pe="logit:1 gq:2 gk:2 comb:2 s:4", act="exps:1 s_out:4",
                    dve="sub:1 wk_scaled:2 wv_scaled:2 comb_out:2", each="soft_mm less_max exp weighted")
        f1 = stages("f1", pe="picked_T:1", act="g:4", dve="picked:1 x_out:4", each="rt_out wbc xw gate silu up h y")
        m2 = stages("m2", pe="bc_mm:8 dt_mm:1 cum:1 tot:1 cumT:1 bt:4 gt:4 rms:4",
                    act="arow:1 bc_pad:8 bc_tap:4 dt_soft:1 dec:1 cdec:1 hi_mid:8 neg:4 bc:4 bt_out:4 rstd:4",
                    dve="row:1 dt_biased:1 bc_conv:2 dt:1 adt:1 acum:1 dec_sub:1 parts:4 bc_conv1:2 gt_out:4 s_out:4",
                    each="mid w_in0 w_in1 h_mm h_pad h_tap g_mm sg conv hc tr hdt hdd arg L sdo_mm sdo st rec M yoff ydiag yd yoff_used y_sum y sqr ss wo outp first_out")
        f2 = stages("f2", pe="logit:1 picked_T:1 y:4", act="sig:1 y_out:4 g:4", dve="picked:1 x_out:4", each="rt_out h gelu wbc hw")
        m3 = stages("m3", pe="qk:8 v:4", act="qk_out:8 v_out:4", dve="s_out:2", each="s peak e p pT pT_out o o_out")
        f3 = stages("f3", pe="y:4", act="g:4", dve="x_out:4", each="h relu")
        ends = [f0, f1, f2, f3]
        done = sems("done", "stored")
        block = ctx.enter_context(nc.Block())

        def norm_pe(pe, r, src, ready=None, ready_at=0):
            def var(k):
                pe.wait_ge(norm["square"], NB * r + k + 1)
                if k >= 2:
                    pe.wait_ge(norm["log"], NB * r + k - 1)
                pe.matmul(ps[:, 2 + k % 2, :], ones_d[:, :], sq[:, k % 2, :], start=True, stop=True).then_inc(norm["var"], 1)

            for k in range(NB):
                if ready is not None:
                    pe.wait_ge(ready, ready_at + k + 1)
                if k >= 2:
                    pe.wait_ge(norm["centred"], NB * r + k - 1)
                pe.matmul(ps[:, k % 2, :], ones_d[:, :], blk(src, k), start=True, stop=True).then_inc(norm["mean"], 1)
                if k >= 1:
                    var(k - 1)
            var(NB - 1)

        def norm_dve(dve, own, r, src, dst, gain=None, bias=None):
            def scale(k):
                dve.wait_ge(norm["rstd"], NB * r + k + 1)
                mul = dve.tensor_tensor(blk(dst, k), blk(dst, k), rs[:, k % 2, :], ALU.mult)
                if gain is None:
                    mul.then_inc(norm["out"], 1)
                else:
                    own(mul)
                    dve.tensor_scalar(blk(dst, k), blk(dst, k), gain, bias, ALU.mult, ALU.add).then_inc(norm["out"], 1)

            for k in range(NB):
                dve.wait_ge(norm["mean"], NB * r + k + 1)
                dve.tensor_tensor(blk(dst, k), blk(src, k), ps[:, k % 2, :], ALU.subtract).then_inc(norm["centred"], 1)
                if k >= 1:
                    scale(k - 1)
            scale(NB - 1)

        def norm_act(act, r, dst):
            def root(k):
                act.wait_ge(norm["var"], NB * r + k + 1)
                act.activation(lnv[:, k % 2, :], ps[:, 2 + k % 2, :], ACT.Ln, bias=eps_t[:, :]).then_inc(norm["log"], 1)
                act.wait_ge(norm["log"], NB * r + k + 1)
                if k >= 2:
                    act.wait_ge(norm["out"], NB * r + k - 1)
                act.activation(rs[:, k % 2, :], lnv[:, k % 2, :], ACT.Exp, scale=-0.5).then_inc(norm["rstd"], 1)

            act.preload_act_table_set("natural_log_exp_and_others")
            for k in range(NB):
                act.wait_ge(norm["centred"], NB * r + k + 1)
                if k >= 2:
                    act.wait_ge(norm["var"], NB * r + k - 1)
                act.activation(sq[:, k % 2, :], blk(dst, k), ACT.Square).then_inc(norm["square"], 1)
                if k >= 1:
                    root(k - 1)
            root(NB - 1)

        def top2(dve, own, score, ind):
            cur, eq, t, pick = rw[:, 2], rw[:, 3], rw[:, 4], rw[:, 5]
            bc = lambda m: m.unsqueeze(2).to_broadcast([P, NT, E])
            for k in range(2):
                s = score if k == 0 else cur
                own(dve.tensor_reduce(rm[:, 0, :], s, AX.X, ALU.max))
                own(dve.tensor_tensor(eq, s, bc(rm[:, 0, :]), ALU.is_equal))
                own(dve.tensor_tensor(t, eq, tie[:, :, :], ALU.mult))
                own(dve.tensor_reduce(rm[:, 1, :], t, AX.X, ALU.max))
                if k == 0:
                    own(dve.tensor_tensor(ind, t, bc(rm[:, 1, :]), ALU.is_equal))
                    own(dve.scalar_tensor_tensor(cur, ind, -BIG, score, ALU.mult, ALU.add))
                else:
                    own(dve.tensor_tensor(pick, t, bc(rm[:, 1, :]), ALU.is_equal))
                    own(dve.tensor_tensor(ind, ind, pick, ALU.add))

        def split3(dve, own, w):
            hi, mid, lo = (rt[:, :, E * (k + 1):E * (k + 2)] for k in range(3))
            rest = rw[:, 3]
            own(dve.tensor_copy(rwb[:, 0], w))
            own(dve.tensor_copy(hi, rwb[:, 0]))
            own(dve.tensor_tensor(rest, w, hi, ALU.subtract))
            own(dve.tensor_copy(rwb[:, 1], rest))
            own(dve.tensor_copy(mid, rwb[:, 1]))
            return dve.tensor_tensor(lo, rest, mid, ALU.subtract)

        X1, H0 = slot(6), slot(3)
        gated = [slot(4), slot(5)]
        zgate = [slot(4), slot(5)]
        seqs = lambda n: slots(n, 2).rearrange("p (b t) -> p b t", t=SEQ)
        XS, DL, DX = seqs(7), seqs(9), seqs(11)
        dA = slot(13).rearrange("p (k t) -> p k t", t=SEQ)
        HS = [half for n in (3, 1) for half in (slot(n)[:, 0:SEQ], slot(n)[:, SEQ:])]
        BB = [slot(2)[:, 0:SEQ], slot(2)[:, SEQ:]]
        CB = [shared[:, 0:SEQ], shared[:, SEQ:2 * SEQ]]
        BMM, CMM, YACC = 0, 2, 4
        AT = dict(drive=3, state=3, scan=2, ysum=4)
        PER = DS * MI
        tmp4 = slot(13).rearrange("p (k t) -> p k t", t=BL)
        dt_low = slot(11)[0:DR, :]
        bc_rest = slot(12)[0:32, :].rearrange("p (k t) -> p k t", t=BL)

        def l0_up_pe(pe):
            norm_pe(pe, 1, XN, norm["out"])
            pe.wait_ge(m0["dve"], m0["weff"] + 1)
            for k in range(NB):
                pe.wait_ge(norm["out"], NB * 1 + k + 1)
                for m in range(MI):
                    n = MI * k + m
                    if n >= 4:
                        pe.wait_ge(m0["act"], m0["biased"] + n - 3)
                    pe.matmul(ps[:, 4 + n % 4, :], W["w1"][:, m * P:(m + 1) * P], blk(H0, k),
                              start=True, stop=True).then_inc(m0["pe"], 1)

        def l0_down_pe(pe):
            for k in range(NB):
                pe.wait_ge(m0["dve"], m0["gated"] + MI * (k + 1))
                if k >= 2:
                    pe.wait_ge(m0["dve"], m0["x1"] + k - 1)
                for m in range(MI):
                    mm = pe.matmul(ps[:, k % 2, :], W["w2"][:, m * P:(m + 1) * P], blk(gated[m], k),
                                   start=(m == 0), stop=(m == MI - 1))
                mm.then_inc(m0["pe"], 1)

        def l0_pe(pe):
            pe.wait_ge(load["weights"], 16 * len(FIRST))
            pe.wait_ge(f0["act"], f0["v_out"] + 1)
            norm_pe(pe, 2, X1, m0["dve"], m0["scaled"])
            for k in range(NB):
                pe.wait_ge(norm["out"], NB * 2 + k + 1)
                for m in range(2 * MI):
                    n = 2 * MI * k + m
                    if n >= 4:
                        pe.wait_ge(m0["act"], m0["evac"] + n - 3)
                    pe.matmul(ps[:, 4 + m, :], W["in_proj"][:, m * P:(m + 1) * P], blk(H0, k),
                              start=True, stop=True).then_inc(m0["pe"], 1)
            for k in range(NB):
                b, h = divmod(k, NB // BATCH)
                pe.wait_ge(m0["act"], m0["xs"] + MI * (b + 1))
                if k >= 2:
                    pe.wait_ge(m0["act"], m0["xd_out"] + k - 1)
                    pe.wait_ge(m0["dve"], m0["bc"] + k - 1)
                for part, (c0, c1) in enumerate(((0, DR), (DR, DR + 2 * DS))):
                    for m in range(MI):
                        mm = pe.matmul(ps[0:c1 - c0, 2 * (k % 2) + part, :],
                                       W["x_proj"][:, m * (DR + 2 * DS) + c0:m * (DR + 2 * DS) + c1],
                                       XS[:, MI * b + m, h * BL:(h + 1) * BL], start=(m == 0), stop=(m == MI - 1))
                    mm.then_inc(m0["pe"], 1)
            for k in range(NB):
                pe.wait_ge(m0["act"], m0["xd_out"] + k + 1)
                for m in range(MI):
                    n = MI * k + m
                    if n >= 4:
                        pe.wait_ge(m0["dve"], m0["delta"] + n - 3)
                    pe.matmul(ps[:, 4 + n % 4, :], W["dt_proj"][:, m * P:(m + 1) * P], blk(dt_low, k),
                              start=True, stop=True).then_inc(m0["pe"], 1)

            def spread(b, s, g):
                for first, bank, free, mm_sem in ((0, BMM, m0["b_ready"], m0["b_mm"]), (DS, CMM, m0["c_ready"], m0["c_mm"])):
                    if not (isinstance(g, int) and g == 0):
                        pe.wait_ge(free, g)
                    for h in range(2):
                        mm = pe.matmul(ps[:, bank + h, :], sel[:, bass.ds(first + s, 1), :].rearrange("k a p -> k (a p)"),
                                       parts[:, b * SEQ + h * BL:b * SEQ + (h + 1) * BL], start=True, stop=True)
                    mm.then_inc(mm_sem, 1)

            def add_up(n, v):
                pe.wait_ge(m0["state"], n + (AT["state"] + 1))
                for h in range(2):
                    mm = pe.matmul(ps[:, YACC + 2 * (v % MI) + h, :], ident[:, :], HS[v][:, h * BL:(h + 1) * BL],
                                   start=False, stop=False, skip_group_check=True)
                mm.then_inc(m0["ysum"], 1)

            pe.wait_ge(m0["dve"], m0["bc"] + NB)
            pe.wait_ge(const["ready"], 3)
            spread(0, 0, 0)
            pe.wait_ge(m0["dve"], m0["delta"] + MI * NB)
            pe.sem_inc(m0["ysum"], AT["ysum"])
            for b in range(BATCH):
                if b > 0:
                    pe.wait_ge(m0["act"], m0["sum_out"] + MI * b)
                for k in range(2 * MI):
                    pe.matmul(ps[:, YACC + k, :], zero[:, :], XS[:, 0, 0:BL], start=True, stop=False, skip_group_check=True)

                def pair(i, last):
                    for v2 in range(2):
                        if v2 == 0 or not last:
                            spread(b, i * 2 + (v2 + 1), i * 2 + (DS * b + v2 + 1))
                        elif b + 1 < BATCH:
                            spread(b + 1, 0, DS * (b + 1))
                        for m in range(MI):
                            add_up(i * 4 + (PER * b + MI * v2 + m), MI * v2 + m)

                with pe.Fori(0, DS // 2 - 1) as i:
                    pair(i, False)
                pair(DS // 2 - 1, True)
            for k in range(NB):
                b, h = divmod(k, NB // BATCH)
                pe.wait_ge(m0["dve"], m0["ygate"] + MI * (b + 1))
                for m in range(MI):
                    mm = pe.matmul(ps[:, k, :], W["out_proj"][:, m * P:(m + 1) * P],
                                   XS[:, MI * b + m, h * BL:(h + 1) * BL], start=(m == 0), stop=(m == MI - 1))
                mm.then_inc(m0["pe"], 1)

        def l0_up_act(act):
            act.wait_ge(load["weights"], 16 * len(SOON))
            act.activation(tmp4[:, 0, 0:DI], W["w1"][:, :], ACT.Sign).then_inc(m0["act"], 1)
            act.activation(tmp4[:, 1, 0:DI], W["w2"][:, :], ACT.Sign).then_inc(m0["act"], 1)
            act.activation(A[:, :], vec[:, VCOL["a_log"]:VCOL["a_log"] + MI * DS], ACT.Exp).then_inc(m0["act"], 1)
            norm_act(act, 1, H0)
            for k in range(NB):
                for m in range(MI):
                    act.wait_ge(m0["pe"], m0["up"] + MI * k + m + 1)
                    act.activation(blk(gated[m], k), ps[:, 4 + (MI * k + m) % 4, :], ACT.Identity,
                                   bias=V("b1", m)).then_inc(m0["act"], 1)

        def l0_act(act, own):
            norm_act(act, 2, H0)
            for k in range(NB):
                b, h = divmod(k, NB // BATCH)
                for m in range(2 * MI):
                    act.wait_ge(m0["pe"], m0["proj"] + 2 * MI * k + m + 1)
                    if m < MI:
                        act.activation(pad[:, MI * b + m, DC - 1 + h * BL:DC - 1 + (h + 1) * BL], ps[:, 4 + m, :],
                                       ACT.Copy).then_inc(m0["act"], 1)
                    else:
                        act.activation(blk(zgate[m - MI], k), ps[:, 4 + m, :], ACT.Silu).then_inc(m0["act"], 1)
            for j in range(BATCH * MI):
                act.wait_ge(m0["dve"], m0["conv"] + j + 1)
                act.activation(XS[:, j, :], DL[:, j, :], ACT.Silu).then_inc(m0["act"], 1)
            for k in range(NB):
                act.wait_ge(m0["pe"], m0["xd"] + 2 * k + 1)
                act.activation(blk(dt_low, k), ps[0:DR, 2 * (k % 2), :], ACT.Copy).then_inc(m0["act"], 1)
            act.preload_act_table_set("natural_log_exp_and_others")
            for k in range(NB):
                for m in range(MI):
                    n = MI * k + m
                    act.wait_ge(m0["pe"], m0["dtp"] + n + 1)
                    if n >= 2:
                        act.wait_ge(m0["dve"], m0["delta"] + n - 1)
                    t = tmp4[:, n % 2, :]
                    own(act.activation(t, ps[:, 4 + n % 4, :], ACT.Abs, bias=V("dt_b", m)))
                    own(act.activation(t, t, ACT.Exp, scale=-1.0))
                    act.activation(t, t, ACT.Ln, bias=1.0).then_inc(m0["act"], 1)
            act.wait_ge(m0["dve"], m0["delta"] + MI * NB)
            for b in range(BATCH):
                with act.Fori(0, DS // 2) as i:
                    for v2 in range(2):
                        g = i * 2 + (DS * b + v2)
                        for mm_sem, bank, dst, used, ready in ((m0["b_mm"], BMM, BB, "drive", m0["b_ready"]),
                                                               (m0["c_mm"], CMM, CB, "state", m0["c_ready"])):
                            act.wait_ge(mm_sem, g + 1)
                            act.wait_ge(m0[used], g * 2 + (AT[used] - 2))
                            act.activation(dst[v2].rearrange("p (k t) -> p k t", t=BL), ps[:, bank:bank + 2, :], ACT.Copy).then_inc(ready, 1)
                        for m in range(MI):
                            act.wait_ge(m0["scan"], g * 2 + (m - 1 + AT["scan"]))
                            act.activation(dA[:, m, :], DL[:, MI * b + m, :], ACT.Exp,
                                           scale=A[:, bass.ds(i * 2 + (m * DS + v2), 1)]).then_inc(m0["decay"], 1)
                act.wait_ge(m0["ysum"], AT["ysum"] + PER * (b + 1))
                for m in range(MI):
                    act.activation(DX[:, MI * b + m, :].rearrange("p (k t) -> p k t", t=BL), ps[:, YACC + 2 * m:YACC + 2 * m + 2, :],
                                   ACT.Copy).then_inc(m0["act"], 1)

        def l0_norm_dve(dve, own):
            dve.wait_ge(m0["act"], m0["sign"] + 3)
            for n, w in enumerate((W["w1"], W["w2"])):
                dve.wait_ge(load["weights"], 16 * len(SOON))
                own(dve.tensor_tensor(tmp4[:, n, 0:DI], tmp4[:, n, 0:DI], w[:, :], ALU.subtract))
                own(dve.tensor_tensor(w[:, :], w[:, :], tmp4[:, n, 0:DI], ALU.add))
            dve.tensor_scalar(A[:, :], A[:, :], -1.0, None, ALU.mult).then_inc(m0["dve"], 1)
            norm_dve(dve, own, 1, XN, H0, V("ln1_g"), V("ln1_b"))

        def l0_clip_dve(dve):
            for k in range(NB):
                for m in range(MI):
                    dve.wait_ge(m0["act"], m0["biased"] + MI * k + m + 1)
                    dve.tensor_scalar(blk(gated[m], k), blk(gated[m], k), 1.0, -1.0, ALU.min, ALU.max).then_inc(m0["dve"], 1)
            for k in range(NB):
                dve.wait_ge(m0["pe"], m0["down"] + k + 1)
                dve.scalar_tensor_tensor(blk(X1, k), ps[:, k % 2, :], V("b2"), blk(XN, k), ALU.add, ALU.add).then_inc(m0["dve"], 1)

        def l0_peak_dve(dve, own):
            dve.wait_ge(m0["dve"], m0["x1"] + NB)
            own(dve.tensor_reduce(gam[:, 0, :], X1.rearrange("p (g t) -> p g t", t=GL), AX.X, ALU.max,
                                  apply_absolute_value=True))
            dve.tensor_tensor(gam[:, 1, 0:GROUPS], gam[:, 0, 0:GROUPS], gam[:, 0, GROUPS:], ALU.max).then_inc(m0["dve"], 1)

        def l0_factor_dve(dve, own):
            g = gam[:, 3, 0:GROUPS]
            dve.wait_ge(m0["gamma"], 1)
            own(dve.tensor_scalar(g, gam[:, 2, 0:GROUPS], EPS, None, ALU.add))
            own(dve.reciprocal(g, g))
            own(dve.tensor_scalar(g, g, QB, None, ALU.mult))

        def l0_scale_dve(dve, own, k):
            lim = QB - EPS
            for h in range(BL // GL):
                part = X1[:, k * BL + h * GL:k * BL + (h + 1) * GL]
                q = (k * BL // GL + h) % GROUPS
                own(dve.tensor_scalar(part, part, gam[:, 3, q:q + 1], lim, ALU.mult, ALU.min))
            dve.tensor_scalar(blk(X1, k), blk(X1, k), -lim, None, ALU.max).then_inc(m0["dve"], 1)

        def l0_dve(dve, own):
            own(dve.memset(pad[:, :, 0:DC - 1], 0.0))
            norm_dve(dve, own, 2, X1, H0, V("ln2_g"), V("ln2_b"))
            for b in range(BATCH):
                dve.wait_ge(m0["act"], m0["evac"] + 2 * MI * (NB // BATCH) * (b + 1))
                for m in range(MI):
                    j = MI * b + m
                    own(dve.tensor_scalar(DL[:, j, :], pad[:, j, DC - 1:DC - 1 + SEQ], V("conv_w", m * DC + DC - 1),
                                          V("conv_b", m), ALU.mult, ALU.add))
                    for i in range(DC - 1):
                        c = dve.scalar_tensor_tensor(DL[:, j, :], pad[:, j, i:i + SEQ], V("conv_w", m * DC + i),
                                                     DL[:, j, :], ALU.mult, ALU.add)
                        if i < DC - 2:
                            own(c)
                    c.then_inc(m0["dve"], 1)
            for k in range(NB):
                dve.wait_ge(m0["pe"], m0["xd"] + 2 * k + 2)
                src = ps[0:32, 2 * (k % 2) + 1, :]
                r, tb = bc_rest[:, k % 2, :], part_tmp[0:32, k % 2, :]
                own(dve.tensor_copy(blk(parts[0:32, :], k), src))
                own(dve.tensor_tensor(r, src, blk(parts[0:32, :], k), ALU.subtract))
                own(dve.tensor_copy(tb, r))
                own(dve.tensor_copy(blk(parts[32:64, :], k), tb))
                dve.tensor_tensor(blk(parts[64:96, :], k), r, tb, ALU.subtract).then_inc(m0["dve"], 1)
            dve.wait_ge(m0["act"], m0["xs"] + BATCH * MI)
            dve.wait_ge(m0["dve"], m0["bc"] + NB)
            for k in range(NB):
                b, h = divmod(k, NB // BATCH)
                for m in range(MI):
                    n, j = MI * k + m, MI * b + m
                    d = DL[:, j, h * BL:(h + 1) * BL]
                    dve.wait_ge(m0["act"], m0["e_ready"] + n + 1)
                    own(dve.tensor_scalar(d, ps[:, 4 + n % 4, :], V("dt_b", m), 0.0, ALU.add, ALU.max))
                    dve.tensor_tensor(d, d, tmp4[:, n % 2, :], ALU.add).then_inc(m0["dve"], 1)
            dve.wait_ge(m0["dve"], m0["delta"] + MI * NB)
            dve.wait_ge(m0["pe"], m0["dtp"] + MI * NB)
            for j in range(BATCH * MI):
                dve.tensor_tensor(DX[:, j, :], DL[:, j, :], XS[:, j, :], ALU.mult).then_inc(m0["dve"], 1)
            dve.wait_ge(m0["dve"], m0["dtx"] + BATCH * MI)
            dve.sem_inc(m0["drive"], AT["drive"])
            dve.sem_inc(m0["scan"], AT["scan"])
            for b in range(BATCH):
                with dve.Fori(0, DS // 2) as i:
                    for v in range(2 * MI):
                        n, m = i * 4 + (PER * b + v), v % MI
                        if m == 0:
                            dve.wait_ge(m0["b_ready"], i * 2 + (DS * b + v // MI + 1))
                        dve.wait_ge(m0["ysum"], n + (AT["ysum"] - 3))
                        dve.tensor_tensor(HS[v], DX[:, MI * b + m, :], BB[v // MI], ALU.mult).then_inc(m0["drive"], 1)
                        dve.wait_ge(m0["drive"], n + (AT["drive"] + 1))
                        dve.wait_ge(m0["decay"], n + 1)
                        dve.tensor_tensor_scan(HS[v], dA[:, m, :], HS[v], 0.0, ALU.mult, ALU.add).then_inc(m0["scan"], 1)
            for j in range(BATCH * MI):
                dve.wait_ge(m0["act"], m0["sum_out"] + j + 1)
                own(dve.scalar_tensor_tensor(XS[:, j, :], XS[:, j, :], V("d", j % MI), DX[:, j, :], ALU.mult, ALU.add))
                dve.tensor_tensor(XS[:, j, :], XS[:, j, :], zgate[j % MI][:, (j // MI) * SEQ:(j // MI + 1) * SEQ],
                                  ALU.mult).then_inc(m0["dve"], 1)
            for k in range(NB):
                dve.wait_ge(m0["pe"], m0["outp"] + k + 1)
                dve.tensor_tensor(blk(S, k), ps[:, k, :], blk(X1, k), ALU.add).then_inc(m0["dve"], 1)

        def l0_pool(pool):
            pool.wait_ge(m0["dve"], m0["peak"] + 1)
            pool.partition_all_reduce(gam[:, 2, 0:GROUPS], gam[:, 1, 0:GROUPS], P, RMAX).then_inc(m0["gamma"], 1)
            pool.sem_inc(m0["state"], AT["state"])
            for b in range(BATCH):
                with pool.Fori(0, DS // 2) as i:
                    for v in range(2 * MI):
                        n = i * 4 + (PER * b + v)
                        pool.wait_ge(m0["scan"], n + (AT["scan"] + 1))
                        if v % MI == 0:
                            pool.wait_ge(m0["c_ready"], i * 2 + (DS * b + v // MI + 1))
                        pool.tensor_tensor(HS[v], HS[v], CB[v // MI], ALU.mult).then_inc(m0["state"], 1)

        def picked_pe(pe, g, bank=4):
            pe.wait_ge(g["dve"], g["picked"] + 1)
            for i in range(NT):
                mm = pe.transpose(ps[0:4 * E, bank + i // 4, (i % 4) * P:(i % 4 + 1) * P], rt[:, i, :], ident[:, :])
            mm.then_inc(g["pe"], 1)

        def picked_out_act(act, g):
            act.wait_ge(g["rt_out"], 1)
            act.activation(rtb[:, :], rtf[:, :], ACT.Copy).then_inc(g["rt_out"], 1)

        def picked_out_dve(dve, g, bank=4):
            dve.wait_ge(g["pe"], g["picked_T"] + 1)
            dve.tensor_copy(rtf[:, :].rearrange("p (k t) -> p k t", t=BL), ps[0:4 * E, bank:bank + 4, :]).then_inc(g["rt_out"], 1)

        lg, pr = slot(11)[0:E, :], slot(12)[0:E, :]
        fh = [[blk(slot(n), u) for u in range(4)] for n in (4, 5, 7)]

        def f0_pe(pe):
            pe.wait_ge(load["weights"], 16 * len(SOON))
            for k in range(NB):
                pe.wait_ge(norm["out"], NB * 0 + k + 1)
                pe.matmul(ps[0:E, 4 + k, :], W["gate0"][:, :], blk(XN, k), start=True, stop=True).then_inc(f0["pe"], 1)
            pe.wait_ge(f0["act"], f0["lg"] + NB)
            l0_up_pe(pe)
            pe.wait_ge(f0["dve"], f0["probs"] + BATCH)
            for i in range(NT):
                mm = pe.transpose(ps[:, 2, i * E:(i + 1) * E], pr[:, i * P:(i + 1) * P], ident[0:E, 0:E])
            mm.then_inc(f0["pe"], 1)
            pe.wait_ge(m0["act"], m0["biased"] + MI * NB)
            l0_down_pe(pe)
            pe.wait_ge(m0["dve"], m0["x1"] + NB)
            pe.wait_ge(f0["dve"], f0["probs_out"] + 1)
            pe.wait_ge(load["pooled"], 16 * len(POOLED))
            N = E * NB
            for n in range(N + 4):
                if n == 4:
                    picked_pe(pe, f0)
                    pe.wait_ge(f0["rt_out"], 2)
                    pe.wait_ge(const["ready"], 2)
                if n < N:
                    e, k = divmod(n, NB)
                    if n >= 2:
                        pe.wait_ge(f0["r1"], n - 1)
                    pe.matmul(ps[:, n % 2, :], W["f1"][:, e * P:(e + 1) * P], blk(XN, k), start=True, stop=True).then_inc(f0["h1"], 1)
                if 2 <= n < N + 2:
                    q = n - 2
                    pe.wait_ge(f0["r1"], q + 1)
                    if q >= 2:
                        pe.wait_ge(f0["r2"], q - 1)
                    pe.matmul(ps[:, 2 + q % 2, :], W["f2"][:, (q // NB) * P:(q // NB + 1) * P], fh[0][q % 4],
                              start=True, stop=True).then_inc(f0["h2"], 1)
                if n >= 4:
                    q = n - 4
                    pe.wait_ge(f0["r2"], q + 1)
                    if q >= 2:
                        pe.wait_ge(f0["r3"], q - 1)
                        pe.wait_ge(f0["pooled"], q - 1)
                    pe.matmul(ps[:, 4 + q % 2, :], W["f3"][:, (q // NB) * P:(q // NB + 1) * P], fh[1][q % 4],
                              start=True, stop=True).then_inc(f0["h3"], 1)
                    pe.matmul(ps[:, 6 + q % 2, :], selr[:, q // NB, :], blk(rtb, q % NB),
                              start=True, stop=True).then_inc(f0["wbc"], 1)
            pe.wait_ge(f0["dve"], f0["v"] + 1)
            pe.transpose(ps[0:E, 0, 0:P], vsum[:, :], ident[:, :]).then_inc(f0["pe"], 1)

        def f0_mix_pe(pe):
            pe.wait_ge(f0["act"], f0["v_out"] + 1)
            for k in range(NB):
                pe.matmul(ps[:, 4 + k, :], vT[:, :], blk(rtf[0:E, :], k), start=True, stop=True).then_inc(f0["pe"], 1)

        def f0_act(act, own):
            for k in range(NB):
                act.wait_ge(f0["pe"], f0["logit"] + k + 1)
                act.activation(blk(lg, k), ps[0:E, 4 + k, :], ACT.Identity, bias=V("gate_b", 0, E)).then_inc(f0["act"], 1)
            for b in range(BATCH):
                act.wait_ge(f0["dve"], f0["top"] + b + 1)
                act.activation(pr[:, b * SEQ:(b + 1) * SEQ], lg[:, b * SEQ:(b + 1) * SEQ], ACT.Exp,
                               bias=gmx[0:E, b:b + 1], accum_out=gsm[0:E, b:b + 1]).then_inc(f0["act"], 1)
            l0_up_act(act)
            N = E * NB
            for n in range(N + 4):
                if n == 4:
                    picked_out_act(act, f0)
                if n < N:
                    act.wait_ge(f0["h1"], n + 1)
                    if n >= 4:
                        act.wait_ge(f0["h2"], n - 3)
                    act.activation(fh[0][n % 4], ps[:, n % 2, :], ACT.Relu, bias=V("fb1", n // NB)).then_inc(f0["r1"], 1)
                if n >= 4:
                    q = n - 4
                    act.wait_ge(f0["h3"], q + 1)
                    if q >= 4:
                        act.wait_ge(f0["pooled"], q - 3)
                    act.activation(fh[2][q % 4], ps[:, 4 + q % 2, :], ACT.Relu, bias=V("fb3", q // NB)).then_inc(f0["r3"], 1)
            act.wait_ge(f0["pe"], f0["vT"] + 1)
            act.activation(vT[:, :], ps[0:E, 0, 0:P], ACT.Copy).then_inc(f0["act"], 1)

        def f0_dve(dve, own):
            for b in range(BATCH):
                dve.wait_ge(f0["act"], f0["lg"] + (b + 1) * NB // BATCH)
                dve.tensor_reduce(gmx[0:E, b:b + 1], lg[:, b * SEQ:(b + 1) * SEQ], AX.X, ALU.max, negate=True).then_inc(f0["dve"], 1)
            l0_norm_dve(dve, own)
            dve.wait_ge(f0["act"], f0["exps"] + BATCH)
            own(dve.reciprocal(gsm[0:E, 2:4], gsm[0:E, 0:2]))
            for b in range(BATCH):
                dve.tensor_scalar(pr[:, b * SEQ:(b + 1) * SEQ], pr[:, b * SEQ:(b + 1) * SEQ], gsm[0:E, 2 + b:3 + b], None,
                                  ALU.mult).then_inc(f0["dve"], 1)
            l0_clip_dve(dve)
            dve.wait_ge(f0["pe"], f0["probs_T"] + 1)
            dve.wait_ge(const["ready"], 2)
            dve.tensor_copy(rw[:, 0], ps[:, 2, 0:NT * E].rearrange("p (i e) -> p i e", e=E)).then_inc(f0["dve"], 1)
            dve.wait_ge(f0["dve"], f0["probs_out"] + 1)
            top2(dve, own, rw[:, 0], rt[:, :, 0:E])
            own(dve.tensor_tensor(rw[:, 1], rw[:, 0], rt[:, :, 0:E], ALU.mult))
            split3(dve, own, rw[:, 1]).then_inc(f0["dve"], 1)
            picked_out_dve(dve, f0)
            N = E * NB
            for n in range(N + 2):
                if n == 4:
                    l0_peak_dve(dve, own)
                elif n == 8:
                    l0_factor_dve(dve, own)
                elif n in range(10, 10 + 2 * NB, 2):
                    l0_scale_dve(dve, own, (n - 10) // 2)
                if n < N:
                    dve.wait_ge(f0["h2"], n + 1)
                    if n >= 4:
                        dve.wait_ge(f0["h3"], n - 3)
                    dve.tensor_scalar(fh[1][n % 4], ps[:, 2 + n % 2, :], V("fb2", n // NB), 0.0, ALU.add, ALU.max).then_inc(f0["r2"], 1)
                if n >= 2:
                    q = n - 2
                    dve.wait_ge(f0["r3"], q + 1)
                    dve.wait_ge(f0["wbc"], q + 1)
                    dve.tensor_tensor_reduce(fh[2][q % 4], fh[2][q % 4], ps[:, 6 + q % 2, :], 1.0, 0.0, ALU.mult, ALU.add,
                                             vacc[:, q:q + 1]).then_inc(f0["pooled"], 1)
            dve.wait_ge(f0["pooled"], N)
            dve.tensor_reduce(vsum[:, :], vacc[:, :].rearrange("p (e k) -> p e k", k=NB), AX.X, ALU.add).then_inc(f0["dve"], 1)

        G = slot(13)

        def gate_act(act, f):
            for k in range(NB):
                act.wait_ge(f["pe"], f["mix"] + k + 1)
                act.activation(blk(G, k), ps[:, 4 + k, :], ACT.Silu).then_inc(f["act"], 1)

        def gate_dve(dve, own, f, s_ready, s_at):
            for k in range(NB):
                dve.wait_ge(f["act"], f["g"] + k + 1)
                dve.wait_ge(s_ready, s_at + k + 1)
                own(dve.tensor_tensor(blk(S, k), blk(S, k), blk(G, k), ALU.mult))
                dve.tensor_tensor(blk(X, k), blk(X, k), blk(S, k), ALU.add).then_inc(f["dve"], 1)

        SC1 = float(P) ** -0.5
        tiles = lambda n: slot(n).rearrange("p (i e) -> p i e", e=P)
        QW, PW = tiles(3), tiles(4)
        tile = lambda t, i: t[:, i * P:(i + 1) * P]
        four = lambda k: ps[:, k, :].rearrange("p (i e) -> p i e", e=P)
        xw = [blk(slot(5), u) for u in range(2)]
        sil = [[blk(slot(6), 2 * u + m) for m in range(2)] for u in range(2)]
        hid = [[blk(slot(7), 2 * u + m) for m in range(2)] for u in range(2)]

        SIDE = 7
        SOFT = {j: 2 * j + 2 * (j // NB) for j in range(2 * NB)}
        GQ = {b: SOFT[NB - 1] + 2 + b for b in range(BATCH)}
        GK = {b: SOFT[2 * NB - 1] + 2 + b for b in range(BATCH)}
        COMB = {b: GK[BATCH - 1] + 1 + b for b in range(BATCH)}
        OUT = {k: COMB[BATCH - 1] + 1 + k for k in range(NB)}
        soft_buf = lambda j: (QW, PW)[j // NB][:, 4 * (j % NB):4 * (j % NB) + 4, :]
        at_step = lambda plan, n: [j for j, step in plan.items() if step == n]

        def l1_side_pe(pe, n):
            for j in at_step(SOFT, n):
                k, b = j % NB, j % NB // (NB // BATCH)
                if j == NB:
                    pe.wait_ge(m1["dve"], m1["wk_scaled"] + BATCH)
                elif j:
                    pe.wait_ge(m1["weighted"], j)
                for i in range(4):
                    mm = pe.matmul(four(SIDE)[:, i, :], tile(XN, 4 * k + i), W["wq"] if j < NB else wks[:, b, :], start=True, stop=True)
                mm.then_inc(m1["soft_mm"], 1)
            for b in at_step(GQ, n):
                pe.wait_ge(m1["weighted"], NB)
                if b:
                    pe.wait_ge(m1["dve"], m1["wk_scaled"] + b)
                for i in range(TB):
                    mm = pe.matmul(ps[:, SIDE, 0:P], ones_1[:, :], QW[:, b * TB + i, :], start=(i == 0), stop=(i == TB - 1))
                mm.then_inc(m1["pe"], 1)
            for b in at_step(GK, n):
                pe.wait_ge(m1["weighted"], 2 * NB)
                if b:
                    pe.wait_ge(m1["dve"], m1["wv_scaled"] + b)
                for i in range(TB):
                    mm = pe.matmul(ps[:, SIDE, 0:1], PW[:, b * TB + i, :], ones_1[:, 0:1], start=(i == 0), stop=(i == TB - 1))
                mm.then_inc(m1["pe"], 1)
            for b in at_step(COMB, n):
                pe.wait_ge(m1["dve"], m1["wv_scaled"] + BATCH if b == 0 else m1["comb_out"] + b)
                pe.matmul(ps[:, SIDE, 0:P], wvs[:, b, :], W["wr"], start=True, stop=True).then_inc(m1["pe"], 1)
            for k in at_step(OUT, n):
                if k == 0:
                    pe.wait_ge(m1["dve"], m1["comb_out"] + BATCH)
                else:
                    pe.wait_ge(m1["act"], m1["s_out"] + k)
                pe.matmul(ps[:, SIDE, :], wcomb[:, k // (NB // BATCH), :], blk(XN, k), start=True, stop=True).then_inc(m1["pe"], 1)

        def l1_side_act(act, n):
            for j in at_step(SOFT, n - 2):
                act.wait_ge(m1["less_max"], j + 1)
                act.activation(soft_buf(j), soft_buf(j), ACT.Exp, scale=SC1).then_inc(m1["exp"], 1)
            for k in at_step(OUT, n - 1):
                act.wait_ge(m1["pe"], m1["s"] + k + 1)
                act.activation(blk(S, k), ps[:, SIDE, :], ACT.Copy).then_inc(m1["act"], 1)

        def l1_side_dve(dve, own, n):
            bc = lambda v: v.unsqueeze(2).to_broadcast([P, 4, P])
            for j in at_step(SOFT, n - 1):
                peak = stat[:, 0, 0:4]
                dve.wait_ge(m1["soft_mm"], j + 1)
                own(dve.tensor_reduce(peak, four(SIDE), AX.X, ALU.max))
                dve.tensor_tensor(soft_buf(j), four(SIDE), bc(peak), ALU.subtract).then_inc(m1["less_max"], 1)
            for j in at_step(SOFT, n - 2):
                q, total = soft_buf(j), stat[:, 1, 0:4]
                dve.wait_ge(m1["exp"], j + 1)
                own(dve.tensor_reduce(total, q, AX.X, ALU.add))
                own(dve.reciprocal(total, total))
                own(dve.tensor_tensor(q, q, four(SIDE), ALU.mult))
                dve.tensor_tensor(q, q, bc(total), ALU.mult).then_inc(m1["weighted"], 1)
            for b in at_step(GQ, n - 1):
                dve.wait_ge(m1["pe"], m1["gq"] + b + 1)
                dve.tensor_tensor(wks[:, b, :], W["wk"], ps[:, SIDE, 0:P], ALU.mult).then_inc(m1["dve"], 1)
            for b in at_step(GK, n - 1):
                dve.wait_ge(m1["pe"], m1["gk"] + b + 1)
                dve.tensor_scalar(wvs[:, b, :], W["wvT"], ps[:, SIDE, 0:1], None, ALU.mult).then_inc(m1["dve"], 1)
            for b in at_step(COMB, n - 1):
                dve.wait_ge(m1["pe"], m1["comb"] + b + 1)
                dve.tensor_tensor(wcomb[:, b, :], W["wq"], ps[:, SIDE, 0:P], ALU.add).then_inc(m1["dve"], 1)

        def l1_pe(pe):
            norm_pe(pe, 3, X, f0["dve"], f0["x_out"])
            pe.wait_ge(norm["out"], NB * 4)
            for i in range(NT):
                mm = pe.matmul(ps[:, 2, i * E:(i + 1) * E], tile(XN, i), W["router"], start=True, stop=True)
            mm.then_inc(m1["pe"], 1)
            picked_pe(pe, f1, 3)
            pe.wait_ge(f1["rt_out"], 2)
            pe.wait_ge(load["experts"], 16 * len(EXPERTS))
            N = E * NB
            for n in range(-1, N + 1):
                if n + 1 < N:
                    k, e = divmod(n + 1, E)
                    if n >= 0:
                        pe.wait_ge(f1["xw"], n + 1)
                    pe.matmul(ps[:, 0, :], selr[:, e, :], blk(rtb, k), start=True, stop=True).then_inc(f1["wbc"], 1)
                    for m in range(2):
                        if n >= 0:
                            pe.wait_ge(f1["silu"], 2 * n + m + 1)
                        c = e * 2 * I1 + m * P
                        pe.matmul(ps[:, 1 + m, :], W["w13"][:, c:c + P], blk(XN, k), start=True, stop=True).then_inc(f1["gate"], 1)
                if 0 <= n < N:
                    k, e = divmod(n, E)
                    pe.wait_ge(f1["xw"], n + 1)
                    for m in range(2):
                        if n >= 1:
                            pe.wait_ge(f1["h"], 2 * (n - 1) + m + 1)
                        c = e * 2 * I1 + I1 + m * P
                        pe.matmul(ps[:, 3 + m, :], W["w13"][:, c:c + P], xw[n % 2], start=True, stop=True).then_inc(f1["up"], 1)
                if n >= 1:
                    q = n - 1
                    k, e = divmod(q, E)
                    if e == 0 and k >= 2:
                        pe.wait_ge(f1["act"], f1["g"] + k - 1)
                    for m in range(2):
                        pe.wait_ge(f1["h"], 2 * q + m + 1)
                        mm = pe.matmul(ps[:, 5 + k % 2, :], W["w2e"][:, (2 * e + m) * P:(2 * e + m + 1) * P], hid[q % 2][m],
                                       start=(e == 0 and m == 0), stop=(e == E - 1 and m == 1))
                    mm.then_inc(f1["y"], 1)
                l1_side_pe(pe, n)

        def l1_act(act, own):
            norm_act(act, 3, XN)
            act.wait_ge(m1["dve"], m1["sub"] + 1)
            act.activation(rw[:, 0], rw[:, 0], ACT.Exp).then_inc(m1["act"], 1)
            picked_out_act(act, f1)
            N = E * NB
            for n in range(N):
                for m in range(2):
                    act.wait_ge(f1["gate"], 2 * n + m + 1)
                    if n >= 2:
                        act.wait_ge(f1["h"], 2 * (n - 2) + m + 1)
                    act.activation(sil[n % 2][m], ps[:, 1 + m, :], ACT.Silu).then_inc(f1["silu"], 1)
                l1_side_act(act, n)
                if n % E == 2 and n > E:
                    k = n // E - 1
                    act.wait_ge(f1["y"], E * (k + 1))
                    act.activation(blk(G, k), ps[:, 5 + k % 2, :], ACT.Silu).then_inc(f1["act"], 1)
            act.wait_ge(f1["y"], N)
            act.activation(blk(G, NB - 1), ps[:, 5 + (NB - 1) % 2, :], ACT.Silu).then_inc(f1["act"], 1)

        def l1_dve(dve, own):
            bc = lambda v: v.unsqueeze(2).to_broadcast([P, NT, E])
            norm_dve(dve, own, 3, X, XN)
            dve.wait_ge(m1["pe"], m1["logit"] + 1)
            lgt = ps[:, 2, 0:NT * E].rearrange("p (i e) -> p i e", e=E)
            own(dve.tensor_reduce(rm[:, 0, :], lgt, AX.X, ALU.max))
            dve.tensor_tensor(rw[:, 0], lgt, bc(rm[:, 0, :]), ALU.subtract).then_inc(m1["dve"], 1)
            dve.wait_ge(m1["act"], m1["exps"] + 1)
            own(dve.tensor_reduce(rm[:, 2, :], rw[:, 0], AX.X, ALU.add))
            own(dve.reciprocal(rm[:, 2, :], rm[:, 2, :]))
            own(dve.tensor_tensor(rw[:, 0], rw[:, 0], bc(rm[:, 2, :]), ALU.mult))
            share(dve, own, rw[:, 0], 1e-6).then_inc(f1["dve"], 1)
            picked_out_dve(dve, f1, 3)
            N = E * NB
            for n in range(N + 1):
                if n < N:
                    dve.wait_ge(f1["wbc"], n + 1)
                    if n >= 2:
                        dve.wait_ge(f1["up"], 2 * (n - 1))
                    dve.tensor_tensor(xw[n % 2], blk(XN, n // E), ps[:, 0, :], ALU.mult).then_inc(f1["xw"], 1)
                if n >= 1:
                    q = n - 1
                    for m in range(2):
                        dve.wait_ge(f1["up"], 2 * q + m + 1)
                        dve.wait_ge(f1["silu"], 2 * q + m + 1)
                        if q >= 2:
                            dve.wait_ge(f1["y"], q - 1)
                        dve.tensor_tensor(hid[q % 2][m], sil[q % 2][m], ps[:, 3 + m, :], ALU.mult).then_inc(f1["h"], 1)
                l1_side_dve(dve, own, n)
            gate_dve(dve, own, f1, m1["act"], m1["s_out"])

        def share(dve, own, score, floor):
            bc = lambda v: v.unsqueeze(2).to_broadcast([P, NT, E])
            top2(dve, own, score, rt[:, :, 0:E])
            own(dve.tensor_tensor(rw[:, 1], score, rt[:, :, 0:E], ALU.mult))
            own(dve.tensor_reduce(rm[:, 2, :], rw[:, 1], AX.X, ALU.add))
            if floor:
                own(dve.tensor_scalar(rm[:, 2, :], rm[:, 2, :], floor, None, ALU.add))
            own(dve.reciprocal(rm[:, 2, :], rm[:, 2, :]))
            own(dve.tensor_tensor(rw[:, 1], rw[:, 1], bc(rm[:, 2, :]), ALU.mult))
            return split3(dve, own, rw[:, 1])

        BCH = [slot(3), slot(4)]
        BT, GT = tiles(5), tiles(6)
        nparts = slot(7)[0:96, 0:T // 2].bitcast(BF16)
        acum = slot(7)[:, SEQ:SEQ + NT * H2]
        DT, ADT, DEC, CDEC = (slot(8)[:, k * NT * H2:(k + 1) * NT * H2].rearrange("p (i h) -> p i h", h=H2) for k in range(4))
        cv = slots(5, 2).rearrange("p (j t) -> p j t", t=SEQ)
        flat = lambda o, n: work[:, 9 * T + o:9 * T + o + n]
        HP = flat(0, 1028)
        HC = [flat(1028 + SEQ * u, SEQ) for u in range(2)]
        SG = [flat(1028 + SEQ * (2 + u), SEQ) for u in range(2)]
        HDT, HDD = flat(1028 + 4 * SEQ, SEQ), flat(1028 + 5 * SEQ, SEQ)
        LM = flat(1028 + 6 * SEQ, 2 * SEQ)
        Y = [slot(2)[:, SEQ * u:SEQ * (u + 1)] for u in range(2)]
        ST = slot(7)[:, SEQ:]
        first_sum = [slot(8)[:, NT * H2:2 * NT * H2], flat(1028 + 8 * SEQ, BL)]
        K3 = DC - 1
        two = lambda k: ps[:, k:k + 2, :]
        wide = lambda t: t.rearrange("p (k t) -> p k t", t=BL)
        flat2 = lambda k: two(k).rearrange("p k t -> p (k t)")
        heads = lambda t: t.rearrange("p (c h q) -> p c h q", h=2, q=P2)
        FRONT, MID, BACK, ACC = 0, 2, 4, 6
        GT_BANK = (2, 3, 6, 7)
        LAST = CT - 1

        par = lambda u, name, k=0: w_t[:, u, TCOL[name] + k:TCOL[name] + k + 1]

        def steps(eng, step):
            for b in range(BATCH):
                n0 = CT * b
                step(n0, b, 0, 0, n0 // 2, 1)
                with eng.Fori(0, (CT - 2) // 2) as i:
                    for v in range(2):
                        step(i * 2 + (n0 + 1 + v), b, i * 2 + (1 + v), (1 + v) % 2, i + (n0 // 2 + 1), i * 2 + (2 + v))
                step(n0 + LAST, b, LAST, LAST % 2, n0 // 2 + CT // 2, None)

        def l2_sync(sp):
            def load_tile(t, u):
                sp.dma_start(w_t[:, u, :], a["tile_w"][:, bass.ds(t * TW, TW)]).then_inc((m2["w_in0"], m2["w_in1"])[u], 16)

            def used(n):
                sp.wait_ge(m2["hc"], n + 1)
                sp.wait_ge(m2["wo"], n + 1)

            load_tile(0, 0)
            load_tile(1, 1)
            for b in range(BATCH):
                with sp.Fori(0, CT // 2 - 1) as i:
                    for u in range(2):
                        used(i * 2 + (CT * b + u))
                        load_tile(i * 2 + (2 + u), u)
                if b < BATCH - 1:
                    for u in range(2):
                        used(CT * b + CT - 2 + u)
                        load_tile(u, u)

        def l2_pe(pe):
            def project_h(n, b, u, half):
                pe.wait_ge((m2["w_in0"], m2["w_in1"])[u], half * 16 + 16)
                for h in range(2):
                    mm = pe.matmul(ps[:, FRONT + h, :], w_t[:, u, TCOL["h"]:TCOL["h"] + P], blk(XN, 2 * b + h), start=True, stop=True)
                mm.then_inc(m2["h_mm"], 1)

            def project_gate(n, b, u):
                pe.wait_ge(m2["h_pad"], n + 1)
                for h in range(2):
                    mm = pe.matmul(ps[:, FRONT + h, :], w_t[:, u, TCOL["gate"]:TCOL["gate"] + P], blk(XN, 2 * b + h), start=True, stop=True)
                mm.then_inc(m2["g_mm"], 1)

            def arguments(n, b, t, quarters):
                for q in quarters:
                    if q >= 2:
                        pe.wait_ge(m2["L"], n * 4 + (q - 1))
                    bank = BACK + q % 2
                    pe.matmul(ps[:, bank, :], ident_b[:, :], mask_t[:, :, :], start=True, stop=False, skip_group_check=True)
                    for cc in range(2):
                        c = b * TB + 2 * q + cc
                        pe.matmul(ps[:, bank, cc * 2 * P:(cc + 1) * 2 * P], nparts[:, c * P:(c + 1) * P],
                                  sel[:, bass.ds(t * 2, 2), :], start=False, stop=False, skip_group_check=True)
                        for h in range(2):
                            mm = pe.matmul(ps[:, bank, (2 * cc + h) * P:(2 * cc + h + 1) * P], sel[:, bass.ds(t * 2 + h, 1), :].rearrange("k a p -> k (a p)"),
                                           parts[:, c * P:(c + 1) * P], start=False, stop=(cc == 1 and h == 1),
                                           skip_group_check=True)
                    mm.then_inc(m2["arg"], 1)

            def turn_h(n, u):
                pe.wait_ge(m2["hc"], n + 1)
                pe.wait_ge(m2["sg"], n + 1)
                for c in range(TB):
                    mm = pe.transpose(four(FRONT + c // 4)[:, c % 4, :], tile(HC[u], c), ident[:, :])
                mm.then_inc(m2["tr"], 1)

            def spread_sums(n, b, t):
                for h in range(2):
                    mm = pe.matmul(ps[:, MID + h, :], sel2[:, bass.ds(t * 2, 2), :].rearrange("k a p -> k (a p)"),
                                   parts[:, b * SEQ + h * BL:b * SEQ + (h + 1) * BL], start=True, stop=True)
                mm.then_inc(m2["sdo_mm"], 1)

            def shares(n, b):
                pe.wait_ge(m2["sdo"], n + 1)
                pe.wait_ge(m2["hdd"], n + 1)
                for c in range(TB - 1):
                    mm = pe.matmul(four(MID + c // 4)[:, c % 4, :], BT[:, b * TB + c, :], HDD[:, c * P:(c + 1) * P], start=True, stop=True)
                mm.then_inc(m2["st"], 1)

            def sum_out(n, u):
                pe.wait_ge(m2["y"], n + 2)
                pe.wait_ge(m2["wo"], n + 1)
                for h in range(2):
                    mm = pe.matmul(ps[:, ACC + h, :], wo_t[:, u, :], Y[u][:, h * BL:(h + 1) * BL], start=False, stop=False,
                                   skip_group_check=True)
                mm.then_inc(m2["outp"], 1)

            def step(n, b, t, u, half, t1):
                b1, u1 = (b, 1 - u) if t1 is not None else (b + 1, 0)
                t1 = 0 if t1 is None else t1
                more = b1 < BATCH
                if more:
                    pe.wait_ge(m2["hdt"], n + 1)
                    project_h(n + 1, b1, u1, half)
                if not (isinstance(n, int) and n == 0):
                    sum_out(n - 1, 1 - u)
                pe.wait_ge(m2["M"], n + 1)
                for c in range(TB):
                    for h in range(2):
                        mm = pe.matmul(four(BACK + c // 4)[h * P2:(h + 1) * P2, c % 4, :], HDT[:, c * P + h * P2:c * P + (h + 1) * P2],
                                       LM[:, (2 * c + h) * P:(2 * c + h + 1) * P], start=True, stop=True)
                mm.then_inc(m2["ydiag"], 1)
                if more:
                    project_gate(n + 1, b1, u1)
                pe.wait_ge(m2["rec"], n + 1)
                for c in range(1, TB):
                    mm = pe.matmul(four(MID + c // 4)[:, c % 4, :], ST[:, c * P:(c + 1) * P], tile(BCH[1], b * TB + c),
                                   start=True, stop=True)
                mm.then_inc(m2["yoff"], 1)
                if more:
                    pe.wait_ge(m2["yd"], n + 1)
                    arguments(n + 1, b1, t1, (0, 1))
                    turn_h(n + 1, u1)
                    arguments(n + 1, b1, t1, (2, 3))
                    pe.wait_ge(m2["yoff_used"], n + 1)
                    spread_sums(n + 1, b1, t1)
                    shares(n + 1, b1)
                if isinstance(t, int) and t == 0:
                    if b > 0:
                        pe.wait_ge(m2["first_out"], 1)
                    for h in range(2):
                        pe.matmul(ps[:, ACC + h, :], zero[:, :], blk(XN, h), start=True, stop=False, skip_group_check=True)

            norm_pe(pe, 4, X, f1["dve"], f1["x_out"])
            pe.wait_ge(norm["out"], NB * 5)
            pe.wait_ge(load["late"], 16 * len(LATE))
            for k in range(NB):
                for m in range(2):
                    n = 2 * k + m
                    if n >= 4:
                        pe.wait_ge(m2["act"], m2["bc_pad"] + n - 3)
                    pe.matmul(ps[:, 4 + n % 4, :], W["w_bc"][:, m * P:(m + 1) * P], blk(XN, k), start=True, stop=True).then_inc(m2["pe"], 1)
            for i in range(NT):
                mm = pe.matmul(ps[:, 0, i * H2:(i + 1) * H2], tile(XN, i), W["w_dt"], start=True, stop=True)
            mm.then_inc(m2["pe"], 1)
            for i in range(NT):
                mm = pe.matmul(ps[:, 3, i * E:(i + 1) * E], tile(XN, i), W["gate2"], start=True, stop=True)
            mm.then_inc(f2["pe"], 1)
            pe.wait_ge(m2["dve"], m2["adt"] + 1)
            adt = slot(8)[:, NT * H2:2 * NT * H2]
            pe.matmul(ps[:, 1, :], upper[:, :], adt, start=True, stop=True).then_inc(m2["pe"], 1)
            pe.matmul(ps[:, 2, :], ones_1[:, :], adt, start=True, stop=True).then_inc(m2["pe"], 1)
            pe.wait_ge(m2["act"], m2["bc_pad"] + 2 * NB)
            for i in range(NT):
                mm = pe.matmul(ps[0:H2, 4 + i // 4, (i % 4) * P:(i % 4 + 1) * P], ADT[:, i, :], upper[:, :], start=True, stop=True)
            mm.then_inc(m2["pe"], 1)
            pe.wait_ge(m2["dve"], m2["acum"] + 1)
            project_h(0, 0, 0, 0)
            project_gate(0, 0, 0)
            pe.wait_ge(m2["dve"], m2["parts"] + NB)
            pe.wait_ge(m2["act"], m2["bc"] + 2 * BATCH)
            for k in range(NB):
                for i in range(4):
                    mm = pe.transpose(four(4 + k)[:, i, :], tile(BCH[0], 4 * k + i), ident[:, :])
                mm.then_inc(m2["pe"], 1)
            for k in range(NB):
                if k == 2:
                    turn_h(0, 0)
                    pe.wait_ge(m2["act"], m2["bt_out"] + NB)
                for i in range(4):
                    c = 4 * k + i
                    mm = pe.matmul(four(GT_BANK[k])[:, i, :], tile(BCH[0], c), tile(BCH[1], c), start=True, stop=True)
                mm.then_inc(m2["pe"], 1)
            pe.wait_ge(m2["dve"], m2["gt_out"] + NB)

            pe.sem_inc(m2["outp"], 1)
            arguments(0, 0, 0, (0, 1, 2, 3))
            pe.wait_ge(m2["dve"], m2["gt_out"] + 2)
            spread_sums(0, 0, 0)
            shares(0, 0)

            steps(pe, step)
            sum_out(CT * BATCH - 1, LAST % 2)
            picked_pe(pe, f2, 2)
            pe.wait_ge(m2["ss"], CT * BATCH + 1)
            for k in range(NB):
                if k >= 2:
                    pe.wait_ge(m2["act"], m2["rstd"] + k - 1)
                pe.matmul(ps[:, k % 2, :], ones_n[:, :], ssum[:, k // 2, (k % 2) * BL:(k % 2 + 1) * BL], start=True, stop=True).then_inc(m2["pe"], 1)

        def bc_convolve(dve, own, b):
            for m in range(2):
                j = 2 * b + m
                dve.wait_ge(m2["act"], m2["bc_tap"] + j + 1)
                for i in range(K3):
                    c = dve.scalar_tensor_tensor(cv[:, j, :], pad[:, j, i:i + SEQ], V("bc_conv", m * DC + i), cv[:, j, :], ALU.mult, ALU.add)
                    if i < K3 - 1:
                        own(c)
                c.then_inc(m2["dve"], 1)

        def l2_act(act, own):
            def pad_h(n, u):
                act.wait_ge(m2["h_mm"], n + 1)
                act.wait_ge(m2["conv"], n + 1)
                act.activation(wide(HP[:, K3:K3 + SEQ]), two(FRONT), ACT.Identity, bias=par(u, "h_bias")).then_inc(m2["h_pad"], 1)
                act.wait_ge(m2["h_pad"], n + 1)
                if not (isinstance(n, int) and n == 0):
                    act.wait_ge(m2["y"], n)
                act.activation(HC[u], HP[:, K3:K3 + SEQ], ACT.Copy, scale=par(u, "taps", K3)).then_inc(m2["h_tap"], 1)

            def silus(n, u):
                act.wait_ge(m2["g_mm"], n + 1)
                act.activation(wide(SG[u]), two(FRONT), ACT.Silu, bias=par(u, "gate_bias")).then_inc(m2["sg"], 1)
                act.wait_ge(m2["conv"], n + 2)
                act.activation(HC[u], HC[u], ACT.Silu).then_inc(m2["hc"], 1)

            def exponentials(n, u):
                for q in range(4):
                    act.wait_ge(m2["arg"], n * 4 + (q + 1))
                    act.activation(LM[:, q * BL:(q + 1) * BL], ps[:, BACK + q % 2, :], ACT.Exp).then_inc(m2["L"], 1)
                act.wait_ge(m2["sdo_mm"], n + 1)
                if not (isinstance(n, int) and n == 0):
                    act.wait_ge(m2["outp"], n)
                    act.wait_ge(m2["sqr"], n)
                act.activation(wide(Y[u]), two(MID), ACT.Exp).then_inc(m2["sdo"], 1)

            norm_act(act, 4, XN)
            act.wait_ge(load["row"], 16)
            act.activation(dtr[:, 2 * H2:], dtr[:, 2 * H2:], ACT.Exp).then_inc(m2["act"], 1)
            for k in range(NB):
                b, h = divmod(k, NB // BATCH)
                for m in range(2):
                    act.wait_ge(m2["pe"], m2["bc_mm"] + 2 * k + m + 1)
                    act.activation(pad[:, 2 * b + m, K3 + h * BL:K3 + (h + 1) * BL], ps[:, 4 + (2 * k + m) % 4, :], ACT.Identity,
                                   bias=V("bc_bias", m)).then_inc(m2["act"], 1)
            for j in range(2 * BATCH):
                act.wait_ge(m2["act"], m2["bc_pad"] + 4 * (j // 2 + 1))
                act.activation(cv[:, j, :], pad[:, j, K3:K3 + SEQ], ACT.Copy, scale=V("bc_conv", (j % 2) * DC + K3)).then_inc(m2["act"], 1)
            act.wait_ge(m2["dve"], m2["dt_biased"] + 1)
            own(act.activation(ADT, DT, ACT.Abs))
            own(act.activation(ADT, ADT, ACT.Exp, scale=-1.0))
            act.activation(ADT, ADT, ACT.Ln, bias=1.0).then_inc(m2["act"], 1)
            act.wait_ge(m2["dve"], m2["dec_sub"] + 1)
            act.activation(DEC, DEC, ACT.Exp).then_inc(m2["act"], 1)
            act.activation(CDEC, ps[:, 2, :].rearrange("p (i h) -> p i h", h=H2), ACT.Exp).then_inc(m2["act"], 1)
            for k in range(NB):
                act.wait_ge(m2["pe"], m2["cumT"] + 1)
                act.activation(blk(parts[0:32, :], k), ps[0:H2, 4 + k, :], ACT.Copy).then_inc(m2["act"], 1)
                act.wait_ge(m2["mid"], k + 1)
                act.activation(blk(parts[32:64, :], k), part_tmp[0:H2, k % 2, :], ACT.Copy).then_inc(m2["act"], 1)
            pad_h(0, 0)
            for k in range(NB):
                act.wait_ge(m2["dve"], m2["parts"] + k + 1)
                act.activation(blk(nparts, k), blk(parts, k), ACT.Copy, scale=-1.0).then_inc(m2["act"], 1)
            act.wait_ge(f2["pe"], f2["logit"] + 1)
            act.activation(rw[:, 0], ps[:, 3, 0:NT * E].rearrange("p (i e) -> p i e", e=E), ACT.Sigmoid).then_inc(f2["act"], 1)
            for j in range(2 * BATCH):
                act.wait_ge(m2["dve"], m2["bc_conv"] + j + 1 if j < 2 else m2["bc_conv1"] + j - 1)
                act.activation(BCH[j % 2][:, (j // 2) * SEQ:(j // 2 + 1) * SEQ], cv[:, j, :], ACT.Silu).then_inc(m2["act"], 1)
            silus(0, 0)
            for k in range(NB):
                act.wait_ge(m2["pe"], m2["bt"] + k + 1)
                act.activation(blk(slot(5), k), ps[:, 4 + k, :], ACT.Copy).then_inc(m2["act"], 1)
            act.sem_inc(m2["sqr"], 1)

            def step(n, b, t, u, half, t1):
                b1, u1 = (b, 1 - u) if t1 is not None else (b + 1, 0)
                if b1 < BATCH:
                    pad_h(n + 1, u1)
                if b > 0 and isinstance(t, int) and t == 0:
                    act.wait_ge(m2["outp"], n + 1)
                    for h in range(2):
                        ins = act.activation(first_sum[h], ps[:, ACC + h, :], ACT.Copy)
                    ins.then_inc(m2["first_out"], 1)
                act.wait_ge(m2["ydiag"], n + 1)
                act.activation(wide(HDD), two(BACK), ACT.Copy).then_inc(m2["yd"], 1)
                if b1 < BATCH:
                    silus(n + 1, u1)
                    exponentials(n + 1, u1)
                act.wait_ge(m2["y"], n + 2)
                act.wait_ge(m2["ss"], n + 1)
                act.activation(rs[:, :, :], wide(Y[u]), ACT.Square).then_inc(m2["sqr"], 1)

            exponentials(0, 0)
            steps(act, step)
            picked_out_act(act, f2)
            act.preload_act_table_set("natural_log_exp_and_others")
            for k in range(NB):
                act.wait_ge(m2["pe"], m2["rms"] + k + 1)
                own(act.activation(flat(k * BL, BL), ps[:, k % 2, :], ACT.Ln, bias=eps_t[:, :]))
                act.activation(flat(k * BL, BL), flat(k * BL, BL), ACT.Exp, scale=-0.5).then_inc(m2["act"], 1)

        def l2_dve(dve, own):
            norm_dve(dve, own, 4, X, XN)
            own(dve.memset(pad[:, :, 0:K3], 0.0))
            dve.wait_ge(load["row"], 16)
            dve.tensor_tensor(dtr[:, 0:H2], dtr[:, 0:H2], dtr[:, H2:2 * H2], ALU.add).then_inc(m2["dve"], 1)
            dve.wait_ge(m2["dve"], m2["row"] + 1)
            dve.wait_ge(m2["pe"], m2["dt_mm"] + 1)
            bc = lambda v: v.unsqueeze(1).to_broadcast([P, NT, H2])
            bank = lambda k: ps[:, k, :].rearrange("p (i h) -> p i h", h=H2)
            dve.tensor_tensor(DT, bank(0), bc(dtr[:, 0:H2]), ALU.add).then_inc(m2["dve"], 1)
            bc_convolve(dve, own, 0)
            dve.wait_ge(m2["act"], m2["dt_soft"] + 1)
            dve.scalar_tensor_tensor(DT, DT, 0.0, ADT, ALU.max, ALU.add).then_inc(m2["dve"], 1)
            dve.wait_ge(m2["act"], m2["arow"] + 1)
            own(dve.tensor_scalar(dtr[:, 2 * H2:], dtr[:, 2 * H2:], -1.0, None, ALU.mult))
            dve.wait_ge(m2["dve"], m2["dt"] + 1)
            dve.tensor_tensor(ADT, DT, bc(dtr[:, 2 * H2:]), ALU.mult).then_inc(m2["dve"], 1)
            dve.wait_ge(m2["pe"], m2["tot"] + 1)
            dve.tensor_copy(acum, ps[:, 1, :]).then_inc(m2["dve"], 1)
            dve.wait_ge(m2["dve"], m2["acum"] + 1)
            dve.tensor_tensor(DEC, bank(2), acum.rearrange("p (i h) -> p i h", h=H2), ALU.subtract).then_inc(m2["dve"], 1)
            for k in range(NB):
                r, tb = rs[0:H2, k % 2, :], part_tmp[0:H2, k % 2, :]
                dve.wait_ge(m2["act"], m2["hi_mid"] + 2 * k + 1)
                own(dve.tensor_tensor(r, ps[0:H2, 4 + k, :], blk(parts[0:32, :], k), ALU.subtract))
                dve.tensor_copy(tb, r).then_inc(m2["mid"], 1)
                dve.wait_ge(m2["mid"], k + 1)
                dve.wait_ge(m2["act"], m2["hi_mid"] + 2 * k + 2)
                dve.tensor_tensor(blk(parts[64:96, :], k), r, tb, ALU.subtract).then_inc(m2["dve"], 1)
            bc_convolve(dve, own, 1)
            own(dve.memset(HP[:, 0:K3], 0.0))
            bc4 = lambda v: v.unsqueeze(3).to_broadcast([P, TB, 2, P2])
            lm = LM.rearrange("p (c h l) -> p c h l", h=2, l=P)
            dve.sem_inc(m2["conv"], 1)

            def convolve(n, u):
                dve.wait_ge(m2["h_tap"], n + 1)
                for tap in range(K3):
                    c = dve.scalar_tensor_tensor(HC[u], HP[:, tap:tap + SEQ], par(u, "taps", tap), HC[u], ALU.mult, ALU.add)
                    if tap < K3 - 1:
                        own(c)
                c.then_inc(m2["conv"], 1)

            convolve(0, 0)
            dve.wait_ge(f2["act"], f2["sig"] + 1)
            own(dve.tensor_scalar(rw[:, 0], rw[:, 0], V("route_scale"), None, ALU.mult))
            share(dve, own, rw[:, 0], 0.0).then_inc(f2["dve"], 1)
            for k in range(NB):
                dve.wait_ge(m2["pe"], m2["gt"] + k + 1)
                dve.tensor_copy(blk(slot(6), k), ps[:, GT_BANK[k], :]).then_inc(m2["dve"], 1)
            def weigh(n, b, t):
                dve.wait_ge(m2["tr"], n + 1)
                dve.tensor_tensor(heads(HDT), two(FRONT).rearrange("p k (c h q) -> p (k c) h q", h=2, q=P2),
                                  bc4(DT[:, b * TB:(b + 1) * TB, bass.ds(t * 2, 2)]), ALU.mult).then_inc(m2["hdt"], 1)
                dve.wait_ge(m2["hdt"], n + 1)
                dve.tensor_tensor(heads(HDD), heads(HDT), bc4(DEC[:, b * TB:(b + 1) * TB, bass.ds(t * 2, 2)]),
                                  ALU.mult).then_inc(m2["hdd"], 1)
                dve.wait_ge(m2["L"], n * 4 + 4)
                dve.tensor_tensor(lm, lm, GT[:, b * TB:(b + 1) * TB, :].unsqueeze(2).to_broadcast([P, TB, 2, P]),
                                  ALU.mult).then_inc(m2["M"], 1)

            def step(n, b, t, u, half, t1):
                b1, u1 = (b, 1 - u) if t1 is not None else (b + 1, 0)
                t1 = 0 if t1 is None else t1
                dve.wait_ge(m2["st"], n + 1)
                if not (isinstance(n, int) and n == 0):
                    dve.wait_ge(m2["yoff"], n)
                own(dve.tensor_copy(ST[:, P:2 * P], four(MID)[:, 0, :]))
                for c in range(2, TB):
                    for h in range(2):
                        o = h * P2
                        if c > 2:
                            own.due(1)
                        s = dve.scalar_tensor_tensor(ST[:, c * P + o:c * P + o + P2], ST[:, (c - 1) * P + o:(c - 1) * P + o + P2],
                                                     CDEC[:, b * TB + c - 1, bass.ds(t * 2 + h, 1)],
                                                     four(MID + (c - 1) // 4)[:, (c - 1) % 4, o:o + P2], ALU.mult, ALU.add)
                        if c < TB - 1 or h == 0:
                            own.later(s)
                s.then_inc(m2["rec"], 1)
                if b1 < BATCH:
                    convolve(n + 1, u1)
                dve.wait_ge(m2["yd"], n + 1)
                own(dve.scalar_tensor_tensor(HDD, HC[u], vec[:, bass.ds(t + VCOL["d2"], 1)], HDD, ALU.mult, ALU.add))
                dve.wait_ge(m2["yoff"], n + 1)
                dve.wait_ge(m2["sdo"], n + 1)
                dve.tensor_tensor(Y[u][:, P:], Y[u][:, P:], flat2(MID)[:, P:], ALU.mult).then_inc(m2["yoff_used"], 1)
                dve.wait_ge(m2["yoff_used"], n + 1)
                dve.tensor_copy(Y[u][:, 0:P], HDD[:, 0:P])
                dve.tensor_tensor(Y[u][:, P:], HDD[:, P:], Y[u][:, P:], ALU.add).then_inc(m2["y_sum"], 1)
                if b1 < BATCH:
                    weigh(n + 1, b1, t1)

            weigh(0, 0, 0)
            for b in range(BATCH):
                per = K3 + 2 * (TB - 2)
                n0 = CT * b
                step(n0, b, 0, 0, None, 1)
                with dve.Fori(0, (CT - 2) // 2) as i:
                    own.rounds(i, 2 * per)
                    for v in range(2):
                        step(i * 2 + (n0 + 1 + v), b, i * 2 + (1 + v), (1 + v) % 2, None, i * 2 + (2 + v))
                    own.end((CT - 2) // 2)
                step(n0 + LAST, b, LAST, LAST % 2, None, None)
            picked_out_dve(dve, f2, 2)
            for k in range(NB):
                b, h = divmod(k, NB // BATCH)
                dve.wait_ge(m2["act"], m2["rstd"] + k + 1)
                dve.wait_ge(m2["outp"], CT * BATCH + 1)
                total = first_sum[h] if b == 0 else ps[:, ACC + h, :]
                own(dve.tensor_tensor(blk(S, k), total, flat(k * BL, BL), ALU.mult))
                dve.tensor_scalar(blk(S, k), blk(S, k), V("b_out"), None, ALU.add).then_inc(m2["dve"], 1)

        def l2_pool(pool, own):
            pool.wait_ge(norm["out"], NB * 5)
            own(pool.memset(ssum[:, :, :], 0.0))
            pool.sem_inc(m2["ss"], 1)
            pool.sem_inc(m2["y"], 1)

            def weights_out(n, u, half):
                pool.wait_ge((m2["w_in0"], m2["w_in1"])[u], half * 16 + 16)
                if not (isinstance(n, int) and n == 0):
                    pool.wait_ge(m2["outp"], n)
                pool.tensor_tensor(wo_t[:, u, :], w_t[:, u, TCOL["out"]:TCOL["out"] + P],
                                   par(u, "norm_w").to_broadcast([P, P]), ALU.mult).then_inc(m2["wo"], 1)

            def step(n, b, t, u, half, t1):
                if t1 is not None or b + 1 < BATCH:
                    weights_out(n + 1, 0 if t1 is None else 1 - u, half)
                pool.wait_ge(m2["y_sum"], n + 1)
                pool.tensor_tensor(Y[u], Y[u], SG[u], ALU.mult).then_inc(m2["y"], 1)
                pool.wait_ge(m2["sqr"], n + 2)
                if not (isinstance(n, int) and n == 0):
                    pool.wait_ge(m2["ss"], n + 1)
                pool.tensor_tensor(ssum[:, b, :], ssum[:, b, :], rs[:, :, :].rearrange("p k t -> p (k t)"), ALU.add).then_inc(m2["ss"], 1)

            weights_out(0, 0, 0)
            steps(pool, step)

        pairs = E * HE // P
        gb = [blk(slot(4), u) for u in range(2)]
        hw = [blk(slot(5), u) for u in range(2)]

        def f2_pe(pe):
            pe.wait_ge(f2["rt_out"], 2)
            pe.wait_ge(m2["act"], m2["rstd"] + NB)
            per = pairs + 1
            for n in range(NB * per + 1):
                if n < NB * per:
                    k, q = divmod(n, per)
                    if n >= 2:
                        pe.wait_ge(f2["gelu"], n - 1)
                        pe.wait_ge(f2["hw"], n - 1)
                    if q < pairs:
                        pe.matmul(ps[:, 4 + n % 2, :], selr2[:, 2 * q:2 * q + 2, :].rearrange("k a p -> k (a p)"), blk(rtb, k),
                                  start=True, stop=True).then_inc(f2["wbc"], 1)
                        pe.matmul(ps[:, n % 2, :], W["ew1"][:, q * P:(q + 1) * P], blk(XN, k), start=True, stop=True).then_inc(f2["h"], 1)
                    else:
                        pe.matmul(ps[0:HE, n % 2, :], W["sw1"], blk(XN, k), start=True, stop=True).then_inc(f2["h"], 1)
                if n >= 1:
                    k, q = divmod(n - 1, per)
                    y = ps[:, 2 + k % 2, :]
                    if q == 0:
                        if k >= 2:
                            pe.wait_ge(f2["act"], f2["y_out"] + k - 1)
                        pe.matmul(y, W["eb2"], blk(rtf, k), start=True, stop=False)
                    pe.wait_ge(f2["hw"], n)
                    if q < pairs:
                        pe.matmul(y, W["ew2"][:, q * P:(q + 1) * P], hw[(n - 1) % 2], start=False, stop=False)
                    else:
                        pe.matmul(y, W["sw2"], hw[(n - 1) % 2][0:HE, :], start=False, stop=True).then_inc(f2["pe"], 1)

        def f2_act(act, own):
            per = pairs + 1
            for n in range(NB * per + 1):
                if n < NB * per:
                    k, q = divmod(n, per)
                    act.wait_ge(f2["h"], n + 1)
                    if n >= 2:
                        act.wait_ge(f2["hw"], n - 1)
                    p = P if q < pairs else HE
                    act.activation(gb[n % 2][0:p, :], ps[0:p, n % 2, :], ACT.Gelu,
                                   bias=V("eb1", q) if q < pairs else V("sb1", 0, HE)).then_inc(f2["gelu"], 1)
                if n >= per and n % per == 0:
                    act.wait_ge(f2["pe"], f2["y"] + n // per)
                    act.activation(blk(G, n // per - 1), ps[:, 2 + (n // per - 1) % 2, :], ACT.Identity,
                                   bias=V("sb2")).then_inc(f2["act"], 1)
            act.wait_ge(f2["act"], f2["y_out"] + NB)
            for k in range(NB):
                act.activation(blk(G, k), blk(G, k), ACT.Silu).then_inc(f2["act"], 1)

        def f2_dve(dve, own):
            per = pairs + 1
            for n in range(NB * per):
                k, q = divmod(n, per)
                dve.wait_ge(f2["gelu"], n + 1)
                if q < pairs:
                    dve.wait_ge(f2["wbc"], k * pairs + q + 1)
                    dve.tensor_tensor(hw[n % 2], gb[n % 2], ps[:, 4 + n % 2, :], ALU.mult).then_inc(f2["hw"], 1)
                else:
                    dve.tensor_copy(hw[n % 2][0:HE, :], gb[n % 2][0:HE, :]).then_inc(f2["hw"], 1)
            gate_dve(dve, own, f2, m2["dve"], m2["s_out"])

        QK = [slot(3), slot(4)]
        VT = tiles(5)
        prob = [slots(6, 1)[:, 0:SEQ], slots(6, 1)[:, SEQ:]]
        probT = [slot(7)[:, 0:SEQ], slot(7)[:, SEQ:]]
        ROWS = BATCH * TB
        assert ROWS == NB * F3 // P
        O_BANK, H_BANK = 6, 7
        mid = [[blk(slot(8 + k), m) for m in range(F3 // P)] for k in range(NB)]
        spans = [(r, r // TB, r % TB, r % TB + 1) for r in range(ROWS)]

        def l3_pe(pe):
            norm_pe(pe, 5, X, f2["dve"], f2["x_out"])
            for k in range(NB):
                pe.wait_ge(norm["out"], NB * 5 + k + 1)
                for m in range(2):
                    n = 2 * k + m
                    if n >= 4:
                        pe.wait_ge(m3["act"], m3["qk_out"] + n - 3)
                    pe.matmul(ps[:, 4 + n % 4, :], W["qkv"][:, m * P:(m + 1) * P], blk(XN, k), start=True, stop=True).then_inc(m3["pe"], 1)
            for k in range(NB):
                for i in range(4):
                    mm = pe.matmul(four(k)[:, i, :], tile(XN, 4 * k + i), W["qkv"][:, 2 * P:], start=True, stop=True)
                mm.then_inc(m3["pe"], 1)
            pe.wait_ge(m3["act"], m3["v_out"] + NB)

            def score(r, b, qi, w):
                if r >= 2:
                    pe.wait_ge(m3["e"], r - 1)
                for h in range((w * P + BL - 1) // BL):
                    c0, c1 = h * BL, min(w * P, (h + 1) * BL)
                    out = ps[:, 2 * (r % 2) + h, 0:c1 - c0]
                    last = c1 == w * P
                    mm = pe.matmul(out, tile(QK[0], r), QK[1][:, b * SEQ + c0:b * SEQ + c1], start=True, stop=not last,
                                   skip_group_check=True)
                    if last:
                        mm = pe.matmul(out[:, c1 - c0 - P:], ident_b[:, :], mask_q[:, :], start=False, stop=True, skip_group_check=True)
                mm.then_inc(m3["s"], 1)

            def values(r, b, qi, w):
                pe.wait_ge(m3["p"], r + 1)
                for h in range((w + 3) // 4):
                    if r >= 1:
                        pe.wait_ge(m3["pT_out"], halves_done[r])
                    for c in range(4 * h, min(w, 4 * h + 4)):
                        mm = pe.transpose(four(4 + h)[:, c % 4, :], prob[r % 2][:, c * P:(c + 1) * P], ident[:, :])
                    mm.then_inc(m3["pT"], 1)
                if r >= 1:
                    pe.wait_ge(m3["o_out"], r)
                for c in range(w):
                    if c % 4 == 0:
                        pe.wait_ge(m3["pT_out"], halves_done[r] + c // 4 + 1)
                    mm = pe.matmul(ps[:, O_BANK, 0:P], VT[:, b * TB + c, :], probT[r % 2][:, c * P:(c + 1) * P],
                                   start=(c == 0), stop=(c == w - 1))
                mm.then_inc(m3["o"], 1)

            for r in range(ROWS + 1):
                if r < ROWS:
                    score(*spans[r])
                    k, m = divmod(r, F3 // P)
                    if r >= 1:
                        pe.wait_ge(f3["relu"], r)
                    pe.matmul(ps[:, H_BANK, :], W["g1"][:, m * P:(m + 1) * P], blk(XN, k), start=True, stop=True).then_inc(f3["h"], 1)
                if r >= 1:
                    values(*spans[r - 1])

        halves_done = [sum((w + 3) // 4 for _, _, _, w in spans[:r]) for r in range(ROWS + 1)]

        def l3_act(act, own):
            norm_act(act, 5, XN)
            for n in range(2 * NB):
                k, m = divmod(n, 2)
                act.wait_ge(m3["pe"], m3["qk"] + n + 1)
                act.activation(blk(QK[m], k), ps[:, 4 + n % 4, :], ACT.Identity, bias=V(("b_q", "b_k")[m])).then_inc(m3["act"], 1)
            for k in range(NB):
                act.wait_ge(m3["pe"], m3["v"] + k + 1)
                act.activation(blk(slot(5), k), ps[:, k, :], ACT.Copy).then_inc(m3["act"], 1)
            for r in range(ROWS + 1):
                if r < ROWS:
                    _, b, qi, w = spans[r]
                    act.wait_ge(m3["peak"], r + 1)
                    if r >= 2:
                        act.wait_ge(m3["pT"], halves_done[r - 1])
                    act.activation(prob[r % 2][:, 0:w * P],
                                   ps[:, 2 * (r % 2):2 * (r % 2) + 2, :].rearrange("p k t -> p (k t)")[:, 0:w * P], ACT.Exp,
                                   bias=stat[:, 1, r:r + 1], scale=SC1, accum_out=stat[:, 2, r:r + 1]).then_inc(m3["e"], 1)
                    act.wait_ge(f3["h"], r + 1)
                    act.activation(mid[r // (F3 // P)][r % (F3 // P)], ps[:, H_BANK, :], ACT.Relu,
                                   bias=V("c1", r % (F3 // P))).then_inc(f3["relu"], 1)
                if r >= 1:
                    act.wait_ge(m3["o"], r)
                    act.activation(tile(S, r - 1), ps[:, O_BANK, 0:P], ACT.Identity, bias=V("b_v")).then_inc(m3["o_out"], 1)

        def l3_dve(dve, own):
            norm_dve(dve, own, 5, X, XN)

            def spread_out(r, b, qi, w):
                for h in range((w + 3) // 4):
                    dve.wait_ge(m3["pT"], halves_done[r] + h + 1)
                    n = min(4, w - 4 * h)
                    if r >= 2 and h == 0:
                        dve.wait_ge(m3["o"], r - 1)
                    dve.tensor_copy(probT[r % 2][:, h * BL:h * BL + n * P], ps[:, 4 + h, 0:n * P]).then_inc(m3["pT_out"], 1)

            for r in range(ROWS + 1):
                if r < ROWS:
                    _, b, qi, w = spans[r]
                    dve.wait_ge(m3["s"], r + 1)
                    own(dve.tensor_reduce(stat[:, 0, r:r + 1],
                                          ps[:, 2 * (r % 2):2 * (r % 2) + 2, :].rearrange("p k t -> p (k t)")[:, 0:w * P], AX.X, ALU.max))
                    dve.tensor_scalar(stat[:, 1, r:r + 1], stat[:, 0, r:r + 1], -SC1, None, ALU.mult).then_inc(m3["peak"], 1)
                if r >= 1:
                    spread_out(*spans[r - 1])
                if r < ROWS:
                    dve.wait_ge(m3["e"], r + 1)
                    own(dve.reciprocal(stat[:, 3, r:r + 1], stat[:, 2, r:r + 1]))
                    dve.tensor_scalar(prob[r % 2][:, 0:w * P], prob[r % 2][:, 0:w * P], stat[:, 3, r:r + 1], None, ALU.mult).then_inc(m3["p"], 1)

        def f3_pe(pe):
            M = F3 // P
            pe.wait_ge(m3["e"], ROWS)
            pe.wait_ge(f3["relu"], ROWS)
            for k in range(NB):
                for m in range(M):
                    mm = pe.matmul(ps[:, k, :], W["g2"][:, m * P:(m + 1) * P], mid[k][m], start=(m == 0), stop=(m == M - 1))
                mm.then_inc(f3["pe"], 1)

        def f3_act(act, own):
            for k in range(NB):
                act.wait_ge(f3["pe"], f3["y"] + k + 1)
                act.activation(blk(G, k), ps[:, k, :], ACT.Silu, bias=V("c2")).then_inc(f3["act"], 1)

        def f3_dve(dve, own):
            for k in range(NB):
                dve.wait_ge(m3["o_out"], ROWS)
                dve.wait_ge(f3["act"], f3["g"] + k + 1)
                own(dve.tensor_tensor(blk(S, k), blk(S, k), blk(G, k), ALU.mult))
                dve.tensor_tensor(blk(X, k), blk(X, k), blk(S, k), ALU.add).then_inc(f3["dve"], 1)

        @block.sync
        def _(sp):
            for k in range(NB):
                sp.dma_start(blk(X, k), a["x"][:, k * BL:(k + 1) * BL]).then_inc(load["x"], 16)
            sp.dma_start(vec[:, :], a["vec"]).then_inc(load["vec"], 16)
            for n, _, _ in SOON:
                sp.dma_start(W[n], a[n]).then_inc(load["weights"], 16)
            for n, _, _ in POOLED:
                sp.dma_start(W[n], a[n]).then_inc(load["pooled"], 16)
            sp.wait_ge(load["weights"], 16 * len(SOON))
            for n, _, _ in FIRST[len(SOON):]:
                sp.dma_start(W[n], a[n]).then_inc(load["weights"], 16)
            sp.dma_start(dtr[:, :], a["dt_row"].to_broadcast([P, 3 * H2])).then_inc(load["row"], 16)
            sp.wait_ge(m0["dve"], m0["ygate"] + BATCH * MI)
            for n, _, _ in LATE:
                sp.dma_start(W[n], a[n]).then_inc(load["late"], 16)
            for n, _, _ in EXPERTS:
                sp.dma_start(W[n], a[n]).then_inc(load["experts"], 16)
            if upto >= 3:
                l2_sync(sp)
            final = ends[upto - 1]
            for k in range(NB):
                sp.wait_ge(final["dve"], final["x_out"] + k + 1)
                sp.dma_start(out[:, k * BL:(k + 1) * BL], blk(X, k)).then_inc(done["stored"], 16)
            sp.wait_ge(done["stored"], 16 * NB)
        @block.gpsimd
        def _(pool):
            own = Chain(pool, pool_own)
            pool.memset(ones_d[:, :], 1.0 / P)
            pool.memset(eps_t[:, :], EPS)
            own(pool.memset(ident[:, :], 0.0))
            pool.affine_select(ident[:, :], ident[:, :], [[-1, P]], ALU.not_equal, 1.0, base=0,
                               channel_multiplier=1).then_inc(const["ready"], 1)
            for e in range(E):
                pool.memset(tie[:, :, e:e + 1], float(E - e))
            for t, w in ((selr, P), (selr2, HE)):
                own(pool.memset(t[:, :, :], 0.0))
                for k in range(3):
                    ins = pool.affine_select(t[:, :, :], t[:, :, :], [[-1, E], [0, w]], ALU.not_equal, 1.0,
                                             base=-E * (k + 1), channel_multiplier=1)
                    if k == 2 and w == P:
                        ins.then_inc(const["ready"], 1)
                        pool.wait_ge(const["ready"], 2)
                    else:
                        own(ins)
            pool.memset(ones_n[:, :], 1.0 / INTER)
            pool.memset(ones_1[:, :], 1.0)
            for t in (ident_b, mask_t, mask_q, zero, sel, sel2):
                pool.memset(t[:, :] if len(t.shape) == 2 else t[:, :, :], 0.0)
            own(pool.memset(upper[:, :], 1.0))
            pool.affine_select(ident_b[:, :], ident_b[:, :], [[-1, P]], ALU.not_equal, 1.0, base=0, channel_multiplier=1)
            pool.affine_select(upper[:, :], upper[:, :], [[1, P]], ALU.is_ge, 0.0, base=0, channel_multiplier=-1)
            pool.affine_select(mask_t[:, :, :], mask_t[:, :, :], [[0, 4], [1, P]], ALU.is_ge, -BIG, base=0, channel_multiplier=-1)
            pool.affine_select(mask_q[:, :], mask_q[:, :], [[-1, P]], ALU.is_ge, -BIG, base=0, channel_multiplier=1)
            for t, w in ((sel2, P2), (sel, P)):
                for k in range(3):
                    ins = pool.affine_select(t[:, :, :], t[:, :, :], [[-1, H2], [0, w]], ALU.not_equal, 1.0,
                                             base=-H2 * k, channel_multiplier=1)
                    if k == 2 and w == P:
                        ins.then_inc(const["ready"], 1)
                    else:
                        own(ins)
            l0_pool(pool)
            if upto >= 3:
                l2_pool(pool, own)

        @block.tensor
        def _(pe):
            pe.wait_ge(const["ready"], 1)
            pe.wait_ge(load["x"], 16 * NB)
            norm_pe(pe, 0, X)
            f0_pe(pe)
            l0_pe(pe)
            f0_mix_pe(pe)
            if upto >= 2:
                l1_pe(pe)
            if upto >= 3:
                l2_pe(pe)
                f2_pe(pe)
            if upto >= 4:
                l3_pe(pe)
                f3_pe(pe)

        @block.scalar
        def _(act):
            own = Chain(act, act_own)
            act.wait_ge(const["ready"], 1)
            act.wait_ge(load["x"], 16 * NB)
            act.wait_ge(load["vec"], 16)
            norm_act(act, 0, XN)
            f0_act(act, own)
            l0_act(act, own)
            gate_act(act, f0)
            if upto >= 2:
                l1_act(act, own)
            if upto >= 3:
                l2_act(act, own)
                f2_act(act, own)
            if upto >= 4:
                l3_act(act, own)
                f3_act(act, own)

        @block.vector
        def _(dve):
            own = Chain(dve, dve_own)
            dve.wait_ge(load["x"], 16 * NB)
            dve.wait_ge(load["vec"], 16)
            dve.wait_ge(const["ready"], 1)
            norm_dve(dve, own, 0, X, XN)
            f0_dve(dve, own)
            l0_dve(dve, own)
            gate_dve(dve, own, f0, m0["dve"], m0["s_out"])
            if upto >= 2:
                l1_dve(dve, own)
            if upto >= 3:
                l2_dve(dve, own)
                f2_dve(dve, own)
            if upto >= 4:
                l3_dve(dve, own)
                f3_dve(dve, own)


def layout(inputs):
    import numpy as np

    f = {k: np.asarray(v) for k, v in inputs.items()}
    a0, f0, a1, f1 = ({k.split(p)[1]: v for k, v in f.items() if k.startswith(p)}
                      for p in ("L0_attn_", "L0_ffn_", "L1_attn_", "L1_ffn_"))
    a2, f2, a3, f3 = ({k.split(p)[1]: v for k, v in f.items() if k.startswith(p)}
                      for p in ("L2_attn_", "L2_ffn_", "L3_attn_", "L3_ffn_"))
    cols = lambda v: v.reshape(-1, P).T
    taps = lambda w: w.reshape(-1, P, w.shape[-1]).transpose(1, 0, 2).reshape(P, -1)
    rows = lambda w: w.reshape(-1, P, w.shape[-1]).transpose(1, 0, 2).reshape(P, -1)

    def low(v):
        z = np.zeros((P, 1), np.float32)
        z[:v.size, 0] = v.reshape(-1)
        return z

    vectors = dict(
        ln1_g=cols(a0["ln1_g"]), ln1_b=cols(a0["ln1_b"]), ln2_g=cols(a0["ln2_g"]), ln2_b=cols(a0["ln2_b"]),
        b1=cols(a0["b1"]), b2=cols(a0["b2"]), conv_w=taps(a0["conv_w"][:, 0, :]), conv_b=cols(a0["conv_b"]),
        dt_b=cols(a0["dt_proj_b"]), a_log=taps(a0["A_log"]), d=cols(a0["D_param"]), gate_b=low(f0["gate_b"]),
        fb1=f0["b1"].T, fb2=f0["b2"].T, fb3=f0["b3"].T,
        bc_bias=cols(a2["b_in"][2 * INTER:2 * INTER + 2 * N2]), bc_conv=taps(a2["conv_w"][INTER:]), b_out=cols(a2["b_out"]),
        d2=cols(np.repeat(a2["D"], P2)),
        eb1=cols(f2["b1"].reshape(-1)), sb1=low(f2["bs1"]), sb2=cols(f2["bs2"]),
        route_scale=np.broadcast_to(f2["route_scale"].reshape(1, 1), (P, 1)),
        b_q=cols(a3["b"][:P]), b_k=cols(a3["b"][P:2 * P]), b_v=cols(a3["b"][2 * P:]),
        c1=cols(f3["b1"]), c2=cols(f3["b2"]))
    w_in = a2["W_in"].T
    by_tile = lambda w: w.reshape(P, CT, -1)
    tile_w = dict(
        gate=by_tile(w_in[:, :INTER]), h=by_tile(w_in[:, INTER:2 * INTER]), out=by_tile(rows(a2["W_out"].T)),
        gate_bias=by_tile(cols(a2["b_in"][:INTER])), h_bias=by_tile(cols(a2["b_in"][INTER:2 * INTER])),
        taps=by_tile(taps(a2["conv_w"][:INTER])), norm_w=by_tile(cols(a2["norm_w"])))
    per_expert = lambda w: w.transpose(1, 0, 2).reshape(w.shape[1], -1)
    out = dict(
        x=f["L0_attn_x"].reshape(T, P).T,
        vec=np.concatenate([vectors[n] for n, _ in VECTORS], axis=1),
        dt_row=np.stack([a2["b_in"][2 * INTER + 2 * N2:], a2["dt_bias"], a2["A_log"]]).reshape(1, -1),
        tile_w=np.concatenate([tile_w[n] for n, _ in TILE_W], axis=2).reshape(P, -1),
        w1=a0["W1"].T, w2=rows(a0["W2"].T), in_proj=a0["in_proj_w"].T, x_proj=rows(a0["x_proj_w"].T),
        dt_proj=a0["dt_proj_w"].T, out_proj=rows(a0["out_proj_w"].T), gate0=f0["gate_w"],
        f1=per_expert(f0["w1"]), f2=per_expert(f0["w2"]), f3=per_expert(f0["w3"]),
        wq=a1["Wq"], wk=a1["Wk"], wvT=a1["Wv"].T, wr=a1["Wr"], router=f1["router_w"].T,
        w13=per_expert(f1["w13"]), w2e=rows(f1["w2"].reshape(E * I1, P)),
        w_bc=w_in[:, 2 * INTER:2 * INTER + 2 * N2], w_dt=w_in[:, 2 * INTER + 2 * N2:],
        gate2=f2["gate_W"], ew1=per_expert(f2["W1"]), ew2=rows(f2["W2"].reshape(E * HE, P)),
        eb2=np.concatenate([np.zeros((E, P), np.float32)] + [f2["b2"]] * 3), sw1=f2["Ws1"], sw2=f2["Ws2"],
        qkv=a3["W"], g1=f3["W1"], g2=rows(f3["W2"]))
    return {k: np.ascontiguousarray(v) for k, v in out.items()}


def kernel(**inputs):
    import numpy as np
    import concourse.bacc as bacc
    from concourse.bass_utils import run_bass_kernel_spmd

    nc = bacc.Bacc("TRN2", target_bir_lowering=False, num_devices=1)
    arrays = {f"in_{k}": v for k, v in layout(inputs).items()}
    a = {k[3:]: nc.dram_tensor(k, v.shape, mybir.dt.from_np(v.dtype), kind="ExternalInput").ap() for k, v in arrays.items()}
    out = nc.dram_tensor("out_x", [P, T], F32, kind="ExternalOutput").ap()
    build(nc, a, out)
    r = run_bass_kernel_spmd(nc, [arrays], core_ids=[0])
    return np.ascontiguousarray(np.asarray(r.results[0]["out_x"]).T).reshape(BATCH, SEQ, P)
```
